# Optimizing a Trainium2 kernel written in Bass

```python
import numpy as np
import jax
import jax.numpy as jnp

def _softmax(x, axis=-1):
    return jax.nn.softmax(x, axis=axis)

def _gelu(x):
    return jax.nn.gelu(x, approximate=True)

def _silu(x):
    return jax.nn.silu(x)

def _sigmoid(x):
    return jax.nn.sigmoid(x)

def _layernorm(x, axis=-1, eps=1e-05):
    m = jnp.mean(x, axis=axis, keepdims=True)
    v = jnp.var(x, axis=axis, keepdims=True)
    return (x - m) / jnp.sqrt(v + eps)

def _scatter_add(tgt, idx, src, axis=0):
    return tgt.at[idx].add(src)

def _segment_sum(src, seg, n):
    return jax.ops.segment_sum(src, seg, n)
kernel_name = 'mk_hybrid_d2_jaxref_r8_23c462'

def setup_inputs(seed: int=0):
    np.random.seed(seed)
    _w = jnp.asarray

    def _L0_attn_a_setup():
        import jax, jax.numpy as jnp
        import numpy as np
        DIM = 128
        HEADS = 16
        KDIM = DIM // 2
        VDIM = DIM
        DK = KDIM // HEADS
        DV = VDIM // HEADS
        LOW = 16
        NORMALIZER = 16.0
        EPS = 1e-05
        B, T = (2, 512)

        def _gla_scan(q, k, v, gk):
            scale = DK ** (-0.5)

            def step(h, inp):
                qt, kt, vt, gt = inp
                h = h * jnp.exp(gt)[..., None] + kt[..., None] * vt[..., None, :]
                ot = jnp.einsum('bhk,bhkv->bhv', qt * scale, h)
                return (h, ot)
            h0 = jnp.zeros((q.shape[0], HEADS, DK, DV), q.dtype)
            xs = tuple((jnp.moveaxis(a, 1, 0) for a in (q, k, v, gk)))
            _, o = jax.lax.scan(step, h0, xs)
            return jnp.moveaxis(o, 0, 1)
        key = jax.random.key(seed)
        ks = jax.random.split(key, 9)

        def lin(k, sh, fan_in):
            return jax.random.normal(k, sh, jnp.float32) * fan_in ** (-0.5)
        return {'x': jax.random.normal(ks[0], (B, T, DIM), jnp.float32), 'Wq': lin(ks[1], (DIM, KDIM), DIM), 'Wk': lin(ks[2], (DIM, KDIM), DIM), 'Wv': lin(ks[3], (DIM, VDIM), DIM), 'Wgk1': lin(ks[4], (DIM, LOW), DIM), 'Wgk2': lin(ks[5], (LOW, KDIM), LOW), 'bgk2': jnp.zeros((KDIM,), jnp.float32), 'Wg': lin(ks[6], (DIM, VDIM), DIM), 'gnw': jnp.ones((DV,), jnp.float32), 'Wo': lin(ks[7], (VDIM, DIM), VDIM)}
    _L0_attn_a_in = _L0_attn_a_setup()

    def _L0_attn_b_setup():
        import jax, jax.numpy as jnp
        import numpy as np
        B, S, E, H, M = (4, 256, 128, 16, 32)
        D = E // H
        LN_EPS = 1e-06

        def softmax_kernel(x, proj):
            x = x * (1.0 / jnp.sqrt(jnp.asarray(x.shape[-1], x.dtype)))
            mapping = jnp.einsum('bhsd,md->bhsm', x, proj)
            correction = jnp.sum(x * x, axis=-1, keepdims=True) * 0.5
            scaling = 1.0 / jnp.sqrt(jnp.asarray(proj.shape[0], x.dtype))
            return scaling * jnp.exp(mapping - correction)

        def favor_forward(x, q_w, q_b, k_w, k_b, v_w, v_b, out_w, out_b, proj, gamma, beta):
            b, s, e = x.shape
            split = lambda y: y.reshape(b, s, H, D).transpose(0, 2, 1, 3)
            Q = split(x @ q_w + q_b)
            K = split(x @ k_w + k_b)
            V = split(x @ v_w + v_b)
            qp = softmax_kernel(Q, proj).transpose(2, 0, 1, 3)
            kp = softmax_kernel(K, proj).transpose(2, 0, 1, 3)
            vs = V.transpose(2, 0, 1, 3)

            def step(carry, inp):
                ksum, kv = carry
                q, k, v = inp
                ksum = ksum + k
                kv = kv + k[..., :, None] * v[..., None, :]
                num = jnp.einsum('bhmd,bhm->bhd', kv, q)
                den = jnp.einsum('bhm,bhm->bh', q, ksum)
                return ((ksum, kv), (num, den))
            init = (jnp.zeros((b, H, M), x.dtype), jnp.zeros((b, H, M, D), x.dtype))
            _, (num, den) = jax.lax.scan(step, init, (qp, kp, vs))
            attn = num / den[..., None]
            attn = attn.transpose(1, 0, 2, 3).reshape(b, s, e)
            main = attn @ out_w + out_b
            res = main + x
            mu = jnp.mean(res, axis=-1, keepdims=True)
            var = jnp.mean(jnp.square(res - mu), axis=-1, keepdims=True)
            return gamma * (res - mu) * jax.lax.rsqrt(var + LN_EPS) + beta
        key = jax.random.key(seed)
        ks = jax.random.split(key, 7)
        glorot = lambda k, sh: jax.random.uniform(k, sh, jnp.float32, -1.0, 1.0) * np.sqrt(6.0 / (sh[0] + sh[1]))
        return {'x': jax.random.normal(ks[0], (B, S, E), jnp.float32), 'q_w': glorot(ks[1], (E, E)), 'q_b': jnp.zeros((E,), jnp.float32), 'k_w': glorot(ks[2], (E, E)), 'k_b': jnp.zeros((E,), jnp.float32), 'v_w': glorot(ks[3], (E, E)), 'v_b': jnp.zeros((E,), jnp.float32), 'out_w': glorot(ks[4], (E, E)), 'out_b': jnp.zeros((E,), jnp.float32), 'proj': jax.random.normal(ks[5], (M, D), jnp.float32), 'gamma': jnp.ones((E,), jnp.float32), 'beta': jnp.zeros((E,), jnp.float32)}
    _L0_attn_b_in = _L0_attn_b_setup()

    def _L0_ffn_setup():
        import jax, jax.numpy as jnp
        import numpy as np
        TAU = 10.0
        EPS = 1e-06
        TOP_K = 8

        def _layernorm(x, g, b):
            mu = jnp.mean(x, axis=-1, keepdims=True)
            var = jnp.var(x, axis=-1, keepdims=True)
            return (x - mu) * jax.lax.rsqrt(var + 1e-05) * g + b

        def _unit_rows(W):
            n = jnp.linalg.norm(W, axis=1, keepdims=True)
            return W / jnp.maximum(n, EPS)
        key = jax.random.key(seed)
        ks = jax.random.split(key, 5)
        D, NB, H = (128, 64, 512)
        B, S = (4, 256)
        x = jax.random.normal(ks[0], (B, S, D), dtype=jnp.float32)
        W1 = jax.random.normal(ks[1], (H, D), dtype=jnp.float32) * (1.0 / np.sqrt(D))
        W2 = jax.random.normal(ks[2], (D, H), dtype=jnp.float32) * (1.0 / np.sqrt(H))
        ln_g = jnp.ones((D,), jnp.float32)
        ln_b = jnp.zeros((D,), jnp.float32)
        router_W = jax.random.normal(ks[3], (NB, D), dtype=jnp.float32) * 0.01
        router_b = jnp.zeros((NB,), jnp.float32)
        raw_U = jax.random.normal(ks[4], (NB, D), dtype=jnp.float32) * 0.02
        raw_V = jax.random.normal(jax.random.fold_in(key, 7), (NB, D), dtype=jnp.float32) * 0.02
        gamma = jnp.ones((1, 1, D), jnp.float32) * 0.1
        return {'x': x, 'W1': W1, 'W2': W2, 'ln_g': ln_g, 'ln_b': ln_b, 'router_W': router_W, 'router_b': router_b, 'raw_U': raw_U, 'raw_V': raw_V, 'gamma': gamma}
    _L0_ffn_in = _L0_ffn_setup()

    def _L1_attn_a_setup():
        import jax, jax.numpy as jnp
        import numpy as np
        B, L, D_MODEL = (4, 256, 128)
        N_HEADS, FEAT, HEAD_DIM = (16, 16, 64)
        CHUNK = 128
        EPS = 1e-12

        def taylor_exp(x):
            f = x.shape[-1]
            r2 = jnp.sqrt(jnp.asarray(2.0, x.dtype))
            rd = jnp.sqrt(jnp.asarray(float(f), x.dtype))
            rrd = jnp.sqrt(rd)
            x2 = (x[..., :, None] * x[..., None, :]).reshape(*x.shape[:-1], f * f) / r2
            ones = jnp.ones_like(x[..., :1])
            return jnp.concatenate([ones, x / rrd, x2 / rd], axis=-1)
        key = jax.random.key(seed)
        k1, k2, k3, k4, k5 = jax.random.split(key, 5)
        s = 0.02
        return {'hidden_states': jax.random.normal(k1, (B, L, D_MODEL), jnp.float32), 'Wq': jax.random.normal(k2, (N_HEADS * FEAT, D_MODEL), jnp.float32) * s, 'Wk': jax.random.normal(k3, (N_HEADS * FEAT, D_MODEL), jnp.float32) * s, 'Wv': jax.random.normal(k4, (N_HEADS * HEAD_DIM, D_MODEL), jnp.float32) * s, 'Wo': jax.random.normal(k5, (D_MODEL, N_HEADS * HEAD_DIM), jnp.float32) * s}
    _L1_attn_a_in = _L1_attn_a_setup()

    def _L1_attn_b_setup():
        import jax, jax.numpy as jnp
        import numpy as np
        B_, L_, DM = (2, 256, 128)
        DS, DC, EXP, HD = (128, 4, 2, 64)
        DI = EXP * DM
        NH = DI // HD
        CONV_DIM = DI + 2 * DS
        DIN = 2 * DI + 2 * DS + NH
        CS = 32
        EPS = 1e-05

        def _segsum(a):
            T = a.shape[-1]
            cs = jnp.cumsum(a, -1)
            seg = cs[..., :, None] - cs[..., None, :]
            mask = jnp.tril(jnp.ones((T, T), bool))
            return jnp.where(mask, seg, -jnp.inf)

        def _ssd(X, A, Bm, Cm):
            b, l, h, p = X.shape
            n, nc = (Bm.shape[-1], l // CS)
            X = X.reshape(b, nc, CS, h, p)
            A = A.reshape(b, nc, CS, h).transpose(0, 3, 1, 2)
            Bm = Bm.reshape(b, nc, CS, n)
            Cm = Cm.reshape(b, nc, CS, n)
            Acs = jnp.cumsum(A, -1)
            Lmat = jnp.exp(_segsum(A))
            Y_diag = jnp.einsum('bcln,bcsn,bhcls,bcshp->bclhp', Cm, Bm, Lmat, X)
            decay_states = jnp.exp(Acs[..., -1:] - Acs)
            states = jnp.einsum('bcln,bhcl,bclhp->bchpn', Bm, decay_states, X)
            states = jnp.concatenate([jnp.zeros_like(states[:, :1]), states], axis=1)
            decay_chunk = jnp.exp(_segsum(jnp.pad(Acs[..., -1], ((0, 0), (0, 0), (1, 0)))))
            states = jnp.einsum('bhzc,bchpn->bzhpn', decay_chunk, states)[:, :-1]
            Y_off = jnp.einsum('bcln,bchpn,bhcl->bclhp', Cm, states, jnp.exp(Acs))
            return (Y_diag + Y_off).reshape(b, l, h, p)

        def _forward(x, norm_w, in_proj_w, conv_w, conv_b, dt_bias, A_log, D, gnorm_w, out_proj_w):
            b, l, _ = x.shape
            xn = x * jax.lax.rsqrt(jnp.mean(x * x, -1, keepdims=True) + EPS) * norm_w
            zxbcdt = jnp.einsum('bld,ed->ble', xn, in_proj_w)
            z = zxbcdt[..., :DI]
            xBC = zxbcdt[..., DI:DI + CONV_DIM]
            dt = zxbcdt[..., -NH:]
            pad = jnp.pad(xBC, ((0, 0), (DC - 1, 0), (0, 0)))
            conv = sum((pad[:, k:k + l, :] * conv_w[:, k] for k in range(DC))) + conv_b
            xBC = conv * jax.nn.sigmoid(conv)
            xs = xBC[..., :DI]
            Bm = xBC[..., DI:DI + DS]
            Cm = xBC[..., DI + DS:]
            dt = jax.nn.softplus(dt + dt_bias)
            A = -jnp.exp(A_log)
            xh = xs.reshape(b, l, NH, HD)
            y = _ssd(xh * dt[..., None], dt * A, Bm, Cm)
            y = y + D[None, None, :, None] * xh
            y = y.reshape(b, l, DI)
            y = y * (z * jax.nn.sigmoid(z))
            y = y * jax.lax.rsqrt(jnp.mean(y * y, -1, keepdims=True) + EPS) * gnorm_w
            return x + jnp.einsum('bld,ed->ble', y, out_proj_w)
        key = jax.random.key(seed)
        ks = jax.random.split(key, 8)
        s = 0.02
        x = jax.random.normal(ks[0], (B_, L_, DM), jnp.float32)
        norm_w = jnp.ones((DM,), jnp.float32)
        in_proj_w = jax.random.normal(ks[1], (DIN, DM), jnp.float32) * s
        conv_w = jax.random.normal(ks[2], (CONV_DIM, DC), jnp.float32) * 0.2
        conv_b = jnp.zeros((CONV_DIM,), jnp.float32)
        dt_bias = jnp.log(jnp.expm1(jax.random.uniform(ks[3], (NH,), minval=0.001, maxval=0.1)))
        A_log = jnp.log(jax.random.uniform(ks[4], (NH,), minval=1.0, maxval=16.0))
        D = jnp.ones((NH,), jnp.float32)
        gnorm_w = jnp.ones((DI,), jnp.float32)
        out_proj_w = jax.random.normal(ks[5], (DM, DI), jnp.float32) * s
        return dict(x=x, norm_w=norm_w, in_proj_w=in_proj_w, conv_w=conv_w, conv_b=conv_b, dt_bias=dt_bias, A_log=A_log, D=D, gnorm_w=gnorm_w, out_proj_w=out_proj_w)
    _L1_attn_b_in = _L1_attn_b_setup()

    def _L1_ffn_setup():
        import jax, jax.numpy as jnp
        import numpy as np
        EMBED = 128
        HEADS = 16
        HEAD_DIM = EMBED // HEADS
        NUM_EXPERTS = 8
        TOP_K = 2
        HIDDEN = (int(2 * (4 * EMBED) / 3) + 63) // 64 * 64
        SEQ = 256
        BATCH = 2
        ROPE_BASE = 10000.0
        EPS = 1e-06

        def _rope_tables(seq_len, dim):
            inv_freq = 1.0 / ROPE_BASE ** (np.arange(0, dim, 2, dtype=np.float32) / dim)
            t = np.arange(seq_len, dtype=np.float32)
            freqs = np.einsum('i,j->ij', t, inv_freq)
            emb = np.concatenate([freqs, freqs], axis=-1)
            return (jnp.asarray(np.cos(emb)), jnp.asarray(np.sin(emb)))

        def _rotate_half(x):
            x1, x2 = jnp.split(x, 2, axis=-1)
            return jnp.concatenate([-x2, x1], axis=-1)

        def _rmsnorm(x, w):
            return x * jax.lax.rsqrt(jnp.mean(x * x, axis=-1, keepdims=True) + EPS) * w

        def _attention(x, wq, wk, wv, wo):
            B, S, _ = x.shape
            q = (x @ wq).reshape(B, S, HEADS, HEAD_DIM).transpose(0, 2, 1, 3)
            k = (x @ wk).reshape(B, S, HEADS, HEAD_DIM).transpose(0, 2, 1, 3)
            v = (x @ wv).reshape(B, S, HEADS, HEAD_DIM).transpose(0, 2, 1, 3)
            cos, sin = _rope_tables(S, HEAD_DIM)
            cos = cos[None, None]
            sin = sin[None, None]
            q = q * cos + _rotate_half(q) * sin
            k = k * cos + _rotate_half(k) * sin
            scale = HEAD_DIM ** (-0.5)
            scores = jnp.einsum('bhqd,bhkd->bhqk', q, k) * scale
            causal = jnp.triu(jnp.ones((S, S), bool), k=1)
            scores = jnp.where(causal, -jnp.inf, scores)
            attn = jax.nn.softmax(scores, axis=-1)
            out = jnp.einsum('bhqk,bhkd->bhqd', attn, v)
            out = out.transpose(0, 2, 1, 3).reshape(B, S, EMBED)
            return out @ wo

        def _moe(x, w_router, wg, wu, wd):
            B, S, E = x.shape
            xf = x.reshape(-1, E)
            logits = xf @ w_router
            probs = jax.nn.softmax(logits, axis=-1)
            topw, topi = jax.lax.top_k(probs, TOP_K)
            topw = topw / jnp.sum(topw, axis=-1, keepdims=True)
            combine = jnp.sum(jax.nn.one_hot(topi, NUM_EXPERTS, dtype=xf.dtype) * topw[..., None], axis=1)
            g = jax.nn.silu(jnp.einsum('td,xdh->txh', xf, wg))
            u = jnp.einsum('td,xdh->txh', xf, wu)
            eo = jnp.einsum('txh,xhd->txd', g * u, wd)
            out = jnp.einsum('txd,tx->td', eo, combine)
            return out.reshape(B, S, E)
        key = jax.random.key(seed)
        ks = jax.random.split(key, 12)
        s = 0.02
        return {'x': jax.random.normal(ks[0], (BATCH, SEQ, EMBED), jnp.float32), 'wq': jax.random.normal(ks[1], (EMBED, EMBED), jnp.float32) * s, 'wk': jax.random.normal(ks[2], (EMBED, EMBED), jnp.float32) * s, 'wv': jax.random.normal(ks[3], (EMBED, EMBED), jnp.float32) * s, 'wo': jax.random.normal(ks[4], (EMBED, EMBED), jnp.float32) * s, 'w_router': jax.random.normal(ks[5], (EMBED, NUM_EXPERTS), jnp.float32) * s, 'wg': jax.random.normal(ks[6], (NUM_EXPERTS, EMBED, HIDDEN), jnp.float32) * s, 'wu': jax.random.normal(ks[7], (NUM_EXPERTS, EMBED, HIDDEN), jnp.float32) * s, 'wd': jax.random.normal(ks[8], (NUM_EXPERTS, HIDDEN, EMBED), jnp.float32) * s, 'g1': jnp.ones((EMBED,), jnp.float32), 'g2': jnp.ones((EMBED,), jnp.float32)}
    _L1_ffn_in = _L1_ffn_setup()
    _d = {'L0_attn_a_x': _L0_attn_a_in['x'], 'L0_attn_a_Wq': _L0_attn_a_in['Wq'], 'L0_attn_a_Wk': _L0_attn_a_in['Wk'], 'L0_attn_a_Wv': _L0_attn_a_in['Wv'], 'L0_attn_a_Wgk1': _L0_attn_a_in['Wgk1'], 'L0_attn_a_Wgk2': _L0_attn_a_in['Wgk2'], 'L0_attn_a_bgk2': _L0_attn_a_in['bgk2'], 'L0_attn_a_Wg': _L0_attn_a_in['Wg'], 'L0_attn_a_gnw': _L0_attn_a_in['gnw'], 'L0_attn_a_Wo': _L0_attn_a_in['Wo'], 'L0_attn_b_q_w': _L0_attn_b_in['q_w'], 'L0_attn_b_q_b': _L0_attn_b_in['q_b'], 'L0_attn_b_k_w': _L0_attn_b_in['k_w'], 'L0_attn_b_k_b': _L0_attn_b_in['k_b'], 'L0_attn_b_v_w': _L0_attn_b_in['v_w'], 'L0_attn_b_v_b': _L0_attn_b_in['v_b'], 'L0_attn_b_out_w': _L0_attn_b_in['out_w'], 'L0_attn_b_out_b': _L0_attn_b_in['out_b'], 'L0_attn_b_proj': _L0_attn_b_in['proj'], 'L0_attn_b_gamma': _L0_attn_b_in['gamma'], 'L0_attn_b_beta': _L0_attn_b_in['beta'], 'L0_ffn_W1': _L0_ffn_in['W1'], 'L0_ffn_W2': _L0_ffn_in['W2'], 'L0_ffn_ln_g': _L0_ffn_in['ln_g'], 'L0_ffn_ln_b': _L0_ffn_in['ln_b'], 'L0_ffn_router_W': _L0_ffn_in['router_W'], 'L0_ffn_router_b': _L0_ffn_in['router_b'], 'L0_ffn_raw_U': _L0_ffn_in['raw_U'], 'L0_ffn_raw_V': _L0_ffn_in['raw_V'], 'L0_ffn_gamma': _L0_ffn_in['gamma'], 'L1_attn_a_Wq': _L1_attn_a_in['Wq'], 'L1_attn_a_Wk': _L1_attn_a_in['Wk'], 'L1_attn_a_Wv': _L1_attn_a_in['Wv'], 'L1_attn_a_Wo': _L1_attn_a_in['Wo'], 'L1_attn_b_norm_w': _L1_attn_b_in['norm_w'], 'L1_attn_b_in_proj_w': _L1_attn_b_in['in_proj_w'], 'L1_attn_b_conv_w': _L1_attn_b_in['conv_w'], 'L1_attn_b_conv_b': _L1_attn_b_in['conv_b'], 'L1_attn_b_dt_bias': _L1_attn_b_in['dt_bias'], 'L1_attn_b_A_log': _L1_attn_b_in['A_log'], 'L1_attn_b_D': _L1_attn_b_in['D'], 'L1_attn_b_gnorm_w': _L1_attn_b_in['gnorm_w'], 'L1_attn_b_out_proj_w': _L1_attn_b_in['out_proj_w'], 'L1_ffn_wq': _L1_ffn_in['wq'], 'L1_ffn_wk': _L1_ffn_in['wk'], 'L1_ffn_wv': _L1_ffn_in['wv'], 'L1_ffn_wo': _L1_ffn_in['wo'], 'L1_ffn_w_router': _L1_ffn_in['w_router'], 'L1_ffn_wg': _L1_ffn_in['wg'], 'L1_ffn_wu': _L1_ffn_in['wu'], 'L1_ffn_wd': _L1_ffn_in['wd'], 'L1_ffn_g1': _L1_ffn_in['g1'], 'L1_ffn_g2': _L1_ffn_in['g2']}
    _x0 = _d['L0_attn_a_x']
    _d['L0_attn_a_x'] = jax.random.normal(jax.random.fold_in(jax.random.key(seed), 1), (8, 512, 128), dtype=_x0.dtype)
    del _x0
    return _d

def reference(L0_attn_a_x, L0_attn_a_Wq, L0_attn_a_Wk, L0_attn_a_Wv, L0_attn_a_Wgk1, L0_attn_a_Wgk2, L0_attn_a_bgk2, L0_attn_a_Wg, L0_attn_a_gnw, L0_attn_a_Wo, L0_attn_b_q_w, L0_attn_b_q_b, L0_attn_b_k_w, L0_attn_b_k_b, L0_attn_b_v_w, L0_attn_b_v_b, L0_attn_b_out_w, L0_attn_b_out_b, L0_attn_b_proj, L0_attn_b_gamma, L0_attn_b_beta, L0_ffn_W1, L0_ffn_W2, L0_ffn_ln_g, L0_ffn_ln_b, L0_ffn_router_W, L0_ffn_router_b, L0_ffn_raw_U, L0_ffn_raw_V, L0_ffn_gamma, L1_attn_a_Wq, L1_attn_a_Wk, L1_attn_a_Wv, L1_attn_a_Wo, L1_attn_b_norm_w, L1_attn_b_in_proj_w, L1_attn_b_conv_w, L1_attn_b_conv_b, L1_attn_b_dt_bias, L1_attn_b_A_log, L1_attn_b_D, L1_attn_b_gnorm_w, L1_attn_b_out_proj_w, L1_ffn_wq, L1_ffn_wk, L1_ffn_wv, L1_ffn_wo, L1_ffn_w_router, L1_ffn_wg, L1_ffn_wu, L1_ffn_wd, L1_ffn_g1, L1_ffn_g2):

    def _L0_attn_a_ref(x, Wq, Wk, Wv, Wgk1, Wgk2, bgk2, Wg, gnw, Wo):
        import jax, jax.numpy as jnp
        import numpy as np
        DIM = 128
        HEADS = 16
        KDIM = DIM // 2
        VDIM = DIM
        DK = KDIM // HEADS
        DV = VDIM // HEADS
        LOW = 16
        NORMALIZER = 16.0
        EPS = 1e-05
        B, T = (2, 512)

        def _gla_scan(q, k, v, gk):
            scale = DK ** (-0.5)

            def step(h, inp):
                qt, kt, vt, gt = inp
                h = h * jnp.exp(gt)[..., None] + kt[..., None] * vt[..., None, :]
                ot = jnp.einsum('bhk,bhkv->bhv', qt * scale, h)
                return (h, ot)
            h0 = jnp.zeros((q.shape[0], HEADS, DK, DV), q.dtype)
            xs = tuple((jnp.moveaxis(a, 1, 0) for a in (q, k, v, gk)))
            _, o = jax.lax.scan(step, h0, xs)
            return jnp.moveaxis(o, 0, 1)
        Bx, Tx, _ = x.shape
        q = (x @ Wq).reshape(Bx, Tx, HEADS, DK)
        k = (x @ Wk).reshape(Bx, Tx, HEADS, DK)
        v = (x @ Wv).reshape(Bx, Tx, HEADS, DV)
        gk = jax.nn.log_sigmoid(x @ Wgk1 @ Wgk2 + bgk2)
        gk = gk.reshape(Bx, Tx, HEADS, DK) / NORMALIZER
        o = _gla_scan(q, k, v, gk)
        g = (x @ Wg).reshape(Bx, Tx, HEADS, DV)
        o = o * jax.lax.rsqrt(jnp.mean(o * o, axis=-1, keepdims=True) + EPS) * gnw
        o = o * (g * jax.nn.sigmoid(g))
        return o.reshape(Bx, Tx, VDIM) @ Wo

    def _L0_attn_b_ref(x, q_w, q_b, k_w, k_b, v_w, v_b, out_w, out_b, proj, gamma, beta):
        import jax, jax.numpy as jnp
        import numpy as np
        B, S, E, H, M = (4, 256, 128, 16, 32)
        D = E // H
        LN_EPS = 1e-06

        def softmax_kernel(x, proj):
            x = x * (1.0 / jnp.sqrt(jnp.asarray(x.shape[-1], x.dtype)))
            mapping = jnp.einsum('bhsd,md->bhsm', x, proj)
            correction = jnp.sum(x * x, axis=-1, keepdims=True) * 0.5
            scaling = 1.0 / jnp.sqrt(jnp.asarray(proj.shape[0], x.dtype))
            return scaling * jnp.exp(mapping - correction)

        def favor_forward(x, q_w, q_b, k_w, k_b, v_w, v_b, out_w, out_b, proj, gamma, beta):
            b, s, e = x.shape
            split = lambda y: y.reshape(b, s, H, D).transpose(0, 2, 1, 3)
            Q = split(x @ q_w + q_b)
            K = split(x @ k_w + k_b)
            V = split(x @ v_w + v_b)
            qp = softmax_kernel(Q, proj).transpose(2, 0, 1, 3)
            kp = softmax_kernel(K, proj).transpose(2, 0, 1, 3)
            vs = V.transpose(2, 0, 1, 3)

            def step(carry, inp):
                ksum, kv = carry
                q, k, v = inp
                ksum = ksum + k
                kv = kv + k[..., :, None] * v[..., None, :]
                num = jnp.einsum('bhmd,bhm->bhd', kv, q)
                den = jnp.einsum('bhm,bhm->bh', q, ksum)
                return ((ksum, kv), (num, den))
            init = (jnp.zeros((b, H, M), x.dtype), jnp.zeros((b, H, M, D), x.dtype))
            _, (num, den) = jax.lax.scan(step, init, (qp, kp, vs))
            attn = num / den[..., None]
            attn = attn.transpose(1, 0, 2, 3).reshape(b, s, e)
            main = attn @ out_w + out_b
            res = main + x
            mu = jnp.mean(res, axis=-1, keepdims=True)
            var = jnp.mean(jnp.square(res - mu), axis=-1, keepdims=True)
            return gamma * (res - mu) * jax.lax.rsqrt(var + LN_EPS) + beta
        return favor_forward(x, q_w, q_b, k_w, k_b, v_w, v_b, out_w, out_b, proj, gamma, beta)

    def _L0_ffn_ref(x, W1, W2, ln_g, ln_b, router_W, router_b, raw_U, raw_V, gamma):
        import jax, jax.numpy as jnp
        import numpy as np
        TAU = 10.0
        EPS = 1e-06
        TOP_K = 8

        def _layernorm(x, g, b):
            mu = jnp.mean(x, axis=-1, keepdims=True)
            var = jnp.var(x, axis=-1, keepdims=True)
            return (x - mu) * jax.lax.rsqrt(var + 1e-05) * g + b

        def _unit_rows(W):
            n = jnp.linalg.norm(W, axis=1, keepdims=True)
            return W / jnp.maximum(n, EPS)
        B, S, D = x.shape
        x_flat = x.reshape(-1, D)
        r_raw = _layernorm(x_flat, ln_g, ln_b) @ router_W.T + router_b
        r = jnp.clip(r_raw, -TAU, TAU)
        alpha = jax.nn.softplus(r)
        phi, idx = jax.lax.top_k(alpha, TOP_K)
        S_sum = jnp.sum(phi, axis=-1, keepdims=True)
        Z = phi / (S_sum + EPS) * jnp.tanh(S_sum)
        U_sel = _unit_rows(raw_U)[idx]
        V_sel = _unit_rows(raw_V)[idx]
        h_lat = jnp.einsum('nd,nkd->nk', x_flat, U_sel)
        dyn = jnp.einsum('nk,nkd->nd', h_lat * Z, V_sel).reshape(B, S, D) * gamma
        static = (jax.nn.gelu(x_flat @ W1.T, approximate=False) @ W2.T).reshape(B, S, D)
        return static + dyn

    def _L1_attn_a_ref(hidden_states, Wq, Wk, Wv, Wo):
        import jax, jax.numpy as jnp
        import numpy as np
        B, L, D_MODEL = (4, 256, 128)
        N_HEADS, FEAT, HEAD_DIM = (16, 16, 64)
        CHUNK = 128
        EPS = 1e-12

        def taylor_exp(x):
            f = x.shape[-1]
            r2 = jnp.sqrt(jnp.asarray(2.0, x.dtype))
            rd = jnp.sqrt(jnp.asarray(float(f), x.dtype))
            rrd = jnp.sqrt(rd)
            x2 = (x[..., :, None] * x[..., None, :]).reshape(*x.shape[:-1], f * f) / r2
            ones = jnp.ones_like(x[..., :1])
            return jnp.concatenate([ones, x / rrd, x2 / rd], axis=-1)
        b, l, _ = hidden_states.shape
        q = (hidden_states @ Wq.T).reshape(b, l, N_HEADS, FEAT).transpose(0, 2, 1, 3)
        k = (hidden_states @ Wk.T).reshape(b, l, N_HEADS, FEAT).transpose(0, 2, 1, 3)
        v = (hidden_states @ Wv.T).reshape(b, l, N_HEADS, HEAD_DIM).transpose(0, 2, 1, 3)
        qf = taylor_exp(q)
        kf = taylor_exp(k)
        De = qf.shape[-1]
        n = l // CHUNK
        qc = jnp.moveaxis(qf.reshape(b, N_HEADS, n, CHUNK, De), 2, 0)
        kc = jnp.moveaxis(kf.reshape(b, N_HEADS, n, CHUNK, De), 2, 0)
        vc = jnp.moveaxis(v.reshape(b, N_HEADS, n, CHUNK, HEAD_DIM), 2, 0)
        mask = jnp.tril(jnp.ones((CHUNK, CHUNK), qf.dtype))

        def step(carry, xs):
            S, z = carry
            qi, ki, vi = xs
            attn = jnp.einsum('bhid,bhjd->bhij', qi, ki) * mask
            num = jnp.einsum('bhij,bhje->bhie', attn, vi) + jnp.einsum('bhid,bhde->bhie', qi, S)
            den = attn.sum(-1) + jnp.einsum('bhid,bhd->bhi', qi, z)
            yi = num / (den[..., None] + EPS)
            S = S + jnp.einsum('bhjd,bhje->bhde', ki, vi)
            z = z + ki.sum(2)
            return ((S, z), yi)
        S0 = jnp.zeros((b, N_HEADS, De, HEAD_DIM), qf.dtype)
        z0 = jnp.zeros((b, N_HEADS, De), qf.dtype)
        _, ys = jax.lax.scan(step, (S0, z0), (qc, kc, vc))
        y = jnp.moveaxis(ys, 0, 2).reshape(b, N_HEADS, l, HEAD_DIM)
        y = y.transpose(0, 2, 1, 3).reshape(b, l, N_HEADS * HEAD_DIM)
        return y @ Wo.T

    def _L1_attn_b_ref(x, norm_w, in_proj_w, conv_w, conv_b, dt_bias, A_log, D, gnorm_w, out_proj_w):
        import jax, jax.numpy as jnp
        import numpy as np
        B_, L_, DM = (2, 256, 128)
        DS, DC, EXP, HD = (128, 4, 2, 64)
        DI = EXP * DM
        NH = DI // HD
        CONV_DIM = DI + 2 * DS
        DIN = 2 * DI + 2 * DS + NH
        CS = 32
        EPS = 1e-05

        def _segsum(a):
            T = a.shape[-1]
            cs = jnp.cumsum(a, -1)
            seg = cs[..., :, None] - cs[..., None, :]
            mask = jnp.tril(jnp.ones((T, T), bool))
            return jnp.where(mask, seg, -jnp.inf)

        def _ssd(X, A, Bm, Cm):
            b, l, h, p = X.shape
            n, nc = (Bm.shape[-1], l // CS)
            X = X.reshape(b, nc, CS, h, p)
            A = A.reshape(b, nc, CS, h).transpose(0, 3, 1, 2)
            Bm = Bm.reshape(b, nc, CS, n)
            Cm = Cm.reshape(b, nc, CS, n)
            Acs = jnp.cumsum(A, -1)
            Lmat = jnp.exp(_segsum(A))
            Y_diag = jnp.einsum('bcln,bcsn,bhcls,bcshp->bclhp', Cm, Bm, Lmat, X)
            decay_states = jnp.exp(Acs[..., -1:] - Acs)
            states = jnp.einsum('bcln,bhcl,bclhp->bchpn', Bm, decay_states, X)
            states = jnp.concatenate([jnp.zeros_like(states[:, :1]), states], axis=1)
            decay_chunk = jnp.exp(_segsum(jnp.pad(Acs[..., -1], ((0, 0), (0, 0), (1, 0)))))
            states = jnp.einsum('bhzc,bchpn->bzhpn', decay_chunk, states)[:, :-1]
            Y_off = jnp.einsum('bcln,bchpn,bhcl->bclhp', Cm, states, jnp.exp(Acs))
            return (Y_diag + Y_off).reshape(b, l, h, p)

        def _forward(x, norm_w, in_proj_w, conv_w, conv_b, dt_bias, A_log, D, gnorm_w, out_proj_w):
            b, l, _ = x.shape
            xn = x * jax.lax.rsqrt(jnp.mean(x * x, -1, keepdims=True) + EPS) * norm_w
            zxbcdt = jnp.einsum('bld,ed->ble', xn, in_proj_w)
            z = zxbcdt[..., :DI]
            xBC = zxbcdt[..., DI:DI + CONV_DIM]
            dt = zxbcdt[..., -NH:]
            pad = jnp.pad(xBC, ((0, 0), (DC - 1, 0), (0, 0)))
            conv = sum((pad[:, k:k + l, :] * conv_w[:, k] for k in range(DC))) + conv_b
            xBC = conv * jax.nn.sigmoid(conv)
            xs = xBC[..., :DI]
            Bm = xBC[..., DI:DI + DS]
            Cm = xBC[..., DI + DS:]
            dt = jax.nn.softplus(dt + dt_bias)
            A = -jnp.exp(A_log)
            xh = xs.reshape(b, l, NH, HD)
            y = _ssd(xh * dt[..., None], dt * A, Bm, Cm)
            y = y + D[None, None, :, None] * xh
            y = y.reshape(b, l, DI)
            y = y * (z * jax.nn.sigmoid(z))
            y = y * jax.lax.rsqrt(jnp.mean(y * y, -1, keepdims=True) + EPS) * gnorm_w
            return x + jnp.einsum('bld,ed->ble', y, out_proj_w)
        return _forward(x, norm_w, in_proj_w, conv_w, conv_b, dt_bias, A_log, D, gnorm_w, out_proj_w)

    def _L1_ffn_ref(x, wq, wk, wv, wo, w_router, wg, wu, wd, g1, g2):
        import jax, jax.numpy as jnp
        import numpy as np
        EMBED = 128
        HEADS = 16
        HEAD_DIM = EMBED // HEADS
        NUM_EXPERTS = 8
        TOP_K = 2
        HIDDEN = (int(2 * (4 * EMBED) / 3) + 63) // 64 * 64
        SEQ = 256
        BATCH = 2
        ROPE_BASE = 10000.0
        EPS = 1e-06

        def _rope_tables(seq_len, dim):
            inv_freq = 1.0 / ROPE_BASE ** (np.arange(0, dim, 2, dtype=np.float32) / dim)
            t = np.arange(seq_len, dtype=np.float32)
            freqs = np.einsum('i,j->ij', t, inv_freq)
            emb = np.concatenate([freqs, freqs], axis=-1)
            return (jnp.asarray(np.cos(emb)), jnp.asarray(np.sin(emb)))

        def _rotate_half(x):
            x1, x2 = jnp.split(x, 2, axis=-1)
            return jnp.concatenate([-x2, x1], axis=-1)

        def _rmsnorm(x, w):
            return x * jax.lax.rsqrt(jnp.mean(x * x, axis=-1, keepdims=True) + EPS) * w

        def _attention(x, wq, wk, wv, wo):
            B, S, _ = x.shape
            q = (x @ wq).reshape(B, S, HEADS, HEAD_DIM).transpose(0, 2, 1, 3)
            k = (x @ wk).reshape(B, S, HEADS, HEAD_DIM).transpose(0, 2, 1, 3)
            v = (x @ wv).reshape(B, S, HEADS, HEAD_DIM).transpose(0, 2, 1, 3)
            cos, sin = _rope_tables(S, HEAD_DIM)
            cos = cos[None, None]
            sin = sin[None, None]
            q = q * cos + _rotate_half(q) * sin
            k = k * cos + _rotate_half(k) * sin
            scale = HEAD_DIM ** (-0.5)
            scores = jnp.einsum('bhqd,bhkd->bhqk', q, k) * scale
            causal = jnp.triu(jnp.ones((S, S), bool), k=1)
            scores = jnp.where(causal, -jnp.inf, scores)
            attn = jax.nn.softmax(scores, axis=-1)
            out = jnp.einsum('bhqk,bhkd->bhqd', attn, v)
            out = out.transpose(0, 2, 1, 3).reshape(B, S, EMBED)
            return out @ wo

        def _moe(x, w_router, wg, wu, wd):
            B, S, E = x.shape
            xf = x.reshape(-1, E)
            logits = xf @ w_router
            probs = jax.nn.softmax(logits, axis=-1)
            topw, topi = jax.lax.top_k(probs, TOP_K)
            topw = topw / jnp.sum(topw, axis=-1, keepdims=True)
            combine = jnp.sum(jax.nn.one_hot(topi, NUM_EXPERTS, dtype=xf.dtype) * topw[..., None], axis=1)
            g = jax.nn.silu(jnp.einsum('td,xdh->txh', xf, wg))
            u = jnp.einsum('td,xdh->txh', xf, wu)
            eo = jnp.einsum('txh,xhd->txd', g * u, wd)
            out = jnp.einsum('txd,tx->td', eo, combine)
            return out.reshape(B, S, E)
        h = x + _attention(_rmsnorm(x, g1), wq, wk, wv, wo)
        y = h + _moe(_rmsnorm(h, g2), w_router, wg, wu, wd)
        return y
    x = L0_attn_a_x
    x = x + _L0_attn_a_ref(_layernorm(x, axis=-1), L0_attn_a_Wq, L0_attn_a_Wk, L0_attn_a_Wv, L0_attn_a_Wgk1, L0_attn_a_Wgk2, L0_attn_a_bgk2, L0_attn_a_Wg, L0_attn_a_gnw, L0_attn_a_Wo)
    x = x + _L0_ffn_ref(_layernorm(x, axis=-1), L0_ffn_W1, L0_ffn_W2, L0_ffn_ln_g, L0_ffn_ln_b, L0_ffn_router_W, L0_ffn_router_b, L0_ffn_raw_U, L0_ffn_raw_V, L0_ffn_gamma)
    x = x + _L0_attn_b_ref(_layernorm(x, axis=-1), L0_attn_b_q_w, L0_attn_b_q_b, L0_attn_b_k_w, L0_attn_b_k_b, L0_attn_b_v_w, L0_attn_b_v_b, L0_attn_b_out_w, L0_attn_b_out_b, L0_attn_b_proj, L0_attn_b_gamma, L0_attn_b_beta)
    x = x + _L0_ffn_ref(_layernorm(x, axis=-1), L0_ffn_W1, L0_ffn_W2, L0_ffn_ln_g, L0_ffn_ln_b, L0_ffn_router_W, L0_ffn_router_b, L0_ffn_raw_U, L0_ffn_raw_V, L0_ffn_gamma)
    x = x + _L1_attn_a_ref(_layernorm(x, axis=-1), L1_attn_a_Wq, L1_attn_a_Wk, L1_attn_a_Wv, L1_attn_a_Wo)
    x = x + _L1_ffn_ref(_layernorm(x, axis=-1), L1_ffn_wq, L1_ffn_wk, L1_ffn_wv, L1_ffn_wo, L1_ffn_w_router, L1_ffn_wg, L1_ffn_wu, L1_ffn_wd, L1_ffn_g1, L1_ffn_g2)
    x = x + _L1_attn_b_ref(_layernorm(x, axis=-1), L1_attn_b_norm_w, L1_attn_b_in_proj_w, L1_attn_b_conv_w, L1_attn_b_conv_b, L1_attn_b_dt_bias, L1_attn_b_A_log, L1_attn_b_D, L1_attn_b_gnorm_w, L1_attn_b_out_proj_w)
    x = x + _L1_ffn_ref(_layernorm(x, axis=-1), L1_ffn_wq, L1_ffn_wk, L1_ffn_wv, L1_ffn_wo, L1_ffn_w_router, L1_ffn_wg, L1_ffn_wu, L1_ffn_wd, L1_ffn_g1, L1_ffn_g2)
    return x

_drawn_inputs = setup_inputs


def setup_inputs(seed=0):
    import zlib

    import numpy as np

    out = dict(_drawn_inputs(seed))
    spreads = {'L0_attn_a_bgk2': (0.0, 0.425),
     'L0_attn_a_gnw': (1.0, 0.2),
     'L0_attn_b_q_b': (0.0, 0.8),
     'L0_attn_b_k_b': (0.0, 0.8),
     'L0_attn_b_v_b': (0.0, 0.1),
     'L0_attn_b_out_b': (0.0, 0.1),
     'L0_attn_b_gamma': (1.0, 0.2),
     'L0_attn_b_beta': (0.0, 0.1),
     'L0_ffn_ln_g': (1.0, 0.6),
     'L0_ffn_ln_b': (0.0, 0.8),
     'L0_ffn_router_b': (0.0, 0.8),
     'L0_ffn_gamma': (0.10000000149011612, 0.6),
     'L1_attn_b_norm_w': (1.0, 0.6),
     'L1_attn_b_conv_b': (0.0, 0.1),
     'L1_attn_b_D': (1.0, 0.6),
     'L1_attn_b_gnorm_w': (1.0, 0.6),
     'L1_ffn_g1': (1.0, 0.6),
     'L1_ffn_g2': (1.0, 0.6)}
    factors = {'L0_ffn_router_W': 8.0,
     'L0_ffn_raw_U': 8.0,
     'L0_ffn_raw_V': 8.0,
     'L1_attn_a_Wq': 8.0,
     'L1_attn_a_Wk': 8.0,
     'L1_attn_a_Wv': 2.822,
     'L1_attn_a_Wo': 2.955,
     'L1_attn_b_dt_bias': 8.0,
     'L1_attn_b_A_log': 8.0,
     'L1_ffn_wq': 8.0,
     'L1_ffn_wk': 8.0,
     'L1_ffn_wv': 7.122,
     'L1_ffn_wo': 6.714,
     'L1_ffn_w_router': 8.0,
     'L1_ffn_wg': 8.0,
     'L1_ffn_wu': 8.0,
     'L1_ffn_wd': 8.0}
    for name, (base, spread) in spreads.items():
        noise = np.random.default_rng([zlib.crc32(name.encode()), seed]).standard_normal(out[name].shape)
        drawn = base * np.exp(spread * noise) if base else spread * noise
        out[name] = jnp.asarray(drawn.astype(out[name].dtype))
    for name, factor in factors.items():
        out[name] = (out[name] * factor).astype(out[name].dtype)
    return out
```

```python
from contextlib import ExitStack

import concourse.bass as bass
from concourse import mybir
import numpy as np

F32 = mybir.dt.float32
BF16 = mybir.dt.bfloat16
ALU = mybir.AluOpType
ACT = mybir.ActivationFunctionType
AX = mybir.AxisListType.X

P = 128
SEQS, SEQ_LEN, DIM = 8, 512, 128
TILES = SEQ_LEN // P
HEADS = 16
STAGES = "gla ffn favor ffn taylor moe ssd moe"


class Steps:

    def __init__(self, eng, sem, s, per):
        self.eng, self.sem, self.s, self.per, self.n = eng, sem, s, per, 0

    def __call__(self, ins):
        ins.then_inc(self.sem, 1)
        self.n += 1
        self.eng.wait_ge(self.sem, self.s * self.per + self.n)

    def end(self):
        assert self.n == self.per, (self.n, self.per)


def log1p_series():
    u = 0.5 - 0.5 * np.cos(np.pi * (np.arange(400) + 0.5) / 400)
    fit = np.polynomial.chebyshev.Chebyshev.fit(u, np.log1p(u) / u, 9, domain=[0, 1])
    return [float(c) for c in fit.convert(kind=np.polynomial.Polynomial).coef]



def parameter_blocks(i):
    f = lambda name: np.asarray(i[name])
    col = lambda v: v.reshape(-1, 1)
    row = lambda v: np.broadcast_to(v.reshape(1, -1), (P, v.size))
    tall = lambda w: w.reshape(-1, P, w.shape[-1]).transpose(1, 0, 2).reshape(P, -1)
    b = {}
    b["ident"] = np.eye(P)
    j, q = np.arange(P)[:, None], np.arange(P)[None, :]
    b["causal"] = (j <= q) * 1.0
    b["after"] = (j > q) * 1.0
    b["ones"] = np.ones((P, P))
    wq, wk, wv = (f("L0_attn_a_" + n) for n in ("Wq", "Wk", "Wv"))
    b["gla_wq"] = np.repeat(wq, 8, axis=1)
    b["gla_wk"] = np.repeat(wk, 8, axis=1)
    b["gla_wv"] = np.repeat(wv.reshape(P, HEADS, 1, 8), 4, axis=2).reshape(P, 512)
    b["gla_wgk1"] = f("L0_attn_a_Wgk1")
    b["gla_wgk2"] = f("L0_attn_a_Wgk2")
    b["gla_bgk2"] = col(f("L0_attn_a_bgk2"))
    b["gla_wg"] = f("L0_attn_a_Wg")
    b["gla_gnw"] = col(np.tile(f("L0_attn_a_gnw"), HEADS))
    b["gla_wo"] = f("L0_attn_a_Wo")
    b["gla_spread"] = (np.arange(64)[:, None] == np.arange(512)[None, :] // 8) * 1.0
    r, c = np.arange(512)[:, None], np.arange(P)[None, :]
    b["gla_sum"] = tall(((r // 32 == c // 8) & (r % 8 == c % 8)) * 1.0)
    b["head_mean"] = (j // 8 == q // 8) / 8.0
    b["ffn_w1"] = f("L0_ffn_W1").T
    b["ffn_w2"] = tall(f("L0_ffn_W2").T)
    b["ffn_ln_g"], b["ffn_ln_b"] = col(f("L0_ffn_ln_g")), col(f("L0_ffn_ln_b"))
    b["ffn_router"] = f("L0_ffn_router_W").T
    b["ffn_router_b"] = row(f("L0_ffn_router_b"))
    b["ffn_u_t"] = f("L0_ffn_raw_U").T
    b["ffn_u"], b["ffn_v"] = f("L0_ffn_raw_U"), f("L0_ffn_raw_V")
    b["ffn_gamma"] = row(f("L0_ffn_gamma"))
    for n in ("q", "k", "v", "out"):
        b[f"favor_{n}_w"] = f(f"L0_attn_b_{n}_w")
    b["favor_q_b"], b["favor_k_b"] = col(f("L0_attn_b_q_b")), col(f("L0_attn_b_k_b"))
    for n in ("v_b", "out_b", "gamma", "beta"):
        b[f"favor_{n}"] = row(f(f"L0_attn_b_{n}"))
    same = j // 8 == np.arange(512)[None, :] // 32
    b["favor_proj"] = np.where(same, np.tile(f("L0_attn_b_proj").T, (HEADS, HEADS)), 0.0)
    b["favor_minus"] = same * -0.5
    b["favor_own"] = (j // 32 == np.arange(36)[None, :] // 9) * 1.0
    for n in ("q", "k", "v"):
        b[f"taylor_w{n}"] = f(f"L1_attn_a_W{n}").T
    b["taylor_wo"] = tall(f("L1_attn_a_Wo").T)
    b["taylor_own"] = (np.arange(P)[:, None] // 16 == np.arange(8)[None, :]) * 1.0
    wide = (j <= np.arange(512)[None, :]) * 1.0
    b["taylor_causal"] = np.concatenate([wide, wide[:, :384], wide[:, :P], wide[:, :256]], axis=1)
    for n in ("q", "k", "v", "o"):
        b[f"attn_w{n}"] = f(f"L1_ffn_w{n}")
    half = np.arange(P) // 8 * 8 + (np.arange(P) + 4) % 8
    b["attn_wq_rot"], b["attn_wk_rot"] = f("L1_ffn_wq")[:, half], f("L1_ffn_wk")[:, half]
    inv_freq = 1.0 / 10000.0 ** (np.arange(0, 8, 2, dtype=np.float32) / 8)
    freqs = np.einsum("i,j->ij", np.arange(SEQ_LEN, dtype=np.float32), inv_freq)
    angle = np.tile(np.concatenate([freqs, freqs], axis=-1).T, (HEADS, 1))
    b["attn_cos"] = np.cos(angle)
    b["attn_sin"] = np.sin(angle) * np.where(np.arange(P) % 8 < 4, -1.0, 1.0)[:, None]
    b["attn_g1"], b["attn_g2"] = col(f("L1_ffn_g1")), col(f("L1_ffn_g2"))
    part_of = {"k": (0, 1, 0, 1, 2, 0), "q": (0, 0, 1, 1, 0, 2)}
    r, c = np.arange(P)[:, None], np.arange(P)[None, :]
    takes = (c < 96) & (r // 8 % 2 == c // 48) & (r % 8 == c % 8)
    b["attn_stack"] = np.concatenate([takes & (np.tile(np.repeat(part_of[side], 8), 3)[:P][None, :] == part)
                                      for side in "kq" for part in range(3)], axis=1) * 1.0
    b["attn_of_pair"] = (r // 16 == np.arange(8)[None, :]) * 1.0
    b["attn_of_head"] = (r // 48 == np.arange(2)[None, :]) * 1.0
    b["attn_pick"] = ((r < 8) & (r % 4 == np.arange(512)[None, :] // P)) * -1.0
    b["attn_den"] = ((r // 16 == c // 16) & (r % 16 == 8)) * 1.0
    wo = np.zeros((HEADS, 16, P), np.float32)
    wo[:, :8] = b.pop("attn_wo").reshape(HEADS, 8, P)
    b["attn_wo_rows"] = tall(wo.reshape(-1, P))
    b["future"] = (j > q) * -1e30
    b["moe_router"] = f("L1_ffn_w_router")
    b["moe_wg"] = f("L1_ffn_wg").transpose(1, 0, 2).reshape(P, -1)
    b["moe_wu"] = f("L1_ffn_wu").transpose(1, 0, 2).reshape(P, -1)
    b["moe_wd"] = tall(f("L1_ffn_wd").reshape(-1, P))
    b["moe_index"] = row(np.arange(8))
    ip = f("L1_attn_b_in_proj_w").T
    b["ssd_wz"], b["ssd_wx"], b["ssd_wdt"] = ip[:, 0:256], ip[:, 256:768], ip[:, 768:772]
    b["ssd_norm_w"] = col(f("L1_attn_b_norm_w"))
    b["ssd_conv_w"] = tall(f("L1_attn_b_conv_w"))
    b["ssd_conv_b"] = tall(col(f("L1_attn_b_conv_b")))
    b["ssd_dt_bias"], b["ssd_a_log"] = row(f("L1_attn_b_dt_bias")), row(f("L1_attn_b_A_log"))
    b["ssd_d"] = row(np.repeat(f("L1_attn_b_D"), 64))
    b["ssd_gnorm_w"] = tall(col(f("L1_attn_b_gnorm_w")))
    b["ssd_wo"] = tall(f("L1_attn_b_out_proj_w").T)
    return {k: np.ascontiguousarray(v, dtype=np.float32) for k, v in b.items()}


EARLY, LATE = ("gla", "ffn", "favor"), ("moe",)
RUN = 512
GROUPS = {"common": ("ident", "causal", "after", "ones"), "gla": ("gla_", "head_mean"), "ffn": ("ffn_",), "favor": ("favor_",),
          "taylor": ("taylor_",), "moe": ("attn_", "moe_", "future"), "ssd": ("ssd_",)}


def placed(blocks):
    at, out, groups = 0, {}, {}
    for group, starts in GROUPS.items():
        first = at
        for name, a in blocks.items():
            if (name in starts) if group == "common" else (name.startswith(starts) and name not in GROUPS["common"]):
                out[name] = (at, *a.shape)
                at += a.shape[1]
        at = -(-at // RUN) * RUN
        groups[group] = (first, at)
    assert len(out) == len(blocks)
    return out, groups, at


def carry_wait(nc, spare):
    nc.vector.tensor_copy(spare[:, 0:1], spare[:, 1:2])


def norm_vector(nc, dve, step, stats, mean_var, rows, fence):
    for t in range(TILES):
        last = nc.vector.bn_stats(stats[:, t, :], rows(t))
    step(last)
    carry_wait(nc, fence)
    for t in range(TILES):
        last = nc.vector.bn_aggr(mean_var[:, t, :], stats[:, t, :])
    return last


def refine_rsqrt(nc, step, out, var, eps, guess, tmp):
    step(nc.vector.scalar_tensor_tensor(tmp, var, eps, guess, ALU.add, ALU.mult))
    step(nc.vector.tensor_tensor(tmp, tmp, guess, ALU.mult))
    step(nc.vector.tensor_scalar(tmp, tmp, -0.5, 1.5, ALU.mult, ALU.add))
    return nc.vector.tensor_tensor(out, tmp, guess, ALU.mult)


class Norm:

    def __init__(self, nc, ctx, k, name, eps, rms=False):
        sb = lambda n, shape: ctx.enter_context(nc.sbuf_tensor(f"{name}_{n}", shape, F32))
        sem = lambda n: k.semaphore(ctx, f"{name}_{n}")
        self.nc, self.k, self.eps, self.rms = nc, k, eps, rms
        self.stats_, self.mean_var = sb("stats", [P, TILES, 6]), sb("mean_var", [P, TILES, 2])
        self.guess, self.rstd, self.tmp = (sb(n, [P, TILES]) for n in ("guess", "rstd", "tmp"))
        self.dve_step, self.act_step = sem("dve_step"), sem("act_step")
        self.var_ready, self.guess_ready, self.rows_ready = sem("var_ready"), sem("guess_ready"), sem("rows_ready")

    def stats(self, dve, s, rows):
        nc, per = self.nc, 7 if self.rms else 5
        self.step = Steps(dve, self.dve_step, s, per)
        for t in range(TILES):
            last = nc.vector.bn_stats(self.stats_[:, t, :], rows(t))
        self.step(last)
        carry_wait(nc, self.k.spare)
        for t in range(TILES):
            last = nc.vector.bn_aggr(self.mean_var[:, t, :], self.stats_[:, t, :])
        if self.rms:
            mean, var = self.mean_var[:, :, 0], self.mean_var[:, :, 1]
            self.step(last)
            self.step(nc.vector.tensor_tensor(mean, mean, mean, ALU.mult))
            last = nc.vector.tensor_tensor(var, var, mean, ALU.add)
        last.then_inc(self.var_ready, 1)

    def first_guess(self, act, s):
        nc = self.nc
        act.wait_ge(self.var_ready, s + 1)
        nc.scalar.activation(self.guess[:, :], self.mean_var[:, :, 1], ACT.Ln, bias=self.k.const(self.eps)).then_inc(self.act_step, 1)
        act.wait_ge(self.act_step, s + 1)
        nc.scalar.activation(self.guess[:, :], self.guess[:, :], ACT.Exp, scale=-0.5).then_inc(self.guess_ready, 1)

    def scale(self, dve, s, out, rows):
        nc, step = self.nc, self.step
        dve.wait_ge(self.guess_ready, s + 1)
        step(refine_rsqrt(nc, step, self.rstd[:, :], self.mean_var[:, :, 1], self.eps, self.guess[:, :], self.tmp[:, :]))
        for t in range(TILES):
            if self.rms:
                last = nc.vector.tensor_scalar(out(t), rows(t), self.rstd[:, t:t + 1], None, ALU.mult)
            else:
                last = nc.vector.tensor_scalar(out(t), rows(t), self.mean_var[:, t, 0:1], self.rstd[:, t:t + 1],
                                               ALU.subtract, ALU.mult)
        last.then_inc(self.rows_ready, 1)
        step.end()


def transpose_tiles(nc, pe, bank, rows, ident):
    for t in range(TILES):
        r = rows(t)
        last = nc.tensor.transpose(bank[:, t * P:(t + 1) * P], r, ident)
    return last


def gla_stage(nc, k, n_stage):
    with ExitStack() as ctx:
        sb = lambda name, shape: ctx.enter_context(nc.sbuf_tensor("gla_" + name, shape, F32))
        sem = lambda name: k.semaphore(ctx, "gla_" + name)
        stats, mean_var = sb("stats", [P, TILES, 6]), sb("mean_var", [P, TILES, 2])
        guess, rstd, tmp = sb("guess", [P, TILES]), sb("rstd", [P, TILES]), sb("tmp", [P, TILES])
        xn, xT = sb("xn", [P, TILES, P]), sb("xT", [P, 512])
        low = sb("low", [16, 512])
        gate, gate_abs, gate_log = sb("gate", [64, 512]), sb("gate_abs", [64, 512]), sb("gate_log", [64, 512])
        decay = sb("decay", [64, 512])
        val, kv, hid = sb("val", [P, 2, 512]), sb("kv", [P, 512]), sb("hid", [P, 512])
        qh = sb("qh", [P, TILES, 512])
        osq, olog, orstd, gsil = sb("osq", [P, 512]), sb("olog", [P, 512]), sb("orstd", [P, 512]), sb("gsil", [P, 512])
        og = sb("og", [P, 512])
        dve_step, act_step = sem("dve_step"), sem("act_step")
        var_ready, guess_ready, xn_ready, xnT_ready, xT_ready = (sem(n) for n in ("var_ready", "guess_ready", "xn_ready", "xnT_ready", "xT_ready"))
        low_done, low_ready, z_done, zlog_ready, zmin_ready, decay_ready = (
            sem(n) for n in ("low_done", "low_ready", "z_done", "zlog_ready", "zmin_ready", "decay_ready"))
        kvq_done, val_ready, kv_ready, scan_done, qh_ready = (sem(n) for n in ("kvq_done", "val_ready", "kv_ready", "scan_done", "qh_ready"))
        o_done, g_done, osq_ready, ms_done, orstd_ready, gsil_ready, og_ready, y_done = (
            sem(n) for n in ("o_done", "g_done", "osq_ready", "ms_done", "orstd_ready", "gsil_ready", "og_ready", "y_done"))
        pxT, pk, pv, pq, pa, po, pm, py = k.banks
        w = k.w

        with nc.Block() as block:
            @block.vector
            def _(dve):
                k.await_parameters(dve, "gla")
                with dve.Fori(0, SEQS) as s:
                    step = Steps(dve, dve_step, s, 7)
                    xs = k.x[:, bass.ds(s * TILES, TILES), :]
                    norm_vector(nc, dve, step, stats, mean_var, lambda t: k.x[:, bass.ds(s * TILES + t, 1), :],
                                k.spare).then_inc(var_ready, 1)
                    dve.wait_ge(guess_ready, s + 1)
                    step(refine_rsqrt(nc, step, rstd[:, :], mean_var[:, :, 1], 1e-5, guess[:, :], tmp[:, :]))
                    for t in range(TILES):
                        nc.vector.tensor_scalar(xn[:, t, :], k.x[:, bass.ds(s * TILES + t, 1), :],
                                                mean_var[:, t, 0:1], rstd[:, t:t + 1],
                                                ALU.subtract, ALU.mult).then_inc(xn_ready, 1)
                    dve.wait_ge(zlog_ready, s + 1)
                    nc.vector.scalar_tensor_tensor(gate_log[:, :], gate[:, :], 0.0, gate_log[:, :], ALU.min,
                                                   ALU.subtract).then_inc(zmin_ready, 1)
                    for t in range(TILES):
                        dve.wait_ge(val_ready, s * TILES + t + 1)
                        nc.vector.tensor_tensor(kv[:, :], pk[:, :], val[:, t % 2, :], ALU.mult).then_inc(kv_ready, 1)
                        dve.wait_ge(kv_ready, s * TILES + t + 1)
                        nc.vector.tensor_tensor_scan(hid[:, :], pa[:, :], kv[:, :], 0.0, ALU.mult, ALU.add).then_inc(scan_done, 1)
                        dve.wait_ge(scan_done, s * TILES + t + 1)
                        nc.vector.scalar_tensor_tensor(qh[:, t, :], pq[:, :], 0.5, hid[:, :], ALU.mult,
                                                       ALU.mult).then_inc(qh_ready, 1)
                    dve.wait_ge(orstd_ready, s + 1)
                    step(nc.vector.scalar_tensor_tensor(og[:, :], po[:, :], w("gla_gnw"), orstd[:, :], ALU.mult, ALU.mult))
                    dve.wait_ge(gsil_ready, s + 1)
                    nc.vector.tensor_tensor(og[:, :], og[:, :], gsil[:, :], ALU.mult).then_inc(og_ready, 1)
                    dve.wait_ge(y_done, s + 1)
                    step(nc.vector.tensor_tensor(xs, xs, py[:, :].rearrange("p (t d) -> p t d", d=P), ALU.add))
                    step.end()

            @block.scalar
            def _(act):
                k.await_parameters(act, "gla")
                nc.scalar.preload_act_table_set("natural_log_exp_and_others")
                with act.Fori(0, SEQS) as s:
                    step = Steps(act, act_step, s, 6)
                    nc.scalar.preload_act_table_set("natural_log_exp_and_others")
                    act.wait_ge(var_ready, s + 1)
                    step(nc.scalar.activation(guess[:, :], mean_var[:, :, 1], ACT.Ln, bias=k.const(1e-5)))
                    nc.scalar.activation(guess[:, :], guess[:, :], ACT.Exp, scale=-0.5).then_inc(guess_ready, 1)
                    act.wait_ge(xnT_ready, s + 1)
                    nc.scalar.copy(xT[:, :], pxT[:, :]).then_inc(xT_ready, 1)
                    act.wait_ge(low_done, s + 1)
                    nc.scalar.copy(low[:, :], pa[0:16, :]).then_inc(low_ready, 1)
                    act.wait_ge(z_done, s + 1)
                    step(nc.scalar.activation(gate[:, :], pa[0:64, :], ACT.Identity, bias=w("gla_bgk2")))
                    step(nc.scalar.activation(gate_abs[:, :], gate[:, :], ACT.Abs))
                    step(nc.scalar.activation(gate_abs[:, :], gate_abs[:, :], ACT.Exp, scale=-1.0))
                    nc.scalar.activation(gate_log[:, :], gate_abs[:, :], ACT.Ln, bias=k.const(1.0)[0:64, :]).then_inc(zlog_ready, 1)
                    act.wait_ge(zmin_ready, s + 1)
                    nc.scalar.activation(decay[:, :], gate_log[:, :], ACT.Exp, scale=1 / 16).then_inc(decay_ready, 1)
                    for t in range(TILES):
                        act.wait_ge(kvq_done, s * TILES + t + 1)
                        nc.scalar.copy(val[:, t % 2, :], pv[:, :]).then_inc(val_ready, 1)
                    act.wait_ge(o_done, s + 1)
                    nc.scalar.activation(osq[:, :], po[:, :], ACT.Square).then_inc(osq_ready, 1)
                    act.wait_ge(ms_done, s + 1)
                    step(nc.scalar.activation(olog[:, :], pm[:, :], ACT.Ln, bias=k.const(1e-5)))
                    nc.scalar.activation(orstd[:, :], olog[:, :], ACT.Exp, scale=-0.5).then_inc(orstd_ready, 1)
                    act.wait_ge(g_done, s + 1)
                    step(nc.scalar.activation(gsil[:, :], pk[:, :], ACT.Silu))
                    nc.scalar.copy(gsil[:, :], gsil[:, :]).then_inc(gsil_ready, 1)
                    step.end()

            @block.tensor
            def _(pe):
                k.await_parameters(pe, "gla")
                mm = nc.tensor.matmul
                with pe.Fori(0, SEQS) as s:
                    for t in range(TILES):
                        pe.wait_ge(xn_ready, s * TILES + t + 1)
                        last = nc.tensor.transpose(pxT[:, t * P:(t + 1) * P], xn[:, t, :], w("ident"))
                    last.then_inc(xnT_ready, 1)
                    pe.wait_ge(xT_ready, s + 1)
                    mm(pa[0:16, :], w("gla_wgk1"), xT[:, :], start=True, stop=True).then_inc(low_done, 1)
                    pe.wait_ge(low_ready, s + 1)
                    mm(pa[0:64, :], w("gla_wgk2"), low[:, :], start=True, stop=True).then_inc(z_done, 1)
                    for t in range(TILES):
                        if t == 0:
                            pe.wait_ge(decay_ready, s + 1)
                        else:
                            pe.wait_ge(qh_ready, s * TILES + t)
                        c = slice(t * P, (t + 1) * P)
                        mm(pa[:, :], w("gla_spread")[:, c], decay[:, :], start=True, stop=True)
                        mm(pk[:, :], w("gla_wk")[:, c], xT[:, :], start=True, stop=True)
                        mm(pq[:, :], w("gla_wq")[:, c], xT[:, :], start=True, stop=True)
                        mm(pv[:, :], w("gla_wv")[:, c], xT[:, :], start=True, stop=True).then_inc(kvq_done, 1)
                    pe.wait_ge(qh_ready, s * TILES + TILES)
                    for t in range(TILES):
                        last = mm(po[:, :], w("gla_sum")[:, t * P:(t + 1) * P], qh[:, t, :], start=(t == 0), stop=(t == TILES - 1))
                    last.then_inc(o_done, 1)
                    mm(pk[:, :], w("gla_wg"), xT[:, :], start=True, stop=True).then_inc(g_done, 1)
                    pe.wait_ge(osq_ready, s + 1)
                    mm(pm[:, :], w("head_mean"), osq[:, :], start=True, stop=True).then_inc(ms_done, 1)
                    pe.wait_ge(og_ready, s + 1)
                    for t in range(TILES):
                        last = mm(py[:, t * P:(t + 1) * P], og[:, t * P:(t + 1) * P], w("gla_wo"), start=True, stop=True)
                    last.then_inc(y_done, 1)


def ffn_stage(nc, k, n_stage):
    NB = 64
    LOG1P = log1p_series()
    with ExitStack() as ctx:
        sb = lambda name, shape: ctx.enter_context(nc.sbuf_tensor(f"ffn{n_stage}_{name}", shape, F32))
        sem = lambda name: k.semaphore(ctx, f"ffn{n_stage}_{name}")
        w = k.w
        outer = Norm(nc, ctx, k, f"ffn{n_stage}_outer", 1e-5)
        inner = Norm(nc, ctx, k, f"ffn{n_stage}_inner", 1e-5)
        xin, xinT = sb("xin", [P, TILES, P]), sb("xinT", [P, 512])
        yn, yT = sb("yn", [P, TILES, P]), sb("yT", [P, 512])
        norms, inv_norms, inv_tmp = sb("norms", [NB, 2]), sb("inv_norms", [NB, 2]), sb("inv_tmp", [NB, 2])
        squares, v_gamma, unit_scale = sb("squares", [NB, P]), sb("v_gamma", [NB, P]), sb("unit_scale", [NB, 1])
        logits, rest, top = sb("logits", [P, TILES, NB]), sb("rest", [P, TILES, NB]), sb("top", [P, TILES, 8])
        u, series = sb("u", [P, TILES, NB]), sb("series", [P, TILES, NB])
        total, total_tanh, factor = sb("total", [P, TILES]), sb("total_tanh", [P, TILES]), sb("factor", [P, TILES])
        hz, hzT = sb("hz", [P, TILES, P]), sb("hzT", [NB, 512])
        hidden = sb("hidden", [P, 4, 512])
        dve_step, act_step = sem("dve_step"), sem("act_step")
        norms_ready, inv_guess, unit_ready = sem("norms_ready"), sem("inv_guess"), sem("unit_ready")
        xinT_done, xinT_ready, ynT_done, yT_ready = (sem(n) for n in ("xinT_done", "xinT_ready", "ynT_done", "yT_ready"))
        logits_done, logits_ready, u_ready, total_ready, tanh_ready, latent_done = (
            sem(n) for n in ("logits_done", "logits_ready", "u_ready", "total_ready", "tanh_ready", "latent_done"))
        hz_ready, hzT_done, hzT_ready, hidden_done, hidden_ready, out_done = (
            sem(n) for n in ("hz_ready", "hzT_done", "hzT_ready", "hidden_done", "hidden_ready", "out_done"))
        pxT, pyT, pr, pz, ph0, ph1, plat, py = k.banks
        latent = plat[:, 0:TILES * NB].rearrange("p (t n) -> p t n", n=NB)
        router_out = pr[:, 0:TILES * NB].rearrange("p (t n) -> p t n", n=NB)

        with nc.Block() as block:
            @block.vector
            def _(dve):
                k.await_parameters(dve, "ffn")
                step = Steps(dve, norms_ready, 0, 0)
                dve.wait_ge(unit_ready, 2)
                step(nc.vector.tensor_scalar(norms[:, :], norms[:, :], 1e-12, None, ALU.max))
                dve.wait_ge(inv_guess, 1)
                step(refine_rsqrt(nc, step, inv_norms[:, :], norms[:, :], 0.0, inv_norms[:, :], inv_tmp[:, :]))
                step(nc.vector.tensor_tensor(unit_scale[:, :], inv_norms[:, 0:1], inv_norms[:, 1:2], ALU.mult))
                step(nc.vector.tensor_tensor(v_gamma[:, :], w("ffn_v"), w("ffn_gamma")[0:NB, :], ALU.mult))
                step(nc.vector.memset(hz[:, :, NB:P], 0.0))
                with dve.Fori(0, SEQS) as s:
                    outer.stats(dve, s, lambda t: k.x[:, bass.ds(s * TILES + t, 1), :])
                    outer.scale(dve, s, lambda t: xin[:, t, :], lambda t: k.x[:, bass.ds(s * TILES + t, 1), :])
                    dve.wait_ge(outer.rows_ready, s + 1)
                    inner.stats(dve, s, lambda t: xin[:, t, :])
                    inner.scale(dve, s, lambda t: yn[:, t, :], lambda t: xin[:, t, :])
                    step = Steps(dve, dve_step, s, 21)
                    dve.wait_ge(logits_done, s + 1)
                    step(nc.vector.tensor_tensor(logits[:, :, :], router_out, w("ffn_router_b").unsqueeze(1).broadcast_to([P, TILES, NB]), ALU.add))
                    nc.vector.tensor_scalar(logits[:, :, :], logits[:, :, :], 10.0, -10.0, ALU.min, ALU.max).then_inc(logits_ready, 1)
                    dve.wait_ge(logits_ready, s + 1)
                    carry_wait(nc, k.spare)
                    for t in range(TILES):
                        last = nc.vector.max(top[:, t, :], logits[:, t, :])
                    step(last)
                    carry_wait(nc, k.spare)
                    for t in range(TILES):
                        last = nc.vector.match_replace(rest[:, t, :], top[:, t, :], logits[:, t, :], -1e30)
                    step(last)
                    step(nc.vector.tensor_tensor(rest[:, :, :], rest[:, :, :], logits[:, :, :], ALU.not_equal))
                    dve.wait_ge(u_ready, s + 1)
                    step(nc.vector.tensor_scalar(series[:, :, :], u[:, :, :], LOG1P[9], None, ALU.mult))
                    for n in range(8, -1, -1):
                        step(nc.vector.scalar_tensor_tensor(series[:, :, :], series[:, :, :], LOG1P[n], u[:, :, :], ALU.add, ALU.mult))
                    step(nc.vector.scalar_tensor_tensor(series[:, :, :], logits[:, :, :], 0.0, series[:, :, :], ALU.max, ALU.add))
                    step(nc.vector.tensor_tensor(rest[:, :, :], rest[:, :, :], series[:, :, :], ALU.mult))
                    nc.vector.reduce_sum(total[:, :], rest[:, :, :], AX).then_inc(total_ready, 1)
                    dve.wait_ge(total_ready, s + 1)
                    step(nc.vector.tensor_scalar(factor[:, :], total[:, :], 1e-6, None, ALU.add))
                    step(nc.vector.reciprocal(factor[:, :], factor[:, :]))
                    dve.wait_ge(tanh_ready, s + 1)
                    step(nc.vector.tensor_tensor(factor[:, :], factor[:, :], total_tanh[:, :], ALU.mult))
                    step(nc.vector.tensor_tensor(rest[:, :, :], rest[:, :, :], factor[:, :].unsqueeze(2).broadcast_to([P, TILES, NB]), ALU.mult))
                    dve.wait_ge(latent_done, s + 1)
                    nc.vector.tensor_tensor(hz[:, :, 0:NB], latent, rest[:, :, :], ALU.mult).then_inc(hz_ready, 1)
                    dve.wait_ge(out_done, s + 1)
                    xs = k.x[:, bass.ds(s * TILES, TILES), :]
                    step(nc.vector.tensor_tensor(xs, xs, py[:, :].rearrange("p (t d) -> p t d", d=P), ALU.add))
                    step.end()

            @block.scalar
            def _(act):
                k.await_parameters(act, "ffn")
                nc.scalar.preload_act_table_set("natural_log_exp_and_others")
                for n, name in enumerate(("ffn_u", "ffn_v")):
                    nc.scalar.activation(squares[:, :], w(name), ACT.Square, accum_out=norms[:, n:n + 1]).then_inc(unit_ready, 1)
                    act.wait_ge(unit_ready, n + 1)
                act.wait_ge(norms_ready, 1)
                nc.scalar.activation(inv_norms[:, :], norms[:, :], ACT.Ln).then_inc(unit_ready, 1)
                act.wait_ge(unit_ready, 3)
                nc.scalar.activation(inv_norms[:, :], inv_norms[:, :], ACT.Exp, scale=-0.5).then_inc(inv_guess, 1)
                with act.Fori(0, SEQS) as s:
                    nc.scalar.preload_act_table_set("natural_log_exp_and_others")
                    outer.first_guess(act, s)
                    act.wait_ge(xinT_done, s + 1)
                    nc.scalar.copy(xinT[:, :], pxT[:, :]).then_inc(xinT_ready, 1)
                    inner.first_guess(act, s)
                    act.wait_ge(ynT_done, s + 1)
                    nc.scalar.activation(yT[:, :], pyT[:, :], ACT.Identity, scale=w("ffn_ln_g"), bias=w("ffn_ln_b")).then_inc(yT_ready, 1)
                    act.wait_ge(logits_ready, s + 1)
                    step = Steps(act, act_step, s, 1)
                    step(nc.scalar.activation(u[:, :, :], logits[:, :, :], ACT.Abs))
                    nc.scalar.activation(u[:, :, :], u[:, :, :], ACT.Exp, scale=-1.0).then_inc(u_ready, 1)
                    step.end()
                    for m in range(4):
                        act.wait_ge(hidden_done, s * 4 + m + 1)
                        nc.scalar.activation(hidden[:, m, :], (ph0, ph1)[m % 2][:, :], ACT.Gelu).then_inc(hidden_ready, 1)
                    act.wait_ge(total_ready, s + 1)
                    nc.scalar.activation(total_tanh[:, :], total[:, :], ACT.Tanh).then_inc(tanh_ready, 1)
                    act.wait_ge(hzT_done, s + 1)
                    nc.scalar.activation(hzT[:, :], pz[0:NB, :], ACT.Identity, scale=unit_scale[:, :]).then_inc(hzT_ready, 1)

            @block.tensor
            def _(pe):
                k.await_parameters(pe, "ffn")
                mm = nc.tensor.matmul
                with pe.Fori(0, SEQS) as s:
                    pe.wait_ge(outer.rows_ready, s + 1)
                    transpose_tiles(nc, pe, pxT, lambda t: xin[:, t, :], w("ident")).then_inc(xinT_done, 1)
                    pe.wait_ge(inner.rows_ready, s + 1)
                    transpose_tiles(nc, pe, pyT, lambda t: yn[:, t, :], w("ident")).then_inc(ynT_done, 1)
                    pe.wait_ge(yT_ready, s + 1)
                    for t in range(TILES):
                        last = mm(pr[:, t * NB:(t + 1) * NB], yT[:, t * P:(t + 1) * P], w("ffn_router"), start=True, stop=True)
                    last.then_inc(logits_done, 1)
                    pe.wait_ge(xinT_ready, s + 1)
                    for t in range(TILES):
                        last = mm(plat[:, t * NB:(t + 1) * NB], xinT[:, t * P:(t + 1) * P], w("ffn_u_t"), start=True, stop=True)
                    last.then_inc(latent_done, 1)
                    for m in range(4):
                        if m >= 2:
                            pe.wait_ge(hidden_ready, s * 4 + m - 1)
                        mm((ph0, ph1)[m % 2][:, :], w("ffn_w1")[:, m * P:(m + 1) * P], xinT[:, :], start=True, stop=True).then_inc(hidden_done, 1)
                    pe.wait_ge(hz_ready, s + 1)
                    transpose_tiles(nc, pe, pz, lambda t: hz[:, t, :], w("ident")).then_inc(hzT_done, 1)
                    pe.wait_ge(hidden_ready, s * 4 + 4)
                    pe.wait_ge(hzT_ready, s + 1)
                    for t in range(TILES):
                        c = slice(t * P, (t + 1) * P)
                        for m in range(4):
                            mm(py[:, c], hidden[:, m, c], w("ffn_w2")[:, m * P:(m + 1) * P], start=(m == 0), stop=False)
                        last = mm(py[:, c], hzT[:, c], v_gamma[:, :], start=False, stop=True)
                    last.then_inc(out_done, 1)


def favor_stage(nc, k, n_stage):
    M, D = 32, 8
    VW = D + 1
    GROUP = 4
    SCALE = D ** -0.5
    with ExitStack() as ctx:
        sb = lambda name, shape: ctx.enter_context(nc.sbuf_tensor("favor_" + name, shape, F32))
        sem = lambda name: k.semaphore(ctx, "favor_" + name)
        w = k.w
        outer = Norm(nc, ctx, k, "favor_outer", 1e-5)
        post = Norm(nc, ctx, k, "favor_post", 1e-6)
        xin, xinT = sb("xin", [P, TILES, P]), sb("xinT", [P, 512])
        biases = sb("biases", [P, 2])
        q, kk, q2, k2 = (sb(n, [P, 512]) for n in ("q", "k", "q2", "k2"))
        vals = sb("vals", [P, TILES, HEADS, VW])
        qf, kf = sb("qf", [P, TILES, 512]), sb("kf", [P, TILES, 512])
        kf_tok = sb("kf_tok", [P, TILES, 512])
        weights = sb("weights", [P, 2, GROUP, 512])
        state, added = sb("state", [P, 2, TILES, GROUP * VW]), sb("added", [P, TILES, GROUP * VW])
        inv_den = sb("inv_den", [P, HEADS])
        attn, attnT = sb("attn", [P, TILES, HEADS, D]), sb("attnT", [P, 512])
        res, resn = sb("res", [P, TILES, P]), sb("resn", [P, TILES, P])
        dve_step, set_up = sem("dve_step"), sem("set_up")
        xinT_done, xinT_ready, q_done, k_done, v_done, v_ready, q_ready, k_ready, q2_ready, k2_ready = (
            sem(n) for n in ("xinT_done", "xinT_ready", "q_done", "k_done", "v_done", "v_ready", "q_ready", "k_ready", "q2_ready", "k2_ready"))
        feat_done, feat_ready, score_done, weight_ready, before_done, added_done, state_ready, sum_done, attn_ready = (
            sem(n) for n in ("feat_done", "feat_ready", "score_done", "weight_ready", "before_done", "added_done", "state_ready", "sum_done", "attn_ready"))
        attnT_done, attnT_ready, out_done, res_ready = (sem(n) for n in ("attnT_done", "attnT_ready", "out_done", "res_ready"))
        p_t, p_sum, p_add, p_tok = k.banks[0:4]
        p_q, p_k = p_sum, p_add
        p_feat = k.banks[4:8]
        sums = p_sum[:, 0:HEADS * VW].rearrange("p (h v) -> p h v", v=VW)
        tok = p_tok[:, :].rearrange("p (t d) -> p t d", d=P)

        with nc.Block() as block:
            @block.vector
            def _(dve):
                k.await_parameters(dve, "favor")
                nc.vector.memset(vals[:, :, :, D:VW], 1.0).then_inc(set_up, 1)
                nc.vector.tensor_scalar(biases[:, 0:1], w("favor_q_b"), SCALE, None, ALU.mult).then_inc(set_up, 1)
                nc.vector.tensor_scalar(biases[:, 1:2], w("favor_k_b"), SCALE, None, ALU.mult).then_inc(set_up, 1)
                with dve.Fori(0, SEQS) as s:
                    xs = k.x[:, bass.ds(s * TILES, TILES), :]
                    outer.stats(dve, s, lambda t: k.x[:, bass.ds(s * TILES + t, 1), :])
                    outer.scale(dve, s, lambda t: xin[:, t, :], lambda t: k.x[:, bass.ds(s * TILES + t, 1), :])
                    dve.wait_ge(v_done, s + 1)
                    nc.vector.tensor_tensor(vals[:, :, :, 0:D], p_tok[:, :].rearrange("p (t h d) -> p t h d", h=HEADS, d=D),
                                            w("favor_v_b").rearrange("p (h d) -> p h d", d=D).unsqueeze(1).broadcast_to([P, TILES, HEADS, D]),
                                            ALU.add).then_inc(v_ready, 1)
                    dve.wait_ge(q_ready, s + 1)
                    nc.vector.tensor_tensor(q2[:, :], q[:, :], q[:, :], ALU.mult).then_inc(q2_ready, 1)
                    dve.wait_ge(k_ready, s + 1)
                    nc.vector.tensor_tensor(k2[:, :], kk[:, :], kk[:, :], ALU.mult).then_inc(k2_ready, 1)
                    step = Steps(dve, dve_step, s, 10)
                    for c in range(TILES):
                        for r in range(GROUP):
                            dve.wait_ge(score_done, (s * TILES + c) * GROUP + r + 1)
                            nc.vector.tensor_tensor(weights[:, c % 2, r, :].rearrange("p (g i) -> p g i", i=P),
                                                    p_feat[r][:, :].rearrange("p (g i) -> p g i", i=P),
                                                    w("causal").unsqueeze(1).broadcast_to([P, GROUP, P]), ALU.mult).then_inc(weight_ready, 1)
                        if c < TILES - 1:
                            dve.wait_ge(added_done, s * (TILES - 1) + c + 1)
                            own = w("favor_own").unsqueeze(1).broadcast_to([P, TILES, GROUP * VW])
                            add = p_add[:, 0:TILES * GROUP * VW].rearrange("p (g v) -> p g v", v=GROUP * VW)
                            if c == 0:
                                nc.vector.tensor_tensor(state[:, 1, :, :], add, own, ALU.mult).then_inc(state_ready, 1)
                            else:
                                step(nc.vector.tensor_tensor(added[:, :, :], add, own, ALU.mult))
                                dve.wait_ge(state_ready, s * (TILES - 1) + c)
                                nc.vector.tensor_tensor(state[:, (c + 1) % 2, :, :], state[:, c % 2, :, :], added[:, :, :], ALU.add).then_inc(state_ready, 1)
                        dve.wait_ge(sum_done, s * TILES + c + 1)
                        step(nc.vector.reciprocal(inv_den[:, :], sums[:, :, D]))
                        nc.vector.tensor_tensor(attn[:, c, :, :], sums[:, :, 0:D], inv_den[:, :].unsqueeze(2).broadcast_to([P, HEADS, D]),
                                                ALU.mult).then_inc(attn_ready, 1)
                    dve.wait_ge(out_done, s + 1)
                    step(nc.vector.tensor_tensor(res[:, :, :], tok, xin[:, :, :], ALU.add))
                    nc.vector.tensor_tensor(res[:, :, :], res[:, :, :], w("favor_out_b").unsqueeze(1).broadcast_to([P, TILES, P]),
                                            ALU.add).then_inc(res_ready, 1)
                    dve.wait_ge(res_ready, s + 1)
                    post.stats(dve, s, lambda t: res[:, t, :])
                    post.scale(dve, s, lambda t: resn[:, t, :], lambda t: res[:, t, :])
                    dve.wait_ge(post.rows_ready, s + 1)
                    step(nc.vector.tensor_tensor(resn[:, :, :], resn[:, :, :], w("favor_gamma").unsqueeze(1).broadcast_to([P, TILES, P]), ALU.mult))
                    step(nc.vector.tensor_tensor(resn[:, :, :], resn[:, :, :], w("favor_beta").unsqueeze(1).broadcast_to([P, TILES, P]), ALU.add))
                    step(nc.vector.tensor_tensor(xs, xs, resn[:, :, :], ALU.add))
                    step.end()

            @block.scalar
            def _(act):
                k.await_parameters(act, "favor")
                nc.scalar.preload_act_table_set("natural_log_exp_and_others")
                act.wait_ge(set_up, 3)
                with act.Fori(0, SEQS) as s:
                    outer.first_guess(act, s)
                    act.wait_ge(xinT_done, s + 1)
                    nc.scalar.copy(xinT[:, :], p_t[:, :]).then_inc(xinT_ready, 1)
                    act.wait_ge(q_done, s + 1)
                    nc.scalar.activation(q[:, :], p_q[:, :], ACT.Identity, scale=SCALE, bias=biases[:, 0:1]).then_inc(q_ready, 1)
                    act.wait_ge(k_done, s + 1)
                    nc.scalar.activation(kk[:, :], p_k[:, :], ACT.Identity, scale=SCALE, bias=biases[:, 1:2]).then_inc(k_ready, 1)
                    for n in range(3 * TILES):
                        out = (qf, kf, kf_tok)[n // TILES][:, n % TILES, :]
                        act.wait_ge(feat_done, s * 3 * TILES + n + 1)
                        nc.scalar.activation(out, p_feat[n % 4][:, :], ACT.Exp, bias=k.const(-0.5 * float(np.log(32.0)))).then_inc(feat_ready, 1)
                    act.wait_ge(attnT_done, s + 1)
                    nc.scalar.copy(attnT[:, :], p_t[:, :]).then_inc(attnT_ready, 1)
                    post.first_guess(act, s)

            @block.tensor
            def _(pe):
                k.await_parameters(pe, "favor")
                mm = nc.tensor.matmul
                with pe.Fori(0, SEQS) as s:
                    pe.wait_ge(outer.rows_ready, s + 1)
                    transpose_tiles(nc, pe, p_t, lambda t: xin[:, t, :], w("ident")).then_inc(xinT_done, 1)
                    pe.wait_ge(xinT_ready, s + 1)
                    mm(p_q[:, :], w("favor_q_w"), xinT[:, :], start=True, stop=True).then_inc(q_done, 1)
                    mm(p_k[:, :], w("favor_k_w"), xinT[:, :], start=True, stop=True).then_inc(k_done, 1)
                    for t in range(TILES):
                        last = mm(p_tok[:, t * P:(t + 1) * P], xinT[:, t * P:(t + 1) * P], w("favor_v_w"), start=True, stop=True)
                    last.then_inc(v_done, 1)
                    for n in range(3 * TILES):
                        if n == 0:
                            pe.wait_ge(q2_ready, s + 1)
                        if n == TILES:
                            pe.wait_ge(k2_ready, s + 1)
                        if n >= 4:
                            pe.wait_ge(feat_ready, s * 3 * TILES + n - 3)
                        c = slice(n % TILES * P, (n % TILES + 1) * P)
                        bank = p_feat[n % 4][:, :]
                        if n < 2 * TILES:
                            a, a2 = ((q, q2), (kk, k2))[n // TILES]
                            mm(bank, w("favor_proj")[:, c], a[:, :], start=True, stop=False)
                            last = mm(bank, w("favor_minus")[:, c], a2[:, :], start=False, stop=True)
                        else:
                            mm(bank, kk[:, c], w("favor_proj"), start=True, stop=False)
                            last = mm(bank, k2[:, c], w("favor_minus"), start=False, stop=True)
                        last.then_inc(feat_done, 1)
                    for c in range(TILES):
                        tokens = slice(c * P, (c + 1) * P)
                        for r in range(GROUP):
                            if c == 0:
                                pe.wait_ge(feat_ready, s * 3 * TILES + 2 * TILES + r + 1)
                            else:
                                pe.wait_ge(weight_ready, (s * TILES + c - 1) * GROUP + r + 1)
                            rows = slice(r * M, (r + 1) * M)
                            for g in range(TILES):
                                last = mm(p_feat[r][:, g * P:(g + 1) * P], kf[rows, g, tokens], qf[rows, g, tokens], start=True, stop=True)
                            last.then_inc(score_done, 1)
                        if c == 0:
                            pe.wait_ge(v_ready, s + 1)
                        if c < TILES - 1:
                            if c >= 1:
                                pe.wait_ge(state_ready, s * (TILES - 1) + c)
                            for g in range(TILES):
                                last = mm(p_add[:, g * GROUP * VW:(g + 1) * GROUP * VW], kf_tok[:, c, g * P:(g + 1) * P],
                                          vals[:, c, g * GROUP:(g + 1) * GROUP, :], start=True, stop=True)
                            last.then_inc(added_done, 1)
                        if c > 0:
                            pe.wait_ge(state_ready, s * (TILES - 1) + c)
                            pe.wait_ge(attn_ready, s * TILES + c)
                            for g in range(TILES):
                                mm(p_sum[:, g * GROUP * VW:(g + 1) * GROUP * VW], qf[:, g, tokens], state[:, c % 2, g, :],
                                   start=(g == 0), stop=False, skip_group_check=True)
                        for r in range(GROUP):
                            pe.wait_ge(weight_ready, (s * TILES + c) * GROUP + r + 1)
                            for g in range(TILES):
                                h = g * GROUP + r
                                last = mm(p_sum[:, h * VW:(h + 1) * VW], weights[:, c % 2, r, g * P:(g + 1) * P], vals[:, c, h, :],
                                          start=(c == 0 and r == 0 and g == 0), stop=True, skip_group_check=True)
                        last.then_inc(sum_done, 1)
                    pe.wait_ge(attn_ready, (s + 1) * TILES)
                    transpose_tiles(nc, pe, p_t, lambda t: attn[:, t, :, :], w("ident")).then_inc(attnT_done, 1)
                    pe.wait_ge(attnT_ready, s + 1)
                    for t in range(TILES):
                        last = mm(p_tok[:, t * P:(t + 1) * P], attnT[:, t * P:(t + 1) * P], w("favor_out_w"), start=True, stop=True)
                    last.then_inc(out_done, 1)


def taylor_stage(nc, k, n_stage):
    D = 64
    C = 32.0 ** -0.5
    PAIRS = HEADS // 2
    BY_KEYS = [(0, 0), (1, 0), (2, 0), (1, 384)]
    USED, FLAT = (512, 512, 256), (0, 512, 1024)
    with ExitStack() as ctx:
        sb = lambda name, shape: ctx.enter_context(nc.sbuf_tensor("taylor_" + name, shape, F32))
        sem = lambda name: k.semaphore(ctx, "taylor_" + name)
        w = k.w
        outer = Norm(nc, ctx, k, "taylor_outer", 1e-5)
        xin, xinT = sb("xin", [P, TILES, P]), sb("xinT", [P, 512])
        q_own, ks = sb("q_own", [P, HEADS, 512]), sb("k", [P, 2, 512])
        vals = sb("vals", [P, TILES, HEADS, 2 * D])
        weights = sb("weights", [P, 2, 1280])
        den, y = sb("den", [P, 2, 512]), sb("y", [P, 2, 512])
        dve_step, set_up = sem("dve_step"), sem("set_up")
        xinT_done, xinT_ready, qk_done, q_low_ready, q_high_ready, k_ready, v_done, v_low_ready, v_high_ready = (
            sem(n) for n in ("xinT_done", "xinT_ready", "qk_done", "q_low_ready", "q_high_ready", "k_ready", "v_done", "v_low_ready", "v_high_ready"))
        score_done, square_ready, weight_ready, sum_done, den_ready, y_ready, out_done = (
            sem(n) for n in ("score_done", "square_ready", "weight_ready", "sum_done", "den_ready", "y_ready", "out_done"))
        p_score, p_sum, p_out = k.banks[0:3], k.banks[3:7], k.banks[7]
        p_v, p_t, p_qk = k.banks[0:2], k.banks[2], k.banks[3:7]
        low, high = slice(0, D), slice(D, 2 * D)

        def values_of(tile, half):
            pairs = vals[:, tile, half * 8:half * 8 + 8, :].rearrange("p (r e) (c d) -> p r (e c) d", e=2, c=2)
            return pairs[:, :, 0:4:3, :]

        with nc.Block() as block:
            @block.vector
            def _(dve):
                k.await_parameters(dve, "taylor")
                nc.vector.memset(vals[:, :, :, :], 1.0).then_inc(set_up, 1)
                dve.wait_ge(set_up, 1)
                with dve.Fori(0, SEQS) as s:
                    outer.stats(dve, s, lambda t: k.x[:, bass.ds(s * TILES + t, 1), :])
                    outer.scale(dve, s, lambda t: xin[:, t, :], lambda t: k.x[:, bass.ds(s * TILES + t, 1), :])
                    step = Steps(dve, dve_step, s, PAIRS + 1)
                    dve.wait_ge(qk_done, s * 4 + 1)
                    for h in range(8):
                        nc.vector.tensor_scalar(q_own[:, h, :], p_qk[0][:, :], w("taylor_own")[:, h:h + 1], None, ALU.mult).then_inc(q_low_ready, 1)
                    for n in range(1, 2 * TILES, 2):
                        dve.wait_ge(v_done, s * 2 * TILES + n + 1)
                        nc.vector.tensor_copy(values_of(n // 2, 1), p_v[1][:, :].rearrange("p (r e d) -> p r e d", e=2, d=D)).then_inc(v_high_ready, 1)

                    def weigh(h):
                        for b in range(3):
                            dve.wait_ge(square_ready, (s * HEADS + h) * 3 + b + 1)
                            part = weights[:, h % 2, FLAT[b]:FLAT[b] + USED[b]]
                            nc.vector.scalar_tensor_tensor(part, part, 0.5, w("taylor_causal")[:, FLAT[b]:FLAT[b] + USED[b]], ALU.add,
                                                           ALU.mult).then_inc(weight_ready, 1)

                    def normalise(n):
                        if n >= 2:
                            dve.wait_ge(out_done, s * PAIRS + n - 1)
                        dve.wait_ge(den_ready, (s * PAIRS + n + 1) * 2)
                        step(nc.vector.reciprocal(den[:, n % 2, :], den[:, n % 2, :]))
                        for e, rows in enumerate((low, high)):
                            nc.vector.tensor_tensor(y[rows, n % 2, :], p_sum[(2 * n + e) % 4][rows, :], den[rows, n % 2, :],
                                                    ALU.mult).then_inc(y_ready, 1)

                    weigh(0)
                    for h in range(1, HEADS):
                        weigh(h)
                        if h % 2 == 0:
                            normalise(h // 2 - 1)
                    normalise(PAIRS - 1)
                    dve.wait_ge(out_done, (s + 1) * PAIRS)
                    xs = k.x[:, bass.ds(s * TILES, TILES), :]
                    step(nc.vector.tensor_tensor(xs, xs, p_out[:, :].rearrange("p (t d) -> p t d", d=P), ALU.add))
                    step.end()

            @block.scalar
            def _(act):
                k.await_parameters(act, "taylor")
                nc.scalar.preload_act_table_set("natural_log_exp_and_others")
                act.wait_ge(set_up, 1)
                with act.Fori(0, SEQS) as s:
                    outer.first_guess(act, s)
                    act.wait_ge(xinT_done, s + 1)
                    nc.scalar.copy(xinT[:, :], p_t[:, :]).then_inc(xinT_ready, 1)
                    act.wait_ge(qk_done, s * 4 + 2)
                    for h in range(8, HEADS):
                        nc.scalar.activation(q_own[:, h, :], p_qk[1][:, :], ACT.Identity, scale=w("taylor_own")[:, h - 8:h - 7],
                                             bias=k.const(0.0)).then_inc(q_high_ready, 1)
                    for n in range(2):
                        act.wait_ge(qk_done, s * 4 + 2 + n + 1)
                        nc.scalar.copy(ks[:, n, :], p_qk[2 + n][:, :]).then_inc(k_ready, 1)
                    for n in range(0, 2 * TILES, 2):
                        act.wait_ge(v_done, s * 2 * TILES + n + 1)
                        nc.scalar.copy(values_of(n // 2, 0), p_v[0][:, :].rearrange("p (r e d) -> p r e d", e=2, d=D)).then_inc(v_low_ready, 1)

                    def denominators(h):
                        n = h // 2
                        if n >= 2:
                            act.wait_ge(y_ready, (s * PAIRS + n - 1) * 2)
                        act.wait_ge(sum_done, s * HEADS + h + 1)
                        to, of = ((low, high), (high, low))[h % 2]
                        nc.scalar.activation(den[to, n % 2, :], p_sum[h % 4][of, :], ACT.Identity, bias=k.const(1e-12)[of, :]).then_inc(den_ready, 1)

                    for h in range(HEADS):
                        if h >= 2:
                            act.wait_ge(sum_done, s * HEADS + h - 1)
                        for b in range(3):
                            act.wait_ge(score_done, (s * HEADS + h) * 3 + b + 1)
                            nc.scalar.activation(weights[:, h % 2, FLAT[b]:FLAT[b] + USED[b]], p_score[b][:, 0:USED[b]], ACT.Square,
                                                 bias=k.const(4.0 / 32.0 ** 0.5), scale=C).then_inc(square_ready, 1)
                        if h >= 2:
                            denominators(h - 2)
                    denominators(HEADS - 2)
                    denominators(HEADS - 1)

            @block.tensor
            def _(pe):
                k.await_parameters(pe, "taylor")
                mm = nc.tensor.matmul
                with pe.Fori(0, SEQS) as s:
                    pe.wait_ge(outer.rows_ready, s + 1)
                    transpose_tiles(nc, pe, p_t, lambda t: xin[:, t, :], w("ident")).then_inc(xinT_done, 1)
                    pe.wait_ge(xinT_ready, s + 1)
                    for n in range(4):
                        weight = w(("taylor_wq", "taylor_wk")[n // 2])[:, n % 2 * P:(n % 2 + 1) * P]
                        mm(p_qk[n][:, :], weight, xinT[:, :], start=True, stop=True).then_inc(qk_done, 1)
                    for n in range(2 * TILES):
                        if n >= 2:
                            pe.wait_ge((v_low_ready, v_high_ready)[n % 2], s * TILES + n // 2)
                        mm(p_v[n % 2][:, :], xinT[:, n // 2 * P:(n // 2 + 1) * P],
                           w("taylor_wv")[:, n % 2 * 512:(n % 2 + 1) * 512], start=True, stop=True).then_inc(v_done, 1)

                    def scores(h):
                        if h == 0:
                            pe.wait_ge(k_ready, (s + 1) * 2)
                            pe.wait_ge(q_low_ready, (s + 1) * 8)
                            pe.wait_ge(q_high_ready, (s + 1) * 8)
                            pe.wait_ge(v_low_ready, (s + 1) * TILES)
                            pe.wait_ge(v_high_ready, (s + 1) * TILES)
                        for b in range(3):
                            if h > 0:
                                pe.wait_ge(square_ready, (s * HEADS + h - 1) * 3 + b + 1)
                            for j in range(TILES):
                                if BY_KEYS[j][0] == b:
                                    c = BY_KEYS[j][1]
                                    last = mm(p_score[b][:, c:c + 512 - j * P], ks[:, h // 8, j * P:(j + 1) * P], q_own[:, h, j * P:512],
                                              start=True, stop=True)
                            last.then_inc(score_done, 1)

                    def sums(h):
                        if h >= 4:
                            pe.wait_ge(y_ready, (s * PAIRS + h // 2 - 1) * 2)
                        for j in range(TILES):
                            b, c = BY_KEYS[j]
                            pe.wait_ge(weight_ready, (s * HEADS + h) * 3 + b + 1)
                            last = mm(p_sum[h % 4][:, j * P:512], vals[:, j, h, :], weights[:, h % 2, FLAT[b] + c:FLAT[b] + c + 512 - j * P],
                                      start=(j == 0), stop=(j == 0), skip_group_check=(j > 0))
                        last.then_inc(sum_done, 1)

                    def output(n):
                        pe.wait_ge(y_ready, (s * PAIRS + n + 1) * 2)
                        for t in range(TILES):
                            first = n == 0 and t == 0
                            last = mm(p_out[:, t * P:(t + 1) * P], y[:, n % 2, t * P:(t + 1) * P], w("taylor_wo")[:, n * P:(n + 1) * P],
                                      start=first, stop=first, skip_group_check=not first)
                        last.then_inc(out_done, 1)

                    scores(0)
                    for h in range(HEADS):
                        if h + 1 < HEADS:
                            scores(h + 1)
                        sums(h)
                        if h >= 3 and h % 2 == 1:
                            output(h // 2 - 1)
                    output(PAIRS - 1)


def moe_stage(nc, k, n_stage):
    D, VW = 8, 16
    PER = P // VW
    PAIRS = HEADS // 2
    GROUP = 4
    SCALE = D ** -0.5
    EXPERTS, HIDDEN = 8, 384
    HT = HIDDEN // P
    BY_KEYS = [(0, 0), (1, 0), (2, 0), (1, 384)]
    BY_QUERIES = [(1, 384), (2, 0), (1, 0), (0, 0)]
    USED = (512, 512, 256)
    FLAT = (0, 512, 1024)
    with ExitStack() as ctx:
        sb = lambda name, shape, dt=F32: ctx.enter_context(nc.sbuf_tensor(f"moe{n_stage}_{name}", shape, dt))
        sem = lambda name: k.semaphore(ctx, f"moe{n_stage}_{name}")
        w = k.w
        outer = Norm(nc, ctx, k, f"moe{n_stage}_outer", 1e-5)
        first = Norm(nc, ctx, k, f"moe{n_stage}_first", 1e-6, rms=True)
        second = Norm(nc, ctx, k, f"moe{n_stage}_second", 1e-6, rms=True)
        future, ident = sb("future", [P, P], BF16), sb("ident", [P, P], BF16)
        xin, xr, xrT = sb("xin", [P, TILES, P]), sb("xr", [P, TILES, P]), sb("xrT", [P, 512])
        hr, hrT = xr, xrT
        attn, qk = sb("attn", [P, 2, 512]), sb("qk", [P, 2, 512])
        turned, inv_den = attn[:, 0, :], qk
        q_parts, k_parts = sb("q_parts", [P, 3, 512], BF16), sb("k_parts", [P, 3, 512], BF16)
        q_stack, k_stack = sb("q_stack", [P, HEADS, 512], BF16), sb("k_stack", [P, PAIRS, 512], BF16)
        stacker = sb("stacker", [P, PAIRS, 6, P], BF16)
        pick = sb("pick", [P, GROUP * P], BF16)
        vals = sb("vals", [P, TILES * HEADS + 1, P])
        biggest, big_parts = sb("biggest", [P, TILES, HEADS]), sb("big_parts", [P, TILES, HEADS // GROUP, 2 * GROUP], BF16)
        turned_max = sb("turned_max", [P, 2, 512], BF16)
        weights = sb("weights", [P, 2, 1280])
        gate = weights[:, :, 0:512]
        acc = xin
        logits, top = sb("logits", [P, TILES, EXPERTS]), sb("top", [P, TILES, 8])
        index, index_f = sb("index", [P, TILES, 8], mybir.dt.uint32), sb("index_f", [P, TILES, 8])
        e_top, e_sum, combine, second_pick = sb("e_top", [P, TILES, 8]), sb("e_sum", [P, TILES]), sb("combine", [P, TILES, 8]), sb("second_pick", [P, TILES, 8])
        prod = sb("prod", [P, 2, HT, 512])
        dve_step, set_up = sem("dve_step"), sem("set_up")
        xrT_done, xrT_ready, qk_done, part_ready, v_done, v_ready = (
            sem(n) for n in ("xrT_done", "xrT_ready", "qk_done", "part_ready", "v_done", "v_ready"))
        stack_done, q_stack_ready, k_stack_ready, split_ready = (sem(n) for n in ("stack_done", "q_stack_ready", "k_stack_ready", "split_ready"))
        row_done, row_read, max_done, max_ready, score_done, weight_ready, sum_done, sum_ready, den_done, attn_ready = (
            sem(n) for n in ("row_done", "row_read", "max_done", "max_ready", "score_done", "weight_ready", "sum_done", "sum_ready", "den_done", "attn_ready"))
        o_done, h_ready, hrT_done, hrT_ready, logits_done, top_ready, e_ready, combine_ready = (
            sem(n) for n in ("o_done", "h_ready", "hrT_done", "hrT_ready", "logits_done", "top_ready", "e_ready", "combine_ready"))
        gate_done, gate_ready, up_done, prod_ready, down_done, acc_ready = (
            sem(n) for n in ("gate_done", "gate_ready", "up_done", "prod_ready", "down_done", "acc_ready"))
        p_row, p_score, p_sum, p_t = k.banks[0:2], k.banks[2:5], k.banks[5:7], k.banks[7]
        p_stack, p_den, p_logits = k.banks[0:4], p_row, k.banks[6]
        p_q, p_q_rot, p_k, p_k_rot, p_v = k.banks[0:5]
        p_gate, p_up, p_down = k.banks[0:2], k.banks[2:4], k.banks[4:6]

        with nc.Block() as block:
            @block.vector
            def _(dve):
                k.await_parameters(dve, "moe")
                nc.vector.memset(vals[:, :, :], 0.0).then_inc(set_up, 1)
                nc.vector.memset(turned_max[:, :, :], 0.0).then_inc(set_up, 1)
                nc.vector.tensor_copy(pick[:, :], w("attn_pick")).then_inc(set_up, 1)
                for n in range(PAIRS):
                    nc.vector.tensor_scalar(stacker[:, n, :, :], w("attn_stack").rearrange("p (j m) -> p j m", m=P),
                                            w("attn_of_pair")[:, n:n + 1], None, ALU.mult).then_inc(set_up, 1)
                dve.wait_ge(set_up, 1)
                nc.vector.memset(vals[:, 0:TILES * HEADS, P - VW + D:P - VW + D + 1], 1.0).then_inc(set_up, 1)
                nc.vector.tensor_copy(future[:, :], w("future")).then_inc(set_up, 1)
                nc.vector.tensor_copy(ident[:, :], w("ident")).then_inc(set_up, 1)
                with dve.Fori(0, SEQS) as s:
                    outer.stats(dve, s, lambda t: k.x[:, bass.ds(s * TILES + t, 1), :])
                    outer.scale(dve, s, lambda t: xin[:, t, :], lambda t: k.x[:, bass.ds(s * TILES + t, 1), :])
                    dve.wait_ge(outer.rows_ready, s + 1)
                    first.stats(dve, s, lambda t: xin[:, t, :])
                    first.scale(dve, s, lambda t: xr[:, t, :], lambda t: xin[:, t, :])
                    step = Steps(dve, dve_step, s, 2 * 6 + HEADS // GROUP + 2 + 13)
                    for n, (plain, rot, out, parts) in enumerate(((p_q, p_q_rot, qk[:, 0, :], q_parts), (p_k, p_k_rot, qk[:, 1, :], k_parts))):
                        dve.wait_ge(qk_done, s * 4 + 2 * n + 1)
                        step(nc.vector.tensor_tensor(out, plain[:, :], w("attn_cos"), ALU.mult))
                        dve.wait_ge(qk_done, s * 4 + 2 * n + 2)
                        step(nc.vector.tensor_tensor(turned, rot[:, :], w("attn_sin"), ALU.mult))
                        step(nc.vector.tensor_tensor(out, out, turned, ALU.add))
                        step(nc.vector.tensor_copy(parts[:, 0, :], out))
                        step(nc.vector.tensor_tensor(out, out, parts[:, 0, :], ALU.subtract))
                        step(nc.vector.tensor_copy(parts[:, 1, :], out))
                        nc.vector.tensor_tensor(parts[:, 2, :], out, parts[:, 1, :], ALU.subtract).then_inc(part_ready, 1)
                    dve.wait_ge(v_done, s + 1)
                    nc.vector.tensor_copy(vals[:, 0:TILES * HEADS, P - VW:P - VW + D],
                                          p_v[:, :].rearrange("p (n d) -> p n d", d=D)).then_inc(v_ready, 1)
                    for n in range(PAIRS):
                        dve.wait_ge(stack_done, (s * PAIRS + n) * 2 + 2)
                        for e in range(2):
                            nc.vector.tensor_scalar(q_stack[:, 2 * n + e, :], p_stack[(2 * n + 1) % 4][:, :], w("attn_of_head")[:, e:e + 1],
                                                    None, ALU.mult).then_inc(q_stack_ready, 1)

                    def row_max(h):
                        for part in range(3):
                            n = h * 3 + part
                            dve.wait_ge(row_done, s * HEADS * 3 + n + 1)
                            for i in range(TILES):
                                if BY_QUERIES[i][0] == part:
                                    c = BY_QUERIES[i][1]
                                    last = nc.vector.reduce_max(biggest[:, i, h:h + 1], p_row[n % 2][:, c:c + (i + 1) * P], AX)
                            last.then_inc(row_read, 1)
                        if h % GROUP == GROUP - 1:
                            heads = slice(h - GROUP + 1, h + 1)
                            high, low = (big_parts[:, :, h // GROUP, n * GROUP:(n + 1) * GROUP] for n in range(2))
                            dve.wait_ge(row_read, (s * HEADS + h + 1) * 3)
                            step(nc.vector.tensor_copy(high, biggest[:, :, heads]))
                            nc.vector.tensor_tensor(low, biggest[:, :, heads], high, ALU.subtract).then_inc(split_ready, 1)

                    for h in range(HEADS):
                        row_max(h)
                    for n in range(2):
                        dve.wait_ge(den_done, s * 2 + n + 1)
                        step(nc.vector.reciprocal(inv_den[:, n, :], p_den[n][:, :]))
                        nc.vector.tensor_tensor(attn[:, n, :], attn[:, n, :], inv_den[:, n, :], ALU.mult).then_inc(attn_ready, 1)
                    dve.wait_ge(o_done, s + 1)
                    nc.vector.tensor_tensor(acc[:, :, :], xin[:, :, :], p_t[:, :].rearrange("p (t d) -> p t d", d=P), ALU.add).then_inc(h_ready, 1)
                    dve.wait_ge(h_ready, s + 1)
                    second.stats(dve, s, lambda t: acc[:, t, :])
                    second.scale(dve, s, lambda t: hr[:, t, :], lambda t: acc[:, t, :])
                    dve.wait_ge(logits_done, s + 1)
                    step(nc.vector.tensor_copy(logits[:, :, :], p_logits[:, 0:TILES * EXPERTS].rearrange("p (t e) -> p t e", e=EXPERTS)))
                    carry_wait(nc, k.spare)
                    for t in range(TILES):
                        last = nc.vector.max(top[:, t, :], logits[:, t, :])
                    step(last)
                    carry_wait(nc, k.spare)
                    for t in range(TILES):
                        last = nc.vector.max_index(index[:, t, :], top[:, t, :], logits[:, t, :])
                    step(last)
                    step(nc.vector.tensor_copy(index_f[:, :, :], index[:, :, :]))
                    largest = top[:, :, 0:1].broadcast_to([P, TILES, 8])
                    nc.vector.tensor_tensor(e_top[:, :, :], top[:, :, :], largest, ALU.subtract).then_inc(top_ready, 1)
                    dve.wait_ge(e_ready, s + 1)
                    step(nc.vector.reduce_sum(e_sum[:, :], e_top[:, :, :], AX))
                    step(nc.vector.reciprocal(e_sum[:, :], e_sum[:, :]))
                    step(nc.vector.tensor_tensor(e_top[:, :, 0:2], e_top[:, :, 0:2], e_sum[:, :].unsqueeze(2).broadcast_to([P, TILES, 2]), ALU.mult))
                    step(nc.vector.tensor_tensor(e_sum[:, :], e_top[:, :, 0], e_top[:, :, 1], ALU.add))
                    step(nc.vector.reciprocal(e_sum[:, :], e_sum[:, :]))
                    step(nc.vector.tensor_tensor(e_top[:, :, 0:2], e_top[:, :, 0:2], e_sum[:, :].unsqueeze(2).broadcast_to([P, TILES, 2]), ALU.mult))
                    for n, out in enumerate((combine, second_pick)):
                        at = index_f[:, :, n:n + 1].broadcast_to([P, TILES, 8])
                        step(nc.vector.tensor_tensor(out[:, :, :], w("moe_index").unsqueeze(1).broadcast_to([P, TILES, 8]), at, ALU.is_equal))
                        last = nc.vector.tensor_tensor(out[:, :, :], out[:, :, :], e_top[:, :, n:n + 1].broadcast_to([P, TILES, 8]), ALU.mult)
                        last.then_inc(combine_ready, 1)
                    dve.wait_ge(combine_ready, s * 3 + 2)
                    nc.vector.tensor_tensor(combine[:, :, :], combine[:, :, :], second_pick[:, :, :], ALU.add).then_inc(combine_ready, 1)
                    dve.wait_ge(combine_ready, s * 3 + 3)

                    def product(e, m):
                        n = e * HT + m
                        if m == 0 and e >= 2:
                            dve.wait_ge(down_done, s * EXPERTS + e - 1)
                        dve.wait_ge(gate_ready, s * EXPERTS * HT + n + 1)
                        dve.wait_ge(up_done, s * EXPERTS * HT + n + 1)
                        nc.vector.tensor_tensor(prod[:, e % 2, m, :], p_up[n % 2][:, :], gate[:, n % 2, :], ALU.mult).then_inc(prod_ready, 1)

                    def add_expert(e):
                        dve.wait_ge(down_done, s * EXPERTS + e + 1)
                        if e > 0:
                            dve.wait_ge(acc_ready, s * EXPERTS + e)
                        for t in range(TILES):
                            last = nc.vector.scalar_tensor_tensor(acc[:, t, :], p_down[e % 2][:, t * P:(t + 1) * P], combine[:, t, e:e + 1],
                                                                  acc[:, t, :], ALU.mult, ALU.add)
                        last.then_inc(acc_ready, 1)

                    for e in range(EXPERTS):
                        for m in range(HT):
                            product(e, m)
                        if e > 0:
                            add_expert(e - 1)
                    add_expert(EXPERTS - 1)
                    dve.wait_ge(acc_ready, (s + 1) * EXPERTS)
                    xs = k.x[:, bass.ds(s * TILES, TILES), :]
                    step(nc.vector.tensor_tensor(xs, xs, acc[:, :, :], ALU.add))
                    step.end()

            @block.scalar
            def _(act):
                k.await_parameters(act, "moe")
                nc.scalar.preload_act_table_set("natural_log_exp_and_others")
                with act.Fori(0, SEQS) as s:
                    nc.scalar.preload_act_table_set("natural_log_exp_and_others")
                    outer.first_guess(act, s)
                    first.first_guess(act, s)
                    act.wait_ge(xrT_done, s + 1)
                    nc.scalar.activation(xrT[:, :], p_t[:, :], ACT.Identity, scale=w("attn_g1"), bias=k.const(0.0)).then_inc(xrT_ready, 1)

                    for n in range(PAIRS):
                        act.wait_ge(stack_done, (s * PAIRS + n) * 2 + 1)
                        nc.scalar.copy(k_stack[:, n, :], p_stack[2 * n % 4][:, :]).then_inc(k_stack_ready, 1)

                    def turn(g):
                        act.wait_ge(max_done, s * GROUP + g + 1)
                        nc.scalar.copy(turned_max[0:2 * GROUP, g % 2, :], p_t[0:2 * GROUP, :]).then_inc(max_ready, 1)

                    turn(0)
                    for h in range(HEADS):
                        if h >= 2:
                            act.wait_ge(sum_done, s * HEADS + h - 1)
                        for bank in range(3):
                            act.wait_ge(score_done, (s * HEADS + h) * 3 + bank + 1)
                            nc.scalar.activation(weights[:, h % 2, FLAT[bank]:FLAT[bank] + USED[bank]], p_score[bank][:, 0:USED[bank]],
                                                 ACT.Exp, scale=SCALE).then_inc(weight_ready, 1)
                        if h % GROUP == GROUP - 1 and h + 1 < HEADS:
                            turn(h // GROUP + 1)
                        if h == PER + 1 or h == HEADS - 1:
                            n = 0 if h == PER + 1 else 1
                            act.wait_ge(sum_done, s * HEADS + (n + 1) * PER)
                            nc.scalar.copy(attn[:, n, :], p_sum[n][:, :]).then_inc(sum_ready, 1)
                    second.first_guess(act, s)
                    act.wait_ge(hrT_done, s + 1)
                    nc.scalar.activation(hrT[:, :], p_t[:, :], ACT.Identity, scale=w("attn_g2"), bias=k.const(0.0)).then_inc(hrT_ready, 1)
                    act.wait_ge(top_ready, s + 1)
                    nc.scalar.activation(e_top[:, :, :], e_top[:, :, :], ACT.Exp).then_inc(e_ready, 1)
                    for n in range(EXPERTS * HT):
                        act.wait_ge(gate_done, s * EXPERTS * HT + n + 1)
                        if n >= 2:
                            act.wait_ge(prod_ready, s * EXPERTS * HT + n - 1)
                        nc.scalar.activation(gate[:, n % 2, :], p_gate[n % 2][:, :], ACT.Silu).then_inc(gate_ready, 1)

            @block.tensor
            def _(pe):
                k.await_parameters(pe, "moe")
                mm = nc.tensor.matmul
                pe.wait_ge(set_up, 6 + PAIRS)
                with pe.Fori(0, SEQS) as s:
                    pe.wait_ge(first.rows_ready, s + 1)
                    transpose_tiles(nc, pe, p_t, lambda t: xr[:, t, :], w("ident")).then_inc(xrT_done, 1)
                    pe.wait_ge(xrT_ready, s + 1)
                    for bank, name in ((p_q, "attn_wq"), (p_q_rot, "attn_wq_rot"), (p_k, "attn_wk"), (p_k_rot, "attn_wk_rot")):
                        mm(bank[:, :], w(name), xrT[:, :], start=True, stop=True).then_inc(qk_done, 1)
                    for t in range(TILES):
                        last = mm(p_v[:, t * P:(t + 1) * P], xrT[:, t * P:(t + 1) * P], w("attn_wv"), start=True, stop=True)
                    last.then_inc(v_done, 1)

                    for n in range(2 * PAIRS):
                        parts = (k_parts, q_parts)[n % 2]
                        if n == 0:
                            pe.wait_ge(part_ready, s * 2 + 2)
                            pe.wait_ge(v_ready, s + 1)
                        if n >= 4:
                            if n % 2 == 0:
                                pe.wait_ge(k_stack_ready, s * PAIRS + n // 2 - 1)
                            else:
                                pe.wait_ge(q_stack_ready, s * HEADS + (n // 2 - 1) * 2)
                        for j in range(3):
                            last = mm(p_stack[n % 4][:, :], stacker[:, n // 2, n % 2 * 3 + j, :], parts[:, j, :], start=(j == 0), stop=(j == 2))
                        last.then_inc(stack_done, 1)

                    def query_rows(h):
                        if h == 0:
                            pe.wait_ge(q_stack_ready, (s + 1) * HEADS)
                            pe.wait_ge(k_stack_ready, (s + 1) * PAIRS)
                        for part in range(3):
                            n = h * 3 + part
                            if n >= 2:
                                pe.wait_ge(row_read, s * HEADS * 3 + n - 1)
                            for i in range(TILES):
                                if BY_QUERIES[i][0] == part:
                                    c = BY_QUERIES[i][1]
                                    mm(p_row[n % 2][:, c + i * P:c + (i + 1) * P], future[:, :], ident[:, :],
                                       start=True, stop=True)
                                    last = mm(p_row[n % 2][:, c:c + (i + 1) * P], q_stack[:, h, i * P:(i + 1) * P],
                                              k_stack[:, h // 2, 0:(i + 1) * P], start=False, stop=True, skip_group_check=True)
                            last.then_inc(row_done, 1)

                    def turn_max(g):
                        pe.wait_ge(split_ready, s * GROUP + g + 1)
                        if g > 0:
                            pe.wait_ge(max_ready, s * GROUP + g)
                        for t in range(TILES):
                            last = mm(p_t[0:2 * GROUP, t * P:(t + 1) * P], big_parts[:, t, g, :], ident[:, :],
                                      start=True, stop=True)
                        last.then_inc(max_done, 1)

                    def key_rows(h):
                        g, r = h // GROUP, h % GROUP
                        if r == 0:
                            pe.wait_ge(max_ready, s * GROUP + g + 1)
                        for bank in range(3):
                            if h > 0:
                                pe.wait_ge(weight_ready, (s * HEADS + h - 1) * 3 + bank + 1)
                            for i in range(TILES):
                                if BY_KEYS[i][0] == bank:
                                    c, n = BY_KEYS[i][1], 512 - i * P
                                    out = p_score[bank][:, c:c + n]
                                    mm(p_score[bank][:, c:c + P], ident[:, :], future[:, :], start=True, stop=True)
                                    mm(out, pick[:, r * P:(r + 1) * P], turned_max[:, g % 2, i * P:512], start=False, stop=False,
                                       skip_group_check=True)
                                    last = mm(out, k_stack[:, h // 2, i * P:(i + 1) * P], q_stack[:, h, i * P:512], start=False, stop=True,
                                              skip_group_check=True)
                            last.then_inc(score_done, 1)

                    def sums(h):
                        flat = vals[:, :, :].rearrange("p n v -> p (n v)")
                        for j in range(TILES):
                            bank, c = BY_KEYS[j]
                            pe.wait_ge(weight_ready, (s * HEADS + h) * 3 + (bank + 1 if j != 3 else 2))
                            at = (j * HEADS + h) * P + P - VW - h % PER * VW
                            last = mm(p_sum[h // PER][:, j * P:512], flat[:, at:at + P], weights[:, h % 2, FLAT[bank] + c:FLAT[bank] + c + 512 - j * P],
                                      start=(h % PER == 0 and j == 0), stop=(h % PER == 0 and j == 0),
                                      skip_group_check=not (h % PER == 0 and j == 0))
                        last.then_inc(sum_done, 1)

                    for h in range(GROUP):
                        query_rows(h)
                    turn_max(0)
                    for h in range(HEADS):
                        if h + GROUP < HEADS:
                            query_rows(h + GROUP)
                        key_rows(h)
                        if h > 0:
                            sums(h - 1)
                        if h % GROUP == GROUP - 1 and h + 1 < HEADS:
                            turn_max(h // GROUP + 1)
                    sums(HEADS - 1)
                    for n in range(2):
                        pe.wait_ge(sum_ready, s * 2 + n + 1)
                        mm(p_den[n][:, :], w("attn_den"), attn[:, n, :], start=True, stop=True).then_inc(den_done, 1)
                    pe.wait_ge(attn_ready, (s + 1) * 2)
                    for t in range(TILES):
                        for n in range(2):
                            last = mm(p_t[:, t * P:(t + 1) * P], attn[:, n, t * P:(t + 1) * P], w("attn_wo_rows")[:, n * P:(n + 1) * P],
                                      start=(n == 0), stop=(n == 1))
                    last.then_inc(o_done, 1)
                    pe.wait_ge(second.rows_ready, s + 1)
                    transpose_tiles(nc, pe, p_t, lambda t: hr[:, t, :], w("ident")).then_inc(hrT_done, 1)
                    pe.wait_ge(hrT_ready, s + 1)
                    for t in range(TILES):
                        last = mm(p_logits[:, t * EXPERTS:(t + 1) * EXPERTS], hrT[:, t * P:(t + 1) * P], w("moe_router"), start=True, stop=True)
                    last.then_inc(logits_done, 1)

                    def up(e):
                        for m in range(HT):
                            n = e * HT + m
                            c = slice(n * P, (n + 1) * P)
                            if n >= 2:
                                pe.wait_ge(gate_ready, s * EXPERTS * HT + n - 1)
                            mm(p_gate[n % 2][:, :], w("moe_wg")[:, c], hrT[:, :], start=True, stop=True).then_inc(gate_done, 1)
                            if n >= 2:
                                pe.wait_ge(prod_ready, s * EXPERTS * HT + n - 1)
                            mm(p_up[n % 2][:, :], w("moe_wu")[:, c], hrT[:, :], start=True, stop=True).then_inc(up_done, 1)

                    def down(e):
                        pe.wait_ge(prod_ready, s * EXPERTS * HT + (e + 1) * HT)
                        if e >= 2:
                            pe.wait_ge(acc_ready, s * EXPERTS + e - 1)
                        for t in range(TILES):
                            for m in range(HT):
                                n = e * HT + m
                                last = mm(p_down[e % 2][:, t * P:(t + 1) * P], prod[:, e % 2, m, t * P:(t + 1) * P],
                                          w("moe_wd")[:, n * P:(n + 1) * P], start=(m == 0), stop=(m == HT - 1))
                        last.then_inc(down_done, 1)

                    up(0)
                    for e in range(EXPERTS):
                        if e + 1 < EXPERTS:
                            up(e + 1)
                        down(e)


def ssd_stage(nc, k, n_stage):
    H, HD, INNER = 4, 64, 256
    LOG1P = log1p_series()
    with ExitStack() as ctx:
        sb = lambda name, shape: ctx.enter_context(nc.sbuf_tensor("ssd_" + name, shape, F32))
        sem = lambda name: k.semaphore(ctx, "ssd_" + name)
        w = k.w
        outer = Norm(nc, ctx, k, "ssd_outer", 1e-5)
        first = Norm(nc, ctx, k, "ssd_first", 1e-5, rms=True)
        gnorm = Norm(nc, ctx, k, "ssd_gnorm", 1e-5, rms=True)
        xin, xn, xnT = sb("xin", [P, TILES, P]), sb("xn", [P, TILES, P]), sb("xnT", [P, 512])
        padded, conv, chan = sb("padded", [P, 4, 515]), sb("conv", [P, 4, 512]), sb("chan", [P, 4, 512])
        zs = sb("zs", [P, TILES, INNER])
        a_rate = sb("a_rate", [P, H])
        raw, u, dt, da = (sb(n, [P, TILES, H]) for n in ("raw", "u", "dt", "da"))
        tok = sb("tok", [P, 2, 384])
        decays = sb("decays", [P, 2, 3 * H])
        after_da, seg = sb("after_da", [P, H, P]), sb("seg", [P, H, P])
        cb, mix = sb("cb", [P, P]), sb("mix", [P, H, P])
        xdt, xdecay = sb("xdt", [P, H, HD]), sb("xdecay", [P, H, HD])
        state, faded = sb("state", [P, 2, H, HD]), sb("faded", [P, H, HD])
        y, skip, yn, ynT = sb("y", [P, TILES, INNER]), sb("skip", [P, INNER]), sb("yn", [P, TILES, INNER]), sb("ynT", [P, 2, 512])
        dve_step, act_step, set_up = sem("dve_step"), sem("act_step"), sem("set_up")
        xnT_done, xnT_ready, chan_done, padded_ready, conv_ready, chan_ready, z_done, zs_ready, dt_done, raw_ready, u_ready, da_ready = (
            sem(n) for n in ("xnT_done", "xnT_ready", "chan_done", "padded_ready", "conv_ready", "chan_ready", "z_done", "zs_ready",
                             "dt_done", "raw_ready", "u_ready", "da_ready"))
        tok_done, tok_ready, sums_done, decays_ready, after_ready, seg_done, seg_ready, cb_done, mix_ready, xdt_ready, xdecay_ready = (
            sem(n) for n in ("tok_done", "tok_ready", "sums_done", "decays_ready", "after_ready", "seg_done", "seg_ready", "cb_done",
                             "mix_ready", "xdt_ready", "xdecay_ready"))
        off_done, add_done, diag_done, state_ready, y_ready, ynT_done, ynT_ready, out_done = (
            sem(n) for n in ("off_done", "add_done", "diag_done", "state_ready", "y_ready", "ynT_done", "ynT_ready", "out_done"))
        p_t, p_seg, p_cb, p_diag, p_off, p_add, p_z, p_small = k.banks
        p_chan = k.banks[1:5]
        p_zs = (p_add, p_z)

        with nc.Block() as block:
            @block.vector
            def _(dve):
                k.await_parameters(dve, "ssd")
                nc.vector.memset(padded[:, :, 0:3], 0.0).then_inc(set_up, 1)
                with dve.Fori(0, SEQS) as s:
                    outer.stats(dve, s, lambda t: k.x[:, bass.ds(s * TILES + t, 1), :])
                    outer.scale(dve, s, lambda t: xin[:, t, :], lambda t: k.x[:, bass.ds(s * TILES + t, 1), :])
                    dve.wait_ge(outer.rows_ready, s + 1)
                    first.stats(dve, s, lambda t: xin[:, t, :])
                    first.scale(dve, s, lambda t: xn[:, t, :], lambda t: xin[:, t, :])
                    step = Steps(dve, dve_step, s, 45)
                    dve.wait_ge(dt_done, s + 1)
                    nc.vector.tensor_tensor(raw[:, :, :], p_small[:, 0:TILES * H].rearrange("p (t h) -> p t h", h=H),
                                            w("ssd_dt_bias").unsqueeze(1).broadcast_to([P, TILES, H]), ALU.add).then_inc(raw_ready, 1)
                    dve.wait_ge(u_ready, s + 1)
                    step(nc.vector.tensor_scalar(dt[:, :, :], u[:, :, :], LOG1P[9], None, ALU.mult))
                    for n in range(8, -1, -1):
                        step(nc.vector.scalar_tensor_tensor(dt[:, :, :], dt[:, :, :], LOG1P[n], u[:, :, :], ALU.add, ALU.mult))
                    step(nc.vector.scalar_tensor_tensor(dt[:, :, :], raw[:, :, :], 0.0, dt[:, :, :], ALU.max, ALU.add))
                    nc.vector.scalar_tensor_tensor(da[:, :, :], dt[:, :, :], -1.0, a_rate[:, :].unsqueeze(1).broadcast_to([P, TILES, H]),
                                                   ALU.mult, ALU.mult).then_inc(da_ready, 1)
                    for m in range(4):
                        dve.wait_ge(padded_ready, s * 4 + m + 1)
                        cw = w("ssd_conv_w")
                        step(nc.vector.tensor_scalar(conv[:, m, :], padded[:, m, 0:512], cw[:, 4 * m:4 * m + 1],
                                                     w("ssd_conv_b")[:, m:m + 1], ALU.mult, ALU.add))
                        for tap in range(1, 4):
                            last = nc.vector.scalar_tensor_tensor(conv[:, m, :], padded[:, m, tap:tap + 512], cw[:, 4 * m + tap:4 * m + tap + 1],
                                                                  conv[:, m, :], ALU.mult, ALU.add)
                            if tap < 3:
                                step(last)
                        last.then_inc(conv_ready, 1)
                    dve.wait_ge(da_ready, s + 1)
                    for c in range(TILES):
                        b = c % 2
                        per_head = lambda ap, n: ap.unsqueeze(2).broadcast_to([P, H, n])
                        for h in range(H):
                            last = nc.vector.tensor_scalar(after_da[:, h, :], w("after"), da[:, c, h:h + 1], None, ALU.mult)
                        last.then_inc(after_ready, 1)
                        dve.wait_ge(tok_ready, s * TILES + c + 1)
                        inputs = tok[:, b, 0:INNER].rearrange("p (h d) -> p h d", d=HD)
                        nc.vector.tensor_tensor(xdt[:, :, :], inputs, per_head(dt[:, c, :], HD), ALU.mult).then_inc(xdt_ready, 1)
                        step(nc.vector.tensor_tensor(skip[:, :], tok[:, b, 0:INNER], w("ssd_d"), ALU.mult))
                        dve.wait_ge(decays_ready, s * TILES + c + 1)
                        dve.wait_ge(xdt_ready, s * TILES + c + 1)
                        nc.vector.tensor_tensor(xdecay[:, :, :], xdt[:, :, :], per_head(decays[:, b, H:2 * H], HD), ALU.mult).then_inc(xdecay_ready, 1)
                        dve.wait_ge(cb_done, s * TILES + c + 1)
                        step(nc.vector.tensor_tensor(cb[:, :], p_cb[:, 0:P], w("causal"), ALU.mult))
                        dve.wait_ge(seg_ready, s * TILES + c + 1)
                        nc.vector.tensor_tensor(mix[:, :, :], seg[:, :, :], cb[:, :].unsqueeze(1).broadcast_to([P, H, P]), ALU.mult).then_inc(mix_ready, 1)
                        add = p_add[:, 0:INNER].rearrange("p (h d) -> p h d", d=HD)
                        if c < TILES - 1:
                            dve.wait_ge(add_done, s * (TILES - 1) + c + 1)
                            if c == 0:
                                nc.vector.tensor_copy(state[:, 1, :, :], add).then_inc(state_ready, 1)
                            else:
                                step(nc.vector.tensor_tensor(faded[:, :, :], state[:, b, :, :], per_head(decays[:, b, 2 * H:3 * H], HD), ALU.mult))
                                nc.vector.tensor_tensor(state[:, 1 - b, :, :], faded[:, :, :], add, ALU.add).then_inc(state_ready, 1)
                        yc = y[:, c, :]
                        yh = yc.rearrange("p (h d) -> p h d", d=HD)
                        if c > 0:
                            dve.wait_ge(off_done, s * (TILES - 1) + c)
                            off = p_off[:, 0:INNER].rearrange("p (h d) -> p h d", d=HD)
                            step(nc.vector.tensor_tensor(yh, off, per_head(decays[:, b, 0:H], HD), ALU.mult))
                            step(nc.vector.tensor_tensor(skip[:, :], skip[:, :], yc, ALU.add))
                        dve.wait_ge(diag_done, s * TILES + c + 1)
                        step(nc.vector.tensor_tensor(skip[:, :], p_diag[:, 0:INNER], skip[:, :], ALU.add))
                        dve.wait_ge(zs_ready, (s + 1) * 2)
                        nc.vector.tensor_tensor(yc, skip[:, :], zs[:, c, :], ALU.mult).then_inc(y_ready, 1)
                        dve.wait_ge(y_ready, s * TILES + c + 1)
                        if c < TILES - 1:
                            dve.wait_ge(state_ready, s * (TILES - 1) + c + 1)
                    gnorm.stats(dve, s, lambda t: y[:, t, :])
                    gnorm.scale(dve, s, lambda t: yn[:, t, :], lambda t: y[:, t, :])
                    xs = k.x[:, bass.ds(s * TILES, TILES), :]
                    step(nc.vector.tensor_tensor(xs, xs, xin[:, :, :], ALU.add))
                    dve.wait_ge(out_done, s + 1)
                    step(nc.vector.tensor_tensor(xs, xs, p_small[:, :].rearrange("p (t d) -> p t d", d=P), ALU.add))
                    step.end()

            @block.scalar
            def _(act):
                k.await_parameters(act, "ssd")
                nc.scalar.preload_act_table_set("natural_log_exp_and_others")
                act.wait_ge(set_up, 1)
                nc.scalar.activation(a_rate[:, :], w("ssd_a_log"), ACT.Exp).then_inc(set_up, 1)
                act.wait_ge(set_up, 2)
                with act.Fori(0, SEQS) as s:
                    nc.scalar.preload_act_table_set("natural_log_exp_and_others")
                    outer.first_guess(act, s)
                    first.first_guess(act, s)
                    act.wait_ge(xnT_done, s + 1)
                    nc.scalar.activation(xnT[:, :], p_t[:, :], ACT.Identity, scale=w("ssd_norm_w"), bias=k.const(0.0)).then_inc(xnT_ready, 1)
                    step = Steps(act, act_step, s, 1)
                    for m in range(4):
                        act.wait_ge(chan_done, s * 4 + m + 1)
                        nc.scalar.copy(padded[:, m, 3:515], p_chan[m][:, :]).then_inc(padded_ready, 1)
                    act.wait_ge(raw_ready, s + 1)
                    step(nc.scalar.activation(u[:, :, :], raw[:, :, :], ACT.Abs))
                    nc.scalar.activation(u[:, :, :], u[:, :, :], ACT.Exp, scale=-1.0).then_inc(u_ready, 1)
                    for n in range(2):
                        act.wait_ge(z_done, s * 2 + n + 1)
                        nc.scalar.activation(zs[:, 2 * n:2 * n + 2, :], p_zs[n][:, :].rearrange("p (t d) -> p t d", d=INNER), ACT.Silu).then_inc(zs_ready, 1)
                    for m in range(4):
                        act.wait_ge(conv_ready, s * 4 + m + 1)
                        nc.scalar.activation(chan[:, m, :], conv[:, m, :], ACT.Silu).then_inc(chan_ready, 1)
                    for c in range(TILES):
                        b = c % 2
                        act.wait_ge(tok_done, s * TILES + c + 1)
                        nc.scalar.copy(tok[:, b, :], p_t[:, 0:384]).then_inc(tok_ready, 1)
                        act.wait_ge(sums_done, s * TILES + c + 1)
                        nc.scalar.activation(decays[:, b, :], p_small[:, 0:3 * H], ACT.Exp).then_inc(decays_ready, 1)
                        act.wait_ge(seg_done, s * TILES + c + 1)
                        nc.scalar.activation(seg[:, :, :], p_seg[:, :].rearrange("p (h i) -> p h i", i=P), ACT.Exp).then_inc(seg_ready, 1)
                    gnorm.first_guess(act, s)
                    for n in range(2):
                        act.wait_ge(ynT_done, s * 2 + n + 1)
                        nc.scalar.activation(ynT[:, n, :], (p_t, p_z)[n][:, :], ACT.Identity, scale=w("ssd_gnorm_w")[:, n:n + 1],
                                             bias=k.const(0.0)).then_inc(ynT_ready, 1)
                    step.end()

            @block.tensor
            def _(pe):
                k.await_parameters(pe, "ssd")
                mm = nc.tensor.matmul
                with pe.Fori(0, SEQS) as s:
                    pe.wait_ge(first.rows_ready, s + 1)
                    transpose_tiles(nc, pe, p_t, lambda t: xn[:, t, :], w("ident")).then_inc(xnT_done, 1)
                    pe.wait_ge(xnT_ready, s + 1)
                    for t in range(TILES):
                        last = mm(p_small[:, t * H:(t + 1) * H], xnT[:, t * P:(t + 1) * P], w("ssd_wdt"), start=True, stop=True)
                    last.then_inc(dt_done, 1)
                    for m in range(4):
                        mm(p_chan[m][:, :], w("ssd_wx")[:, m * P:(m + 1) * P], xnT[:, :], start=True, stop=True).then_inc(chan_done, 1)
                    for n in range(2):
                        for t in (2 * n, 2 * n + 1):
                            last = mm(p_zs[n][:, t % 2 * INNER:(t % 2 + 1) * INNER], xnT[:, t * P:(t + 1) * P], w("ssd_wz"), start=True, stop=True)
                        last.then_inc(z_done, 1)
                    pe.wait_ge(padded_ready, (s + 1) * 4)
                    pe.wait_ge(zs_ready, (s + 1) * 2)
                    for c in range(TILES):
                        tokens = slice(c * P, (c + 1) * P)
                        if c == 0:
                            pe.wait_ge(da_ready, s + 1)
                        else:
                            pe.wait_ge(decays_ready, s * TILES + c)
                        for n, name in enumerate(("causal", "after", "ones")):
                            last = mm(p_small[:, n * H:(n + 1) * H], w(name), da[:, c, :], start=True, stop=True)
                        last.then_inc(sums_done, 1)
                        pe.wait_ge(after_ready, s * TILES + c + 1)
                        if c > 0:
                            pe.wait_ge(seg_ready, s * TILES + c)
                        for h in range(H):
                            last = mm(p_seg[:, h * P:(h + 1) * P], after_da[:, h, :], w("causal"), start=True, stop=True)
                        last.then_inc(seg_done, 1)
                        if c == 0:
                            pe.wait_ge(chan_ready, (s + 1) * 4)
                        else:
                            pe.wait_ge(tok_ready, s * TILES + c)
                        for m in range(3):
                            last = nc.tensor.transpose(p_t[:, m * P:(m + 1) * P], chan[:, m, tokens], w("ident"))
                        last.then_inc(tok_done, 1)
                        if c > 0:
                            pe.wait_ge(mix_ready, s * TILES + c)
                        mm(p_cb[:, 0:P], chan[:, 2, tokens], chan[:, 3, tokens], start=True, stop=True).then_inc(cb_done, 1)
                        if c > 0:
                            pe.wait_ge(state_ready, s * (TILES - 1) + c)
                            pe.wait_ge(y_ready, s * TILES + c)
                            mm(p_off[:, 0:INNER], chan[:, 3, tokens], state[:, c % 2, :, :], start=True, stop=True).then_inc(off_done, 1)
                        if c < TILES - 1:
                            pe.wait_ge(xdecay_ready, s * TILES + c + 1)
                            mm(p_add[:, 0:INNER], tok[:, c % 2, INNER:384], xdecay[:, :, :], start=True, stop=True).then_inc(add_done, 1)
                        pe.wait_ge(mix_ready, s * TILES + c + 1)
                        for h in range(H):
                            last = mm(p_diag[:, h * HD:(h + 1) * HD], mix[:, h, :], xdt[:, h, :], start=True, stop=True)
                        last.then_inc(diag_done, 1)
                    pe.wait_ge(gnorm.rows_ready, s + 1)
                    for n in range(2):
                        transpose_tiles(nc, pe, (p_t, p_z)[n], lambda t: yn[:, t, n * P:(n + 1) * P], w("ident")).then_inc(ynT_done, 1)
                    pe.wait_ge(ynT_ready, (s + 1) * 2)
                    for t in range(TILES):
                        for n in range(2):
                            last = mm(p_small[:, t * P:(t + 1) * P], ynT[:, n, t * P:(t + 1) * P], w("ssd_wo")[:, n * P:(n + 1) * P],
                                      start=(n == 0), stop=(n == 1))
                    last.then_inc(out_done, 1)


class Kit:

    FIRST = 128

    def __init__(self, nc):
        self.nc, self.semaphores = nc, []

    def semaphore(self, ctx, name):
        self.semaphores.append(ctx.enter_context(self.nc.semaphore(name, num=self.FIRST + len(self.semaphores))))
        return self.semaphores[-1]

    def end_stage(self):
        self.nc.gpsimd.sem_clear(range(self.FIRST, self.FIRST + len(self.semaphores)))
        self.nc.all_engine_barrier()
        self.semaphores = []


STAGE = {"gla": gla_stage, "ffn": ffn_stage, "favor": favor_stage, "taylor": taylor_stage, "moe": moe_stage, "ssd": ssd_stage}
CONSTS = (0.0, 1e-12, 1e-5, 1e-6, 1.0, -0.5 * float(np.log(32.0)), 4.0 / 32.0 ** 0.5)


def program(nc, x_dram, w_dram, out_dram, places, groups, width):
    k = Kit(nc)
    with ExitStack() as ctx:
        k.x = ctx.enter_context(nc.sbuf_tensor("x", [P, SEQS * TILES, DIM], F32))
        sizes = {g: z - a for g, (a, z) in groups.items()}
        on_chip, at = {}, 0
        for g in groups:
            if g not in EARLY + LATE:
                on_chip[g] = at
                at += sizes[g]
        ends = []
        for shared in (EARLY, LATE):
            end = at
            for g in shared:
                on_chip[g] = end
                end += sizes[g]
            ends.append(end)
        weights = ctx.enter_context(nc.sbuf_tensor("weights", [P, max(ends)], F32))
        consts = ctx.enter_context(nc.sbuf_tensor("consts", [P, len(CONSTS)], F32))
        k.spare = ctx.enter_context(nc.sbuf_tensor("spare", [P, 2], F32))
        k.banks = [ctx.enter_context(nc.psum_tensor(f"bank{n}", [P, 512], F32)) for n in range(8)]
        x_loaded = ctx.enter_context(nc.semaphore("x_loaded"))
        loaded = {g: ctx.enter_context(nc.semaphore(g + "_loaded")) for g in groups}
        consts_set = ctx.enter_context(nc.semaphore("consts_set"))
        stored = ctx.enter_context(nc.semaphore("stored"))

        def w(name):
            at, rows, cols = places[name]
            group = next(g for g, (a, z) in groups.items() if a <= at < z)
            at += on_chip[group] - groups[group][0]
            return weights[0:rows, at:at + cols]

        def load(sp, group):
            (a, z), at = groups[group], on_chip[group]
            sp.dma_start(weights[:, at:at + z - a].rearrange("p (r c) -> p r c", c=RUN),
                         w_dram[:, a:z].rearrange("p (r c) -> p r c", c=RUN)).then_inc(loaded[group], 16)

        def await_parameters(eng, group):
            eng.wait_ge(loaded["common"], 16)
            eng.wait_ge(loaded[group], 16)

        k.w = w
        k.await_parameters = await_parameters
        k.const = lambda v: consts[:, CONSTS.index(v):CONSTS.index(v) + 1]
        x_tiles = x_dram.rearrange("b (t p) d -> p (b t) d", p=P)
        out_tiles = out_dram.rearrange("b (t p) d -> p (b t) d", p=P)

        with nc.Block() as block:
            @block.sync
            def _(sp):
                sp.dma_start(k.x[:, :, :], x_tiles).then_inc(x_loaded, 16)
                for g in groups:
                    if g not in LATE:
                        load(sp, g)
                sp.wait_ge(x_loaded, 16)

            @block.vector
            def _(dve):
                for n, v in enumerate(CONSTS):
                    nc.vector.memset(consts[:, n:n + 1], v).then_inc(consts_set, 1)
                nc.vector.memset(k.spare[:, :], 0.0).then_inc(consts_set, 1)
                dve.wait_ge(consts_set, len(CONSTS) + 1)

        stages = STAGES.split()
        for n, name in enumerate(stages):
            if name not in EARLY and not set(stages[:n]) - set(EARLY):
                with nc.Block() as block:
                    @block.sync
                    def _(sp):
                        for g in EARLY:
                            sp.wait_ge(loaded[g], 16)
                        for g in LATE:
                            load(sp, g)
            STAGE[name](nc, k, n)
            k.end_stage()

        with nc.Block() as block:
            @block.sync
            def _(sp):
                for g in groups:
                    if g in EARLY or set(stages) - set(EARLY):
                        sp.wait_ge(loaded[g], 16)
                sp.dma_start(out_tiles, k.x[:, :, :]).then_inc(stored, 16)
                sp.wait_ge(stored, 16)


def kernel(**inputs):
    import concourse.bacc as _bacc
    from concourse.bass_utils import run_bass_kernel_spmd as _run

    nc = _bacc.Bacc("TRN2", target_bir_lowering=False, num_devices=1)
    blocks = parameter_blocks(inputs)
    places, groups, width = placed(blocks)
    packed = np.zeros((P, width), np.float32)
    for name, (at, rows, cols) in places.items():
        packed[:rows, at:at + cols] = blocks[name]
    x = np.ascontiguousarray(inputs["L0_attn_a_x"])
    x_dram = nc.dram_tensor("x_dram", x.shape, F32, kind="ExternalInput").ap()
    w_dram = nc.dram_tensor("w_dram", packed.shape, F32, kind="ExternalInput").ap()
    out_dram = nc.dram_tensor("out_dram", x.shape, F32, kind="ExternalOutput").ap()
    program(nc, x_dram, w_dram, out_dram, places, groups, width)
    r = _run(nc, [{"x_dram": x, "w_dram": packed}], core_ids=[0])
    return r.results[0]["out_dram"]
```

```python
from contextlib import ExitStack

import concourse.bass as bass
from concourse import mybir
import numpy as np

F32 = mybir.dt.float32
BF16 = mybir.dt.bfloat16
ALU = mybir.AluOpType
ACT = mybir.ActivationFunctionType
AX = mybir.AxisListType.X

P = 128
SEQS, SEQ_LEN, DIM = 8, 512, 128
TILES = SEQ_LEN // P
HEADS = 16
STAGES = "gla ffn favor ffn taylor moe ssd moe"


class Steps:

    def __init__(self, eng, sem, s, per):
        self.eng, self.sem, self.s, self.per, self.n = eng, sem, s, per, 0

    def __call__(self, ins):
        ins.then_inc(self.sem, 1)
        self.n += 1
        self.eng.wait_ge(self.sem, self.s * self.per + self.n)

    def end(self):
        assert self.n == self.per, (self.n, self.per)


def log1p_series():
    u = 0.5 - 0.5 * np.cos(np.pi * (np.arange(400) + 0.5) / 400)
    fit = np.polynomial.chebyshev.Chebyshev.fit(u, np.log1p(u) / u, 9, domain=[0, 1])
    return [float(c) for c in fit.convert(kind=np.polynomial.Polynomial).coef]



def parameter_blocks(i):
    f = lambda name: np.asarray(i[name])
    col = lambda v: v.reshape(-1, 1)
    row = lambda v: np.broadcast_to(v.reshape(1, -1), (P, v.size))
    tall = lambda w: w.reshape(-1, P, w.shape[-1]).transpose(1, 0, 2).reshape(P, -1)
    b = {}
    b["ident"] = np.eye(P)
    j, q = np.arange(P)[:, None], np.arange(P)[None, :]
    b["causal"] = (j <= q) * 1.0
    b["after"] = (j > q) * 1.0
    b["ones"] = np.ones((P, P))
    b["attn_den"] = b["favor_den"] = ((j // 16 == q // 16) & (j % 16 == 8)) * 1.0
    wq, wk, wv = (f("L0_attn_a_" + n) for n in ("Wq", "Wk", "Wv"))
    b["gla_wq"] = np.repeat(wq, 8, axis=1)
    b["gla_wk"] = np.repeat(wk, 8, axis=1)
    b["gla_wv"] = np.repeat(wv.reshape(P, HEADS, 1, 8), 4, axis=2).reshape(P, 512)
    b["gla_wgk1"] = f("L0_attn_a_Wgk1")
    b["gla_wgk2"] = f("L0_attn_a_Wgk2")
    b["gla_bgk2"] = col(f("L0_attn_a_bgk2"))
    b["gla_wg"] = f("L0_attn_a_Wg")
    b["gla_gnw"] = col(np.tile(f("L0_attn_a_gnw"), HEADS))
    b["gla_wo"] = f("L0_attn_a_Wo")
    b["gla_spread"] = (np.arange(64)[:, None] == np.arange(512)[None, :] // 8) * 1.0
    r, c = np.arange(512)[:, None], np.arange(P)[None, :]
    b["gla_sum"] = tall(((r // 32 == c // 8) & (r % 8 == c % 8)) * 1.0)
    b["head_mean"] = (j // 8 == q // 8) / 8.0
    b["ffn_w1"] = f("L0_ffn_W1").T
    b["ffn_w2"] = tall(f("L0_ffn_W2").T)
    b["ffn_ln_g"], b["ffn_ln_b"] = col(f("L0_ffn_ln_g")), col(f("L0_ffn_ln_b"))
    b["ffn_router"] = f("L0_ffn_router_W").T
    b["ffn_router_b"] = row(f("L0_ffn_router_b"))
    b["ffn_u_t"] = f("L0_ffn_raw_U").T
    b["ffn_u"], b["ffn_v"] = f("L0_ffn_raw_U"), f("L0_ffn_raw_V")
    b["ffn_gamma"] = row(f("L0_ffn_gamma"))
    for n in ("q", "k", "v", "out"):
        b[f"favor_{n}_w"] = f(f"L0_attn_b_{n}_w")
    for n in "qk":
        weight, bias = b.pop(f"favor_{n}_w").reshape(P, 2, 1, 64), f(f"L0_attn_b_{n}_b").reshape(2, 1, 64)
        b[f"favor_{n}_w2"] = np.broadcast_to(weight, (P, 2, 2, 64)).reshape(P, 256)
        b[f"favor_{n}_b2"] = np.broadcast_to(bias, (2, 2, 64)).reshape(2, P).T
    for n in ("v_b", "out_b", "gamma", "beta"):
        b[f"favor_{n}"] = row(f(f"L0_attn_b_{n}"))
    same = np.arange(64)[:, None] // 8 == np.arange(256)[None, :] // 32
    b["favor_map"] = np.concatenate([np.where(same, np.tile(f("L0_attn_b_proj").T, (8, 8)), 0.0), same * -0.5])
    b["favor_own"] = (j // 32 == np.arange(64)[None, :] // 16) * 1.0
    b["favor_own_rows"] = (j // 32 == np.arange(4)[None, :]) * 1.0
    b["favor_own_bias"] = np.where(j // 32 == np.arange(4)[None, :], -0.5 * np.log(32.0), -1e30)
    pad = np.zeros((HEADS, 16, P), np.float32)
    pad[:, :8] = b.pop("favor_out_w").reshape(HEADS, 8, P)
    b["favor_out_rows"] = tall(pad.reshape(-1, P))
    for n in ("q", "k", "v"):
        b[f"taylor_w{n}"] = f(f"L1_attn_a_W{n}").T
    b["taylor_wo"] = tall(f("L1_attn_a_Wo").T)
    b["taylor_own"] = (np.arange(P)[:, None] // 16 == np.arange(8)[None, :]) * 1.0
    wide = (j <= np.arange(512)[None, :]) * 1.0
    b["taylor_causal"] = np.concatenate([wide, wide[:, :384], wide[:, :P], wide[:, :256]], axis=1)
    for n in ("q", "k", "v", "o"):
        b[f"attn_w{n}"] = f(f"L1_ffn_w{n}")
    half = np.arange(P) // 8 * 8 + (np.arange(P) + 4) % 8
    b["attn_wq_rot"], b["attn_wk_rot"] = f("L1_ffn_wq")[:, half], f("L1_ffn_wk")[:, half]
    inv_freq = 1.0 / 10000.0 ** (np.arange(0, 8, 2, dtype=np.float32) / 8)
    freqs = np.einsum("i,j->ij", np.arange(SEQ_LEN, dtype=np.float32), inv_freq)
    angle = np.tile(np.concatenate([freqs, freqs], axis=-1).T, (HEADS, 1))
    b["attn_cos"] = np.cos(angle)
    b["attn_sin"] = np.sin(angle) * np.where(np.arange(P) % 8 < 4, -1.0, 1.0)[:, None]
    b["attn_g1"], b["attn_g2"] = col(f("L1_ffn_g1")), col(f("L1_ffn_g2"))
    part_of = {"k": (0, 1, 0, 1, 2, 0), "q": (0, 0, 1, 1, 0, 2)}
    r, c = np.arange(P)[:, None], np.arange(P)[None, :]
    takes = (c < 96) & (r // 8 % 2 == c // 48) & (r % 8 == c % 8)
    b["attn_stack"] = np.concatenate([takes & (np.tile(np.repeat(part_of[side], 8), 3)[:P][None, :] == part)
                                      for side in "kq" for part in range(3)], axis=1) * 1.0
    b["attn_of_pair"] = (r // 16 == np.arange(8)[None, :]) * 1.0
    b["attn_of_head"] = (r // 48 == np.arange(2)[None, :]) * 1.0
    b["attn_pick"] = ((r < 8) & (r % 4 == np.arange(4)[None, :])) * -1.0
    wo = np.zeros((HEADS, 16, P), np.float32)
    wo[:, :8] = b.pop("attn_wo").reshape(HEADS, 8, P)
    b["attn_wo_rows"] = tall(wo.reshape(-1, P))
    b["future"] = (j > q) * -1e30
    b["moe_router"] = f("L1_ffn_w_router")
    b["expert_wg"] = f("L1_ffn_wg").transpose(1, 0, 2).reshape(P, -1)
    b["expert_wu"] = f("L1_ffn_wu").transpose(1, 0, 2).reshape(P, -1)
    b["moe_wd"] = tall(f("L1_ffn_wd").reshape(-1, P))
    b["moe_index"] = row(np.arange(8))
    ip = f("L1_attn_b_in_proj_w").T
    b["ssd_wz"], b["ssd_wx"], b["ssd_wdt"] = ip[:, 0:256], ip[:, 256:768], ip[:, 768:772]
    b["ssd_norm_w"] = col(f("L1_attn_b_norm_w"))
    b["ssd_conv_w"] = tall(f("L1_attn_b_conv_w"))
    b["ssd_conv_b"] = tall(col(f("L1_attn_b_conv_b")))
    b["ssd_dt_bias"], b["ssd_a_log"] = row(f("L1_attn_b_dt_bias")), row(f("L1_attn_b_A_log"))
    b["ssd_d"] = row(np.repeat(f("L1_attn_b_D"), 64))
    b["ssd_gnorm_w"] = tall(col(f("L1_attn_b_gnorm_w")))
    b["ssd_wo"] = tall(f("L1_attn_b_out_proj_w").T)
    return {k: np.ascontiguousarray(v, dtype=np.float32) for k, v in b.items()}


EARLY, LATE = ("gla", "ffn", "favor"), ("moe", "ssd")
SPLIT = "expert"
RUN = 512
GROUPS = {"common": ("ident", "causal", "after", "ones"), "gla": ("gla_", "head_mean"), "ffn": ("ffn_",), "favor": ("favor_",),
          "taylor": ("taylor_",), "moe": ("attn_", "moe_", "future"), "ssd": ("ssd_",),
          "expert": ("expert_",)}


def placed(blocks):
    at, out, groups = 0, {}, {}
    for group, starts in GROUPS.items():
        first = at
        for name, a in blocks.items():
            if (name in starts) if group == "common" else (name.startswith(starts) and name not in GROUPS["common"]):
                out[name] = (at, *a.shape)
                at += a.shape[1]
        at = -(-at // RUN) * RUN
        groups[group] = (first, at)
    assert len(out) == len(blocks)
    return out, groups, at


def carry_wait(nc, spare):
    return nc.vector.tensor_copy(spare[:, 0:1], spare[:, 1:2])


def refine_rsqrt(nc, step, out, var, eps, guess, tmp):
    step(nc.vector.scalar_tensor_tensor(tmp, var, eps, guess, ALU.add, ALU.mult))
    step(nc.vector.tensor_tensor(tmp, tmp, guess, ALU.mult))
    step(nc.vector.tensor_scalar(tmp, tmp, -0.5, 1.5, ALU.mult, ALU.add))
    return nc.vector.tensor_tensor(out, tmp, guess, ALU.mult)


class Norm:

    def __init__(self, nc, ctx, k, name, eps, rms=False):
        sb = lambda n, shape: ctx.enter_context(nc.sbuf_tensor(f"{name}_{n}", shape, F32))
        sem = lambda n: k.semaphore(ctx, f"{name}_{n}")
        self.nc, self.k, self.eps, self.rms = nc, k, eps, rms
        self.stats_, self.mean_var = sb("stats", [P, TILES, 6]), sb("mean_var", [P, TILES, 2])
        self.guess, self.rstd, self.tmp = (sb(n, [P, TILES]) for n in ("guess", "rstd", "tmp"))
        self.dve_step, self.act_step = sem("dve_step"), sem("act_step")
        self.var_ready, self.guess_ready, self.rows_ready = sem("var_ready"), sem("guess_ready"), sem("rows_ready")

    def stats(self, dve, s, rows):
        nc, per = self.nc, 7 if self.rms else 5
        self.step = Steps(dve, self.dve_step, s, per)
        for t in range(TILES):
            last = nc.vector.bn_stats(self.stats_[:, t, :], rows(t))
        self.step(last)
        carry_wait(nc, self.k.spare)
        for t in range(TILES):
            last = nc.vector.bn_aggr(self.mean_var[:, t, :], self.stats_[:, t, :])
        if self.rms:
            mean, var = self.mean_var[:, :, 0], self.mean_var[:, :, 1]
            self.step(last)
            self.step(nc.vector.tensor_tensor(mean, mean, mean, ALU.mult))
            last = nc.vector.tensor_tensor(var, var, mean, ALU.add)
        last.then_inc(self.var_ready, 1)

    def first_guess(self, act, s):
        nc = self.nc
        act.wait_ge(self.var_ready, s + 1)
        nc.scalar.activation(self.guess[:, :], self.mean_var[:, :, 1], ACT.Ln, bias=self.k.const(self.eps)).then_inc(self.act_step, 1)
        act.wait_ge(self.act_step, s + 1)
        nc.scalar.activation(self.guess[:, :], self.guess[:, :], ACT.Exp, scale=-0.5).then_inc(self.guess_ready, 1)

    def scale(self, dve, s, out, rows):
        nc, step = self.nc, self.step
        dve.wait_ge(self.guess_ready, s + 1)
        step(refine_rsqrt(nc, step, self.rstd[:, :], self.mean_var[:, :, 1], self.eps, self.guess[:, :], self.tmp[:, :]))
        for t in range(TILES):
            if self.rms:
                last = nc.vector.tensor_scalar(out(t), rows(t), self.rstd[:, t:t + 1], None, ALU.mult)
            else:
                last = nc.vector.tensor_scalar(out(t), rows(t), self.mean_var[:, t, 0:1], self.rstd[:, t:t + 1],
                                               ALU.subtract, ALU.mult)
        last.then_inc(self.rows_ready, 1)
        step.end()


def transpose_tiles(nc, pe, bank, rows, ident):
    for t in range(TILES):
        r = rows(t)
        last = nc.tensor.transpose(bank[:, t * P:(t + 1) * P], r, ident)
    return last


class InputNorm:

    def __init__(self, nc, ctx, k, name, eps, second_eps=None):
        sb = lambda n, shape: ctx.enter_context(nc.sbuf_tensor(f"{name}_{n}", shape, F32))
        sem = lambda n: k.semaphore(ctx, f"{name}_{n}")
        self.nc, self.k, self.eps = nc, k, [eps] + [second_eps] * (second_eps is not None)
        self.rows = SEQS * TILES
        self.phases = slice(0, TILES), slice(TILES, self.rows)
        self.row_stats, self.mean_var = sb("stats", [P, self.rows, 6]), sb("mean_var", [P, self.rows, 2])
        self.var = sb("var", [P, self.rows])
        self.guess, self.tmp = sb("guess", [P, self.rows]), sb("tmp", [P, self.rows])
        self.rstd = [sb(f"rstd{n}", [P, self.rows]) for n in range(len(self.eps))]
        self.vector_step, self.scalar_step = sem("vector_step"), sem("scalar_step")
        self.var_ready, self.guess_ready = sem("var_ready"), sem("guess_ready")
        self.rows_ready = [sem(f"rows_ready{n}") for n in range(len(self.eps))]

    def statistics(self, dve, phase):
        nc = self.nc
        if phase == 0:
            self.step = Steps(dve, self.vector_step, 0, 0)
        step, ready = self.step, phase * len(self.eps)
        rows = self.phases[phase]
        for at in range(rows.start, rows.stop, TILES):
            for t in range(TILES):
                last = nc.vector.bn_stats(self.row_stats[:, at + t, :], self.k.x[:, at + t, :])
        step(last)
        for t in range(rows.start, rows.stop):
            last = nc.vector.bn_aggr(self.mean_var[:, t, :], self.row_stats[:, t, :])
        step(last)
        var, guess, tmp = self.var[:, rows], self.guess[:, rows], self.tmp[:, rows]
        rstd = [r[:, rows] for r in self.rstd]
        nc.vector.tensor_copy(var, self.mean_var[:, rows, 1]).then_inc(self.var_ready, 1)
        dve.wait_ge(self.var_ready, ready + 1)
        dve.wait_ge(self.guess_ready, ready + 1)
        step(refine_rsqrt(nc, step, rstd[0], var, self.eps[0], guess, tmp))
        if len(rstd) == 2:
            step(nc.vector.tensor_tensor(var, var, rstd[0], ALU.mult))
            nc.vector.tensor_tensor(var, var, rstd[0], ALU.mult).then_inc(self.var_ready, 1)
            dve.wait_ge(self.var_ready, ready + 2)
            dve.wait_ge(self.guess_ready, ready + 2)
            step(refine_rsqrt(nc, step, rstd[1], var, self.eps[1], guess, tmp))
            step(nc.vector.tensor_tensor(rstd[1], rstd[1], rstd[0], ALU.mult))

    def first_guesses(self, act, phase):
        nc, rows = self.nc, self.phases[phase]
        for n, eps in enumerate(self.eps):
            ready = phase * len(self.eps) + n + 1
            act.wait_ge(self.var_ready, ready)
            nc.scalar.activation(self.guess[:, rows], self.var[:, rows], ACT.Ln, bias=self.k.const(eps)).then_inc(self.scalar_step, 1)
            act.wait_ge(self.scalar_step, ready)
            nc.scalar.activation(self.guess[:, rows], self.guess[:, rows], ACT.Exp, scale=-0.5).then_inc(self.guess_ready, 1)

    def scale(self, s, out, n=0, signal=None):
        for t in range(TILES):
            row = bass.ds(s * TILES + t, 1)
            last = self.nc.vector.tensor_scalar(out(t), self.k.x[:, row, :], self.mean_var[:, row, 0], self.rstd[n][:, row],
                                                ALU.subtract, ALU.mult)
        last.then_inc(signal or self.rows_ready[n], 1)


def gla_stage(nc, k, n_stage):
    with ExitStack() as ctx:
        sb = lambda name, shape: ctx.enter_context(nc.sbuf_tensor("gla_" + name, shape, F32))
        sem = lambda name: k.semaphore(ctx, "gla_" + name)
        outer = InputNorm(nc, ctx, k, "gla_outer", 1e-5)
        xn, xT = sb("xn", [P, TILES, P]), sb("xT", [P, 512])
        low = sb("low", [16, 512])
        gate, gate_abs, gate_log = sb("gate", [64, 512]), sb("gate_abs", [64, 512]), sb("gate_log", [64, 512])
        decay = sb("decay", [64, 512])
        val, kv, hid = sb("val", [P, 2, 512]), sb("kv", [P, 512]), sb("hid", [P, 512])
        qh = sb("qh", [P, TILES, 512])
        osq, olog, orstd, gsil = sb("osq", [P, 512]), sb("olog", [P, 512]), sb("orstd", [P, 512]), sb("gsil", [P, 512])
        og = sb("og", [P, 512])
        dve_step, act_step, gate_step, out_taken = (sem(n) for n in ("dve_step", "act_step", "gate_step", "out_taken"))
        xnT_ready, xT_ready = sem("xnT_ready"), sem("xT_ready")
        low_done, low_ready, z_done, zlog_ready, zmin_ready, decay_ready = (
            sem(n) for n in ("low_done", "low_ready", "z_done", "zlog_ready", "zmin_ready", "decay_ready"))
        kvq_done, val_ready, kv_ready, scan_done, qh_ready = (sem(n) for n in ("kvq_done", "val_ready", "kv_ready", "scan_done", "qh_ready"))
        o_done, g_done, osq_ready, ms_done, orstd_ready, gsil_ready, og_ready, y_done = (
            sem(n) for n in ("o_done", "g_done", "osq_ready", "ms_done", "orstd_ready", "gsil_ready", "og_ready", "y_done"))
        p_tile = k.banks[0:4], k.banks[4:8]
        po, pg, pm, py = p_tile[0]
        pxT, pz = p_tile[1][0:2]
        w = k.w

        with nc.Block() as block:
            @block.vector
            def _(dve):
                k.await_parameters(dve, "gla")
                outer.statistics(dve, 0)

                def log_decay(s):
                    dve.wait_ge(zlog_ready, s + 1)
                    nc.vector.scalar_tensor_tensor(gate_log[:, :], gate[:, :], 0.0, gate_log[:, :], ALU.min,
                                                   ALU.subtract).then_inc(zmin_ready, 1)

                def sequence(s, more):
                    step = Steps(dve, dve_step, s, 2)
                    xs = k.x[:, bass.ds(s * TILES, TILES), :]
                    for t in range(TILES):
                        pk, _, pq, pa = p_tile[t % 2]
                        dve.wait_ge(val_ready, s * TILES + t + 1)
                        nc.vector.tensor_tensor(kv[:, :], pk[:, :], val[:, t % 2, :], ALU.mult).then_inc(kv_ready, 1)
                        dve.wait_ge(kv_ready, s * TILES + t + 1)
                        nc.vector.tensor_tensor_scan(hid[:, :], pa[:, :], kv[:, :], 0.0, ALU.mult, ALU.add).then_inc(scan_done, 1)
                        dve.wait_ge(scan_done, s * TILES + t + 1)
                        nc.vector.scalar_tensor_tensor(qh[:, t, :], pq[:, :], 0.5, hid[:, :], ALU.mult,
                                                       ALU.mult).then_inc(qh_ready, 1)
                    if more:
                        outer.scale(s + 1, lambda t: xn[:, t, :])
                    dve.wait_ge(orstd_ready, s + 1)
                    step(nc.vector.scalar_tensor_tensor(og[:, :], po[:, :], w("gla_gnw"), orstd[:, :], ALU.mult, ALU.mult))
                    dve.wait_ge(gsil_ready, s + 1)
                    nc.vector.tensor_tensor(og[:, :], og[:, :], gsil[:, :], ALU.mult).then_inc(og_ready, 1)
                    if more:
                        log_decay(s + 1)
                    dve.wait_ge(y_done, s + 1)
                    step(nc.vector.tensor_tensor(xs, xs, py[:, :].rearrange("p (t d) -> p t d", d=P), ALU.add))
                    carry_wait(nc, k.spare).then_inc(out_taken, 1)
                    step.end()

                outer.scale(0, lambda t: xn[:, t, :])
                outer.statistics(dve, 1)
                log_decay(0)
                carry_wait(nc, k.spare).then_inc(out_taken, 1)
                with dve.Fori(0, SEQS - 1) as s:
                    sequence(s, True)
                sequence(SEQS - 1, False)

            @block.scalar
            def _(act):
                k.await_parameters(act, "gla")
                nc.scalar.preload_act_table_set("natural_log_exp_and_others")
                outer.first_guesses(act, 0)

                def turn_rows(s):
                    act.wait_ge(xnT_ready, s + 1)
                    nc.scalar.copy(xT[:, :], pxT[:, :]).then_inc(xT_ready, 1)

                def low_rank(s):
                    act.wait_ge(low_done, s + 1)
                    nc.scalar.copy(low[:, :], pz[0:16, :]).then_inc(low_ready, 1)

                def decays(s):
                    step = Steps(act, gate_step, s, 3)
                    nc.scalar.preload_act_table_set("natural_log_exp_and_others")
                    act.wait_ge(z_done, s + 1)
                    step(nc.scalar.activation(gate[:, :], pz[0:64, :], ACT.Identity, bias=w("gla_bgk2")))
                    step(nc.scalar.activation(gate_abs[:, :], gate[:, :], ACT.Abs))
                    step(nc.scalar.activation(gate_abs[:, :], gate_abs[:, :], ACT.Exp, scale=-1.0))
                    nc.scalar.activation(gate_log[:, :], gate_abs[:, :], ACT.Ln, bias=k.const(1.0)[0:64, :]).then_inc(zlog_ready, 1)
                    act.wait_ge(zmin_ready, s + 1)
                    nc.scalar.activation(decay[:, :], gate_log[:, :], ACT.Exp, scale=1 / 16).then_inc(decay_ready, 1)
                    step.end()

                def sequence(s, more):
                    step = Steps(act, act_step, s, 2)
                    for t in range(TILES):
                        act.wait_ge(kvq_done, s * TILES + t + 1)
                        if t >= 2:
                            act.wait_ge(kv_ready, s * TILES + t - 1)
                        nc.scalar.copy(val[:, t % 2, :], p_tile[t % 2][1][:, :]).then_inc(val_ready, 1)
                    act.wait_ge(o_done, s + 1)
                    nc.scalar.activation(osq[:, :], po[:, :], ACT.Square).then_inc(osq_ready, 1)
                    if more:
                        turn_rows(s + 1)
                    act.wait_ge(ms_done, s + 1)
                    step(nc.scalar.activation(olog[:, :], pm[:, :], ACT.Ln, bias=k.const(1e-5)))
                    nc.scalar.activation(orstd[:, :], olog[:, :], ACT.Exp, scale=-0.5).then_inc(orstd_ready, 1)
                    if more:
                        low_rank(s + 1)
                    act.wait_ge(g_done, s + 1)
                    step(nc.scalar.activation(gsil[:, :], pg[:, :], ACT.Silu))
                    nc.scalar.copy(gsil[:, :], gsil[:, :]).then_inc(gsil_ready, 1)
                    if more:
                        decays(s + 1)
                    step.end()

                turn_rows(0)
                outer.first_guesses(act, 1)
                low_rank(0)
                decays(0)
                with act.Fori(0, SEQS - 1) as s:
                    sequence(s, True)
                sequence(SEQS - 1, False)

            @block.tensor
            def _(pe):
                k.await_parameters(pe, "gla")
                mm = nc.tensor.matmul

                def turn_rows(s):
                    pe.wait_ge(outer.rows_ready[0], s + 1)
                    transpose_tiles(nc, pe, pxT, lambda t: xn[:, t, :], w("ident")).then_inc(xnT_ready, 1)

                def low_rank(s):
                    pe.wait_ge(xT_ready, s + 1)
                    mm(pz[0:16, :], w("gla_wgk1"), xT[:, :], start=True, stop=True).then_inc(low_done, 1)

                def gates(s):
                    pe.wait_ge(low_ready, s + 1)
                    mm(pz[0:64, :], w("gla_wgk2"), low[:, :], start=True, stop=True).then_inc(z_done, 1)

                def sequence(s, more):
                    for t in range(TILES):
                        pk, pv, pq, pa = p_tile[t % 2]
                        if t >= 2:
                            pe.wait_ge(qh_ready, s * TILES + t - 1)
                        c = slice(t * P, (t + 1) * P)
                        if t == 1:
                            pe.wait_ge(decay_ready, s + 1)
                        mm(pk[:, :], w("gla_wk")[:, c], xT[:, :], start=True, stop=True)
                        mm(pq[:, :], w("gla_wq")[:, c], xT[:, :], start=True, stop=True)
                        mm(pv[:, :], w("gla_wv")[:, c], xT[:, :], start=True, stop=True)
                        if t == 0:
                            pe.wait_ge(out_taken, s + 1)
                            pe.wait_ge(decay_ready, s + 1)
                        mm(pa[:, :], w("gla_spread")[:, c], decay[:, :], start=True, stop=True).then_inc(kvq_done, 1)
                    pe.wait_ge(qh_ready, s * TILES + TILES)
                    for t in range(TILES):
                        last = mm(po[:, :], w("gla_sum")[:, t * P:(t + 1) * P], qh[:, t, :], start=(t == 0), stop=(t == TILES - 1))
                    last.then_inc(o_done, 1)
                    mm(pg[:, :], w("gla_wg"), xT[:, :], start=True, stop=True).then_inc(g_done, 1)
                    if more:
                        turn_rows(s + 1)
                    pe.wait_ge(osq_ready, s + 1)
                    mm(pm[:, :], w("head_mean"), osq[:, :], start=True, stop=True).then_inc(ms_done, 1)
                    if more:
                        low_rank(s + 1)
                        gates(s + 1)
                    pe.wait_ge(og_ready, s + 1)
                    for t in range(TILES):
                        last = mm(py[:, t * P:(t + 1) * P], og[:, t * P:(t + 1) * P], w("gla_wo"), start=True, stop=True)
                    last.then_inc(y_done, 1)

                turn_rows(0)
                low_rank(0)
                gates(0)
                with pe.Fori(0, SEQS - 1) as s:
                    sequence(s, True)
                sequence(SEQS - 1, False)


def ffn_stage(nc, k, n_stage):
    NB = 64
    LOG1P = log1p_series()
    with ExitStack() as ctx:
        sb = lambda name, shape: ctx.enter_context(nc.sbuf_tensor(f"ffn{n_stage}_{name}", shape, F32))
        sem = lambda name: k.semaphore(ctx, f"ffn{n_stage}_{name}")
        w = k.w
        outer = InputNorm(nc, ctx, k, f"ffn{n_stage}_outer", 1e-5, 1e-5)
        xin, xinT = sb("xin", [P, TILES, P]), sb("xinT", [P, 512])
        yn, yT = sb("yn", [P, TILES, P]), sb("yT", [P, 512])
        norms, inv_norms, inv_tmp = sb("norms", [NB, 2]), sb("inv_norms", [NB, 2]), sb("inv_tmp", [NB, 2])
        squares, v_gamma, unit_scale = sb("squares", [NB, P]), sb("v_gamma", [NB, P]), sb("unit_scale", [NB, 1])
        logits, rest, top = sb("logits", [P, TILES, NB]), sb("rest", [P, TILES, NB]), sb("top", [P, TILES, 8])
        u, series = sb("u", [P, TILES, NB]), sb("series", [P, TILES, NB])
        total, total_tanh, factor = sb("total", [P, TILES]), sb("total_tanh", [P, TILES]), sb("factor", [P, TILES])
        hz, hzT = sb("hz", [P, TILES, P]), sb("hzT", [NB, 512])
        hidden = sb("hidden", [P, 4, 512])
        chain_step, dve_step, act_step, out_taken = (sem(n) for n in ("chain_step", "dve_step", "act_step", "out_taken"))
        norms_ready, inv_guess, unit_ready = sem("norms_ready"), sem("inv_guess"), sem("unit_ready")
        xinT_done, xinT_ready, ynT_done, yT_ready = (sem(n) for n in ("xinT_done", "xinT_ready", "ynT_done", "yT_ready"))
        logits_done, logits_ready, u_ready, total_ready, tanh_ready, latent_done = (
            sem(n) for n in ("logits_done", "logits_ready", "u_ready", "total_ready", "tanh_ready", "latent_done"))
        hz_ready, hzT_done, hzT_ready, hidden_done, hidden_ready, out_done = (
            sem(n) for n in ("hz_ready", "hzT_done", "hzT_ready", "hidden_done", "hidden_ready", "out_done"))
        pxT, pyT, pr, pz, ph0, ph1, plat, py = k.banks
        latent = plat[:, 0:TILES * NB].rearrange("p (t n) -> p t n", n=NB)
        router_out = pr[:, 0:TILES * NB].rearrange("p (t n) -> p t n", n=NB)

        with nc.Block() as block:
            @block.vector
            def _(dve):
                k.await_parameters(dve, "ffn")
                step = Steps(dve, norms_ready, 0, 0)
                dve.wait_ge(unit_ready, 2)
                step(nc.vector.tensor_scalar(norms[:, :], norms[:, :], 1e-12, None, ALU.max))
                dve.wait_ge(inv_guess, 1)
                step(refine_rsqrt(nc, step, inv_norms[:, :], norms[:, :], 0.0, inv_norms[:, :], inv_tmp[:, :]))
                step(nc.vector.tensor_tensor(unit_scale[:, :], inv_norms[:, 0:1], inv_norms[:, 1:2], ALU.mult))
                step(nc.vector.tensor_tensor(v_gamma[:, :], w("ffn_v"), w("ffn_gamma")[0:NB, :], ALU.mult))
                step(nc.vector.memset(hz[:, :, NB:P], 0.0))
                outer.statistics(dve, 0)

                def normalise(s):
                    outer.scale(s, lambda t: yn[:, t, :], 1)
                    outer.scale(s, lambda t: xin[:, t, :])

                def route(s):
                    step = Steps(dve, chain_step, s, 16)
                    dve.wait_ge(logits_done, s + 1)
                    step(nc.vector.tensor_tensor(logits[:, :, :], router_out, w("ffn_router_b").unsqueeze(1).broadcast_to([P, TILES, NB]), ALU.add))
                    nc.vector.tensor_scalar(logits[:, :, :], logits[:, :, :], 10.0, -10.0, ALU.min, ALU.max).then_inc(logits_ready, 1)
                    dve.wait_ge(logits_ready, s + 1)
                    carry_wait(nc, k.spare)
                    for t in range(TILES):
                        last = nc.vector.max(top[:, t, :], logits[:, t, :])
                    step(last)
                    carry_wait(nc, k.spare)
                    for t in range(TILES):
                        last = nc.vector.match_replace(rest[:, t, :], top[:, t, :], logits[:, t, :], -1e30)
                    step(last)
                    step(nc.vector.tensor_tensor(rest[:, :, :], rest[:, :, :], logits[:, :, :], ALU.not_equal))
                    dve.wait_ge(u_ready, s + 1)
                    step(nc.vector.tensor_scalar(series[:, :, :], u[:, :, :], LOG1P[9], None, ALU.mult))
                    for n in range(8, -1, -1):
                        step(nc.vector.scalar_tensor_tensor(series[:, :, :], series[:, :, :], LOG1P[n], u[:, :, :], ALU.add, ALU.mult))
                    step(nc.vector.scalar_tensor_tensor(series[:, :, :], logits[:, :, :], 0.0, series[:, :, :], ALU.max, ALU.add))
                    step(nc.vector.tensor_tensor(rest[:, :, :], rest[:, :, :], series[:, :, :], ALU.mult))
                    nc.vector.reduce_sum(total[:, :], rest[:, :, :], AX).then_inc(total_ready, 1)
                    step.end()

                def sequence(s, more):
                    step = Steps(dve, dve_step, s, 5)
                    if more:
                        normalise(s + 1)
                    dve.wait_ge(total_ready, s + 1)
                    step(nc.vector.tensor_scalar(factor[:, :], total[:, :], 1e-6, None, ALU.add))
                    step(nc.vector.reciprocal(factor[:, :], factor[:, :]))
                    dve.wait_ge(tanh_ready, s + 1)
                    step(nc.vector.tensor_tensor(factor[:, :], factor[:, :], total_tanh[:, :], ALU.mult))
                    step(nc.vector.tensor_tensor(rest[:, :, :], rest[:, :, :], factor[:, :].unsqueeze(2).broadcast_to([P, TILES, NB]), ALU.mult))
                    dve.wait_ge(latent_done, s + 1)
                    nc.vector.tensor_tensor(hz[:, :, 0:NB], latent, rest[:, :, :], ALU.mult).then_inc(hz_ready, 1)
                    if more:
                        route(s + 1)
                    dve.wait_ge(out_done, s + 1)
                    xs = k.x[:, bass.ds(s * TILES, TILES), :]
                    step(nc.vector.tensor_tensor(xs, xs, py[:, :].rearrange("p (t d) -> p t d", d=P), ALU.add))
                    carry_wait(nc, k.spare).then_inc(out_taken, 1)
                    step.end()

                normalise(0)
                outer.statistics(dve, 1)
                route(0)
                carry_wait(nc, k.spare).then_inc(out_taken, 1)
                with dve.Fori(0, SEQS - 1) as s:
                    sequence(s, True)
                sequence(SEQS - 1, False)

            @block.scalar
            def _(act):
                k.await_parameters(act, "ffn")
                nc.scalar.preload_act_table_set("natural_log_exp_and_others")
                for n, name in enumerate(("ffn_u", "ffn_v")):
                    nc.scalar.activation(squares[:, :], w(name), ACT.Square, accum_out=norms[:, n:n + 1]).then_inc(unit_ready, 1)
                    act.wait_ge(unit_ready, n + 1)
                act.wait_ge(norms_ready, 1)
                nc.scalar.activation(inv_norms[:, :], norms[:, :], ACT.Ln).then_inc(unit_ready, 1)
                act.wait_ge(unit_ready, 3)
                nc.scalar.activation(inv_norms[:, :], inv_norms[:, :], ACT.Exp, scale=-0.5).then_inc(inv_guess, 1)
                outer.first_guesses(act, 0)

                def turn_rows(s):
                    act.wait_ge(ynT_done, s + 1)
                    nc.scalar.activation(yT[:, :], pyT[:, :], ACT.Identity, scale=w("ffn_ln_g"), bias=w("ffn_ln_b")).then_inc(yT_ready, 1)
                    act.wait_ge(xinT_done, s + 1)
                    nc.scalar.copy(xinT[:, :], pxT[:, :]).then_inc(xinT_ready, 1)

                def exp_and_gelu(s):
                    step = Steps(act, act_step, s, 1)
                    nc.scalar.preload_act_table_set("natural_log_exp_and_others")
                    act.wait_ge(logits_ready, s + 1)
                    step(nc.scalar.activation(u[:, :, :], logits[:, :, :], ACT.Abs))
                    nc.scalar.activation(u[:, :, :], u[:, :, :], ACT.Exp, scale=-1.0).then_inc(u_ready, 1)
                    step.end()
                    for m in range(4):
                        act.wait_ge(hidden_done, s * 4 + m + 1)
                        nc.scalar.activation(hidden[:, m, :], (ph0, ph1)[m % 2][:, :], ACT.Gelu).then_inc(hidden_ready, 1)

                def sequence(s, more):
                    act.wait_ge(total_ready, s + 1)
                    nc.scalar.activation(total_tanh[:, :], total[:, :], ACT.Tanh).then_inc(tanh_ready, 1)
                    if more:
                        turn_rows(s + 1)
                    act.wait_ge(hzT_done, s + 1)
                    nc.scalar.activation(hzT[:, :], pz[0:NB, :], ACT.Identity, scale=unit_scale[:, :]).then_inc(hzT_ready, 1)
                    if more:
                        exp_and_gelu(s + 1)

                turn_rows(0)
                outer.first_guesses(act, 1)
                exp_and_gelu(0)
                with act.Fori(0, SEQS - 1) as s:
                    sequence(s, True)
                sequence(SEQS - 1, False)

            @block.tensor
            def _(pe):
                k.await_parameters(pe, "ffn")
                mm = nc.tensor.matmul

                def route(s):
                    pe.wait_ge(outer.rows_ready[1], s + 1)
                    transpose_tiles(nc, pe, pyT, lambda t: yn[:, t, :], w("ident")).then_inc(ynT_done, 1)
                    pe.wait_ge(outer.rows_ready[0], s + 1)
                    transpose_tiles(nc, pe, pxT, lambda t: xin[:, t, :], w("ident")).then_inc(xinT_done, 1)
                    pe.wait_ge(yT_ready, s + 1)
                    for t in range(TILES):
                        last = mm(pr[:, t * NB:(t + 1) * NB], yT[:, t * P:(t + 1) * P], w("ffn_router"), start=True, stop=True)
                    last.then_inc(logits_done, 1)

                def latents(s):
                    pe.wait_ge(xinT_ready, s + 1)
                    for t in range(TILES):
                        last = mm(plat[:, t * NB:(t + 1) * NB], xinT[:, t * P:(t + 1) * P], w("ffn_u_t"), start=True, stop=True)
                    last.then_inc(latent_done, 1)

                def hidden_layer(s):
                    for m in range(4):
                        if m >= 2:
                            pe.wait_ge(hidden_ready, s * 4 + m - 1)
                        mm((ph0, ph1)[m % 2][:, :], w("ffn_w1")[:, m * P:(m + 1) * P], xinT[:, :], start=True, stop=True).then_inc(hidden_done, 1)

                def sequence(s, more):
                    if more:
                        route(s + 1)
                    pe.wait_ge(hz_ready, s + 1)
                    transpose_tiles(nc, pe, pz, lambda t: hz[:, t, :], w("ident")).then_inc(hzT_done, 1)
                    if more:
                        latents(s + 1)
                    pe.wait_ge(hidden_ready, s * 4 + 4)
                    pe.wait_ge(hzT_ready, s + 1)
                    pe.wait_ge(out_taken, s + 1)
                    for t in range(TILES):
                        c = slice(t * P, (t + 1) * P)
                        for m in range(4):
                            mm(py[:, c], hidden[:, m, c], w("ffn_w2")[:, m * P:(m + 1) * P], start=(m == 0), stop=False)
                        last = mm(py[:, c], hzT[:, c], v_gamma[:, :], start=False, stop=True)
                    last.then_inc(out_done, 1)
                    if more:
                        hidden_layer(s + 1)

                route(0)
                latents(0)
                hidden_layer(0)
                with pe.Fori(0, SEQS - 1) as s:
                    sequence(s, True)
                sequence(SEQS - 1, False)


def favor_stage(nc, k, n_stage):
    M, D, VW = 32, 8, 16
    PER = P // VW
    GROUP = 4
    UNITS = 3 * TILES
    SCALE = D ** -0.5
    with ExitStack() as ctx:
        sb = lambda name, shape: ctx.enter_context(nc.sbuf_tensor("favor_" + name, shape, F32))
        sem = lambda name: k.semaphore(ctx, "favor_" + name)
        w = k.w
        outer = InputNorm(nc, ctx, k, "favor_outer", 1e-5)
        post = Norm(nc, ctx, k, "favor_post", 1e-6)
        xn, xnT, xin = sb("xn", [P, TILES, P]), sb("xnT", [P, 512]), sb("xin", [P, TILES, P])
        biases = sb("biases", [P, 2, 2])
        q, kk = sb("q", [P, 2, 512]), sb("k", [P, 2, 512])
        vals = sb("vals", [P, TILES * HEADS + 1, P])
        qf, kf = sb("qf", [P, TILES, 512]), sb("kf", [P, TILES, 512])
        qf_own = sb("qf_own", [P, HEADS, 512])
        kf_tok = sb("kf_tok", [P, TILES, 512])
        weights = sb("weights", [P, 2, TILES, 512])
        state, added = sb("state", [P, 2, TILES * P]), sb("added", [P, TILES, GROUP * VW])
        attn, inv_den = sb("attn", [P, 2, 512]), sb("inv_den", [P, 2, 512])
        res = sb("res", [P, TILES, P])
        dve_step, set_up, pool_set_up, xin_ready = sem("dve_step"), sem("set_up"), sem("pool_set_up"), sem("xin_ready")
        xnT_done, xnT_ready, qk_done, v_done, v_ready, qk_ready = (
            sem(n) for n in ("xnT_done", "xnT_ready", "qk_done", "v_done", "v_ready", "qk_ready"))
        feat_done, feat_ready, score_done, weight_ready, added_done, state_ready, sum_done, sum_ready = (
            sem(n) for n in ("feat_done", "feat_ready", "score_done", "weight_ready", "added_done", "state_ready", "sum_done", "sum_ready"))
        den_done, attn_ready, out_done, out_read, res_ready, own_ready = (
            sem(n) for n in ("den_done", "attn_ready", "out_done", "out_read", "res_ready", "own_ready"))
        p_sum, p_add, p_t = k.banks[0:2], k.banks[2], k.banks[3]
        p_feat = k.banks[4:8]
        p_qk, p_v = (p_add, p_t), p_add
        p_den, p_out = p_sum, p_sum[0]

        def by_tile(ap):
            return ap.rearrange("p (a e c) -> p a e c", a=2, c=GROUP * VW)[:, :, 0:4:3, :]

        with nc.Block() as block:
            @block.gpsimd
            def _(pool):
                nc.gpsimd.memset(vals[:, :, :], 0.0).then_inc(pool_set_up, 1)
                nc.gpsimd.memset(state[:, :, :], 0.0).then_inc(set_up, 1)
                pool.wait_ge(pool_set_up, 1)
                nc.gpsimd.memset(vals[:, 0:TILES * HEADS, P - VW + D:P - VW + D + 1], 1.0).then_inc(set_up, 1)
                k.await_parameters(pool, "favor")

                def own_features(s):
                    for t in range(TILES):
                        pool.wait_ge(feat_ready, s * UNITS + 2 * t + 1)
                        for r in range(2, GROUP):
                            nc.gpsimd.tensor_tensor(qf_own[:, t * GROUP + r, :], qf[:, t, :],
                                                    w("favor_own_rows")[:, r:r + 1].broadcast_to([P, 512]), ALU.mult).then_inc(own_ready, 1)

                own_features(0)
                with pool.Fori(0, SEQS - 1) as s:
                    own_features(s + 1)

            @block.vector
            def _(dve):
                k.await_parameters(dve, "favor")
                nc.vector.tensor_scalar(biases[:, 0, :], w("favor_q_b2"), SCALE, None, ALU.mult).then_inc(set_up, 1)
                nc.vector.tensor_scalar(biases[:, 1, :], w("favor_k_b2"), SCALE, None, ALU.mult).then_inc(set_up, 1)
                outer.statistics(dve, 0)
                dve.wait_ge(set_up, 4)

                def values(s):
                    dve.wait_ge(v_done, s + 1)
                    nc.vector.tensor_tensor(vals[:, 0:TILES * HEADS, P - VW:P - VW + D].rearrange("p (t h) d -> p t h d", h=HEADS),
                                            p_v[:, :].rearrange("p (t h d) -> p t h d", h=HEADS, d=D),
                                            w("favor_v_b").rearrange("p (h d) -> p h d", d=D).unsqueeze(1).broadcast_to([P, TILES, HEADS, D]),
                                            ALU.add).then_inc(v_ready, 1)

                def sequence(s, more):
                    step = Steps(dve, dve_step, s, 8)
                    for c in range(TILES):
                        if c >= 2:
                            dve.wait_ge(sum_done, s * TILES + c - 1)
                        for g in range(TILES):
                            dve.wait_ge(score_done, (s * TILES + c) * TILES + g + 1)
                            nc.vector.tensor_tensor(weights[:, c % 2, g, :].rearrange("p (r i) -> p r i", i=P),
                                                    p_feat[g][:, :].rearrange("p (r i) -> p r i", i=P),
                                                    w("causal").unsqueeze(1).broadcast_to([P, GROUP, P]), ALU.mult).then_inc(weight_ready, 1)
                        if c < TILES - 1:
                            dve.wait_ge(added_done, s * (TILES - 1) + c + 1)
                            own = w("favor_own").unsqueeze(1).broadcast_to([P, TILES, GROUP * VW])
                            add = p_add[:, 0:TILES * GROUP * VW].rearrange("p (g v) -> p g v", v=GROUP * VW)
                            step(nc.vector.tensor_tensor(added[:, :, :], add, own, ALU.mult))
                            rows = added[:, :, :].rearrange("p (a e) v -> p a e v", e=2)
                            if c == 0:
                                nc.vector.tensor_copy(by_tile(state[:, 1, :]), rows).then_inc(state_ready, 1)
                            else:
                                dve.wait_ge(state_ready, s * (TILES - 1) + c)
                                nc.vector.tensor_tensor(by_tile(state[:, (c + 1) % 2, :]), by_tile(state[:, c % 2, :]), rows, ALU.add).then_inc(state_ready, 1)
                        if c == 1 and more:
                            outer.scale(s + 1, lambda t: xn[:, t, :])
                    for n in range(2):
                        dve.wait_ge(den_done, s * 2 + n + 1)
                        step(nc.vector.reciprocal(inv_den[:, n, :], p_den[n][:, :]))
                        nc.vector.tensor_tensor(attn[:, n, :], attn[:, n, :], inv_den[:, n, :], ALU.mult).then_inc(attn_ready, 1)
                    if more:
                        values(s + 1)
                    outer.scale(s, lambda t: xin[:, t, :], signal=xin_ready)
                    dve.wait_ge(xin_ready, s + 1)
                    dve.wait_ge(out_done, s + 1)
                    step(nc.vector.tensor_tensor(res[:, :, :], p_out[:, :].rearrange("p (t d) -> p t d", d=P), xin[:, :, :], ALU.add))
                    nc.vector.tensor_tensor(res[:, :, :], res[:, :, :], w("favor_out_b").unsqueeze(1).broadcast_to([P, TILES, P]),
                                            ALU.add).then_inc(res_ready, 1)
                    carry_wait(nc, k.spare).then_inc(out_read, 1)
                    dve.wait_ge(res_ready, s + 1)
                    post.stats(dve, s, lambda t: res[:, t, :])
                    post.scale(dve, s, lambda t: res[:, t, :], lambda t: res[:, t, :])
                    dve.wait_ge(post.rows_ready, s + 1)
                    step(nc.vector.tensor_tensor(res[:, :, :], res[:, :, :], w("favor_gamma").unsqueeze(1).broadcast_to([P, TILES, P]), ALU.mult))
                    step(nc.vector.tensor_tensor(res[:, :, :], res[:, :, :], w("favor_beta").unsqueeze(1).broadcast_to([P, TILES, P]), ALU.add))
                    xs = k.x[:, bass.ds(s * TILES, TILES), :]
                    nc.vector.tensor_tensor(xs, xs, res[:, :, :], ALU.add)
                    step.end()

                outer.scale(0, lambda t: xn[:, t, :])
                outer.statistics(dve, 1)
                values(0)
                carry_wait(nc, k.spare).then_inc(out_read, 1)
                with dve.Fori(0, SEQS - 1) as s:
                    sequence(s, True)
                sequence(SEQS - 1, False)

            @block.scalar
            def _(act):
                k.await_parameters(act, "favor")
                nc.scalar.preload_act_table_set("natural_log_exp_and_others")
                outer.first_guesses(act, 0)
                act.wait_ge(set_up, 4)

                def turn_rows(s):
                    act.wait_ge(xnT_done, s + 1)
                    nc.scalar.copy(xnT[:, :], p_t[:, :]).then_inc(xnT_ready, 1)

                def queries_and_keys(s):
                    for n in range(4):
                        out, bank = (q, kk)[n // 2], p_qk[n % 2]
                        act.wait_ge(qk_done, s * 4 + n + 1)
                        for rows, func in ((slice(0, 64), ACT.Identity), (slice(64, P), ACT.Square)):
                            nc.scalar.activation(out[rows, n % 2, :], bank[rows, :], func, scale=SCALE,
                                                 bias=biases[rows, n // 2, n % 2:n % 2 + 1]).then_inc(qk_ready, 1)

                def features(s):
                    for n in range(UNITS):
                        act.wait_ge(feat_done, s * UNITS + n + 1)
                        bank = p_feat[n % 4][:, :]
                        exp = lambda out, bias: nc.scalar.activation(out, bank, ACT.Exp, bias=bias)
                        scaled = k.const(-0.5 * float(np.log(32.0)))
                        if n >= 2 * TILES:
                            last = exp(kf_tok[:, n - 2 * TILES, :], scaled)
                        elif n % 2 == 1:
                            last = exp(kf[:, n // 2, :], scaled)
                        else:
                            exp(qf[:, n // 2, :], scaled)
                            for r in range(2):
                                last = exp(qf_own[:, n // 2 * GROUP + r, :], w("favor_own_bias")[:, r:r + 1])
                        last.then_inc(feat_ready, 1)

                turn_rows(0)
                outer.first_guesses(act, 1)
                queries_and_keys(0)
                features(0)

                def sequence(s, more):
                    if more:
                        turn_rows(s + 1)
                    for n in range(2):
                        act.wait_ge(sum_done, (s + 1) * TILES)
                        nc.scalar.copy(attn[:, n, :], p_sum[n][:, :]).then_inc(sum_ready, 1)
                    if more:
                        queries_and_keys(s + 1)
                        features(s + 1)
                    post.first_guess(act, s)

                with act.Fori(0, SEQS - 1) as s:
                    sequence(s, True)
                sequence(SEQS - 1, False)

            @block.tensor
            def _(pe):
                k.await_parameters(pe, "favor")
                mm = nc.tensor.matmul
                pe.wait_ge(set_up, 4)

                def turn_rows(s):
                    pe.wait_ge(outer.rows_ready[0], s + 1)
                    transpose_tiles(nc, pe, p_t, lambda t: xn[:, t, :], w("ident")).then_inc(xnT_done, 1)

                def project_qk(s):
                    pe.wait_ge(xnT_ready, s + 1)
                    for n in range(4):
                        if n >= 2:
                            pe.wait_ge(qk_ready, s * 8 + (n - 1) * 2)
                        weight = w(("favor_q_w2", "favor_k_w2")[n // 2])[:, n % 2 * P:(n % 2 + 1) * P]
                        mm(p_qk[n % 2][:, :], weight, xnT[:, :], start=True, stop=True).then_inc(qk_done, 1)

                def project_v(s):
                    pe.wait_ge(qk_ready, s * 8 + 6)
                    for t in range(TILES):
                        last = mm(p_v[:, t * P:(t + 1) * P], xnT[:, t * P:(t + 1) * P], w("favor_v_w"), start=True, stop=True)
                    last.then_inc(v_done, 1)

                def features(s, first, last):
                    for n in range(first, last):
                        if n == 0:
                            pe.wait_ge(qk_ready, (s + 1) * 8)
                        if n >= 4:
                            pe.wait_ge(feat_ready, s * UNITS + n - 3)
                        bank = p_feat[n % 4]
                        t = n // 2 if n < 2 * TILES else n - 2 * TILES
                        if n < 2 * TILES:
                            ins = mm(bank[:, :], w("favor_map")[:, t % 2 * P:(t % 2 + 1) * P], (q, kk)[n % 2][:, t // 2, :], start=True, stop=True)
                        else:
                            for half in range(2):
                                ins = mm(bank[:, half * 256:(half + 1) * 256], kk[:, half, t * P:(t + 1) * P], w("favor_map"), start=True, stop=True)
                        ins.then_inc(feat_done, 1)

                def sequence(s, more):
                    flat = vals[:, :, :].rearrange("p n v -> p (n v)")

                    def scores(c):
                        tokens = slice(c * P, (c + 1) * P)
                        for g in range(TILES):
                            if c == 0:
                                pe.wait_ge(feat_ready, (s + 1) * UNITS)
                                pe.wait_ge(own_ready, (s * TILES + g + 1) * 2)
                            else:
                                pe.wait_ge(weight_ready, (s * TILES + c - 1) * TILES + g + 1)
                            mm(p_feat[g][:, :], kf[:, g, tokens], qf_own[:, g * GROUP:(g + 1) * GROUP, tokens],
                               start=True, stop=True).then_inc(score_done, 1)

                    def add_chunk(c):
                        if c == 0:
                            pe.wait_ge(v_ready, s + 1)
                        else:
                            pe.wait_ge(state_ready, s * (TILES - 1) + c)
                        for g in range(TILES):
                            n = c * HEADS + g * GROUP
                            last = mm(p_add[:, g * GROUP * VW:(g + 1) * GROUP * VW], kf_tok[:, c, g * P:(g + 1) * P],
                                      vals[:, n:n + GROUP, P - VW:P], start=True, stop=True)
                        last.then_inc(added_done, 1)

                    def sums(c):
                        tokens = slice(c * P, (c + 1) * P)
                        if c > 0:
                            pe.wait_ge(state_ready, s * (TILES - 1) + c)
                            for g in range(TILES):
                                mm(p_sum[g // 2][:, tokens], state[:, c % 2, g * P:(g + 1) * P], qf[:, g, tokens],
                                   start=False, stop=True, skip_group_check=True)
                        else:
                            pe.wait_ge(out_read, s + 1)
                        for h in range(HEADS):
                            g, r = h // GROUP, h % GROUP
                            if r == 0:
                                pe.wait_ge(weight_ready, (s * TILES + c) * TILES + g + 1)
                            at = (c * HEADS + h) * P + P - VW - h % PER * VW
                            first = c == 0 and h % PER == 0
                            last = mm(p_sum[h // PER][:, tokens], flat[:, at:at + P], weights[:, c % 2, g, r * P:(r + 1) * P],
                                      start=first, stop=first, skip_group_check=not first)
                        last.then_inc(sum_done, 1)

                    scores(0)
                    for c in range(TILES):
                        if c < TILES - 1:
                            add_chunk(c)
                            scores(c + 1)
                        elif more:
                            turn_rows(s + 1)
                        sums(c)
                    if more:
                        project_qk(s + 1)
                    for n in range(2):
                        pe.wait_ge(sum_ready, s * 2 + n + 1)
                        mm(p_den[n][:, :], w("favor_den"), attn[:, n, :], start=True, stop=True).then_inc(den_done, 1)
                    if more:
                        project_v(s + 1)
                        features(s + 1, 0, 5)
                    pe.wait_ge(attn_ready, (s + 1) * 2)
                    for t in range(TILES):
                        for n in range(2):
                            last = mm(p_out[:, t * P:(t + 1) * P], attn[:, n, t * P:(t + 1) * P], w("favor_out_rows")[:, n * P:(n + 1) * P],
                                      start=(n == 0), stop=(n == 1))
                    last.then_inc(out_done, 1)
                    if more:
                        features(s + 1, 5, UNITS)

                turn_rows(0)
                project_qk(0)
                project_v(0)
                features(0, 0, UNITS)
                with pe.Fori(0, SEQS - 1) as s:
                    sequence(s, True)
                sequence(SEQS - 1, False)


def taylor_stage(nc, k, n_stage):
    D = 64
    C = 32.0 ** -0.5
    PAIRS = HEADS // 2
    BUFFERS = 3
    UNITS = 1 + 4 + 2 * TILES
    BY_KEYS = [(0, 0), (1, 0), (2, 0), (1, 384)]
    USED, FLAT = (512, 512, 256), (0, 512, 1024)
    with ExitStack() as ctx:
        sb = lambda name, shape: ctx.enter_context(nc.sbuf_tensor("taylor_" + name, shape, F32))
        sem = lambda name: k.semaphore(ctx, "taylor_" + name)
        w = k.w
        outer = InputNorm(nc, ctx, k, "taylor_outer", 1e-5)
        xin, xinT = sb("xin", [P, TILES, P]), sb("xinT", [P, 512])
        qs, q_own, ks = sb("q", [P, 2, 512]), sb("q_own", [P, HEADS, 512]), sb("k", [P, 2, 512])
        vals = sb("vals", [P, TILES, HEADS, 2 * D])
        weights = sb("weights", [P, BUFFERS, 1280])
        den, y = sb("den", [P, 2, 512]), sb("y", [P, 2, 512])
        dve_step, set_up = sem("dve_step"), sem("set_up")
        unit_done, unit_taken, own_ready = sem("unit_done"), sem("unit_taken"), sem("own_ready")
        score_done, square_ready, weight_ready, sum_done, den_ready, y_ready, out_done, out_taken = (
            sem(n) for n in ("score_done", "square_ready", "weight_ready", "sum_done", "den_ready", "y_ready", "out_done", "out_taken"))
        p_score, p_sum, p_out = k.banks[0:3], k.banks[3:7], k.banks[7]
        p_unit = p_score
        low, high = slice(0, D), slice(D, 2 * D)

        def values_of(tile, half):
            pairs = vals[:, tile, half * 8:half * 8 + 8, :].rearrange("p (r e) (c d) -> p r (e c) d", e=2, c=2)
            return pairs[:, :, 0:4:3, :]

        with nc.Block() as block:
            @block.gpsimd
            def _(pool):
                nc.gpsimd.memset(vals[:, :, :, :], 1.0).then_inc(set_up, 1)

            @block.vector
            def _(dve):
                k.await_parameters(dve, "taylor")
                outer.statistics(dve, 0)

                def sequence(s, more):
                    step = Steps(dve, dve_step, s, PAIRS + 1)

                    def weigh(h):
                        for b in range(3):
                            dve.wait_ge(square_ready, (s * HEADS + h) * 3 + b + 1)
                            part = weights[:, h % BUFFERS, FLAT[b]:FLAT[b] + USED[b]]
                            nc.vector.scalar_tensor_tensor(part, part, 0.5, w("taylor_causal")[:, FLAT[b]:FLAT[b] + USED[b]], ALU.add,
                                                           ALU.mult).then_inc(weight_ready, 1)

                    def normalise(n):
                        if n >= 2:
                            dve.wait_ge(out_done, s * PAIRS + n - 1)
                        dve.wait_ge(den_ready, (s * PAIRS + n + 1) * 2)
                        step(nc.vector.reciprocal(den[:, n % 2, :], den[:, n % 2, :]))
                        for e, rows in enumerate((low, high)):
                            nc.vector.tensor_tensor(y[rows, n % 2, :], p_sum[(2 * n + e) % 4][rows, :], den[rows, n % 2, :],
                                                    ALU.mult).then_inc(y_ready, 1)

                    for h in range(HEADS):
                        weigh(h)
                        if h % 2 == 1 and h >= 3:
                            normalise(h // 2 - 1)
                        if h == HEADS // 2 and more:
                            outer.scale(s + 1, lambda t: xin[:, t, :])
                    normalise(PAIRS - 1)
                    dve.wait_ge(out_done, (s + 1) * PAIRS)
                    xs = k.x[:, bass.ds(s * TILES, TILES), :]
                    step(nc.vector.tensor_tensor(xs, xs, p_out[:, :].rearrange("p (t d) -> p t d", d=P), ALU.add))
                    carry_wait(nc, k.spare).then_inc(out_taken, 1)
                    step.end()

                outer.scale(0, lambda t: xin[:, t, :])
                outer.statistics(dve, 1)
                carry_wait(nc, k.spare).then_inc(out_taken, 1)
                with dve.Fori(0, SEQS - 1) as s:
                    sequence(s, True)
                sequence(SEQS - 1, False)

            @block.scalar
            def _(act):
                k.await_parameters(act, "taylor")
                nc.scalar.preload_act_table_set("natural_log_exp_and_others")
                outer.first_guesses(act, 0)
                act.wait_ge(set_up, 1)

                def take(s, first, last):
                    for n in range(first, last):
                        act.wait_ge(unit_done, s * UNITS + n + 1)
                        bank = p_unit[n % 3]
                        if n == 0:
                            ins = nc.scalar.copy(xinT[:, :], bank[:, :])
                        elif n <= 2:
                            ins = nc.scalar.copy(qs[:, n - 1, :], bank[:, :])
                        elif n <= 4:
                            ins = nc.scalar.copy(ks[:, n - 3, :], bank[:, :])
                        else:
                            ins = nc.scalar.copy(values_of((n - 5) // 2, (n - 5) % 2), bank[:, :].rearrange("p (r e d) -> p r e d", e=2, d=D))
                        ins.then_inc(unit_taken, 1)

                def own(s, h):
                    if h == 0:
                        act.wait_ge(unit_taken, s * UNITS + 3)
                    nc.scalar.activation(q_own[:, h, :], qs[:, h // 8, :], ACT.Identity, scale=w("taylor_own")[:, h % 8:h % 8 + 1],
                                         bias=k.const(0.0)).then_inc(own_ready, 1)

                def sequence(s, more):
                    def denominators(h):
                        n = h // 2
                        if n >= 2:
                            act.wait_ge(y_ready, (s * PAIRS + n - 1) * 2)
                        act.wait_ge(sum_done, s * HEADS + h + 1)
                        to, of = ((low, high), (high, low))[h % 2]
                        nc.scalar.activation(den[to, n % 2, :], p_sum[h % 4][of, :], ACT.Identity, bias=k.const(1e-12)[of, :]).then_inc(den_ready, 1)

                    for h in range(HEADS):
                        if h >= BUFFERS:
                            act.wait_ge(sum_done, s * HEADS + h - BUFFERS + 1)
                        for b in range(3):
                            act.wait_ge(score_done, (s * HEADS + h) * 3 + b + 1)
                            nc.scalar.activation(weights[:, h % BUFFERS, FLAT[b]:FLAT[b] + USED[b]], p_score[b][:, 0:USED[b]], ACT.Square,
                                                 bias=k.const(4.0 / 32.0 ** 0.5), scale=C).then_inc(square_ready, 1)
                        if h + 3 < HEADS:
                            own(s, h + 3)
                        if h >= 2:
                            denominators(h - 2)
                    if more:
                        take(s + 1, 0, 3)
                    denominators(HEADS - 2)
                    denominators(HEADS - 1)
                    if more:
                        take(s + 1, 3, 5)
                        for h in range(3):
                            own(s + 1, h)
                        take(s + 1, 5, UNITS)

                take(0, 0, 3)
                outer.first_guesses(act, 1)
                take(0, 3, 5)
                for h in range(3):
                    own(0, h)
                take(0, 5, UNITS)
                with act.Fori(0, SEQS - 1) as s:
                    sequence(s, True)
                sequence(SEQS - 1, False)

            @block.tensor
            def _(pe):
                k.await_parameters(pe, "taylor")
                mm = nc.tensor.matmul

                def fill(s, first, last):
                    for n in range(first, last):
                        bank = p_unit[n % 3]
                        if n >= 3:
                            pe.wait_ge(unit_taken, s * UNITS + n - 2)
                        if n == 0:
                            pe.wait_ge(outer.rows_ready[0], s + 1)
                            ins = transpose_tiles(nc, pe, bank, lambda t: xin[:, t, :], w("ident"))
                        elif n <= 4:
                            if n == 1:
                                pe.wait_ge(unit_taken, s * UNITS + 1)
                            weight = w(("taylor_wq", "taylor_wk")[(n - 1) // 2])[:, (n - 1) % 2 * P:((n - 1) % 2 + 1) * P]
                            ins = mm(bank[:, :], weight, xinT[:, :], start=True, stop=True)
                        else:
                            t, half = (n - 5) // 2, (n - 5) % 2
                            ins = mm(bank[:, :], xinT[:, t * P:(t + 1) * P], w("taylor_wv")[:, half * 512:(half + 1) * 512], start=True, stop=True)
                        ins.then_inc(unit_done, 1)

                def sequence(s, more):
                    def scores(h):
                        if h == 0:
                            pe.wait_ge(unit_taken, (s + 1) * UNITS)
                        pe.wait_ge(own_ready, s * HEADS + h + 1)
                        for b in range(3):
                            if h > 0:
                                pe.wait_ge(square_ready, (s * HEADS + h - 1) * 3 + b + 1)
                            for j in range(TILES):
                                if BY_KEYS[j][0] == b:
                                    c = BY_KEYS[j][1]
                                    last = mm(p_score[b][:, c:c + 512 - j * P], ks[:, h // 8, j * P:(j + 1) * P], q_own[:, h, j * P:512],
                                              start=True, stop=True)
                            last.then_inc(score_done, 1)

                    def sums(h):
                        if h >= 4:
                            pe.wait_ge(y_ready, (s * PAIRS + h // 2 - 1) * 2)
                        for j in range(TILES):
                            b, c = BY_KEYS[j]
                            pe.wait_ge(weight_ready, (s * HEADS + h) * 3 + b + 1)
                            last = mm(p_sum[h % 4][:, j * P:512], vals[:, j, h, :], weights[:, h % BUFFERS, FLAT[b] + c:FLAT[b] + c + 512 - j * P],
                                      start=(j == 0), stop=(j == 0), skip_group_check=(j > 0))
                        last.then_inc(sum_done, 1)

                    def output(n):
                        if n == 0:
                            pe.wait_ge(out_taken, s + 1)
                        pe.wait_ge(y_ready, (s * PAIRS + n + 1) * 2)
                        for t in range(TILES):
                            first = n == 0 and t == 0
                            last = mm(p_out[:, t * P:(t + 1) * P], y[:, n % 2, t * P:(t + 1) * P], w("taylor_wo")[:, n * P:(n + 1) * P],
                                      start=first, stop=first, skip_group_check=not first)
                        last.then_inc(out_done, 1)

                    scores(0)
                    scores(1)
                    for h in range(HEADS - 1):
                        if h + 2 < HEADS:
                            scores(h + 2)
                        sums(h)
                        if h >= 4 and h % 2 == 0:
                            output(h // 2 - 2)
                    if more:
                        pe.wait_ge(square_ready, (s + 1) * HEADS * 3)
                        fill(s + 1, 0, 3)
                    sums(HEADS - 1)
                    if more:
                        fill(s + 1, 3, 5)
                    output(PAIRS - 2)
                    if more:
                        fill(s + 1, 5, UNITS)
                    output(PAIRS - 1)

                fill(0, 0, UNITS)
                with pe.Fori(0, SEQS - 1) as s:
                    sequence(s, True)
                sequence(SEQS - 1, False)


def moe_stage(nc, k, n_stage):
    D, VW = 8, 16
    PER = P // VW
    PAIRS = HEADS // 2
    GROUP = 4
    SCALE = D ** -0.5
    EXPERTS, HIDDEN = 8, 384
    HT = HIDDEN // P
    BY_KEYS = [(0, 0), (1, 0), (2, 0), (1, 384)]
    BY_QUERIES = [(1, 384), (2, 0), (1, 0), (0, 0)]
    USED = (512, 512, 256)
    FLAT = (0, 512, 1024)
    with ExitStack() as ctx:
        sb = lambda name, shape, dt=F32: ctx.enter_context(nc.sbuf_tensor(f"moe{n_stage}_{name}", shape, dt))
        sem = lambda name: k.semaphore(ctx, f"moe{n_stage}_{name}")
        w = k.w
        outer = InputNorm(nc, ctx, k, f"moe{n_stage}_outer", 1e-5, 1e-6)
        second = Norm(nc, ctx, k, f"moe{n_stage}_second", 1e-6, rms=True)
        future, ident = sb("future", [P, P], BF16), sb("ident", [P, P], BF16)
        xin, xr, xrT = sb("xin", [P, TILES, P]), sb("xr", [P, TILES, P]), sb("xrT", [P, 512])
        hr, hrT = xr, xrT
        hrT_parts = sb("hrT_parts", [P, 2, 512], BF16)
        attn, qk = sb("attn", [P, 2, 512]), sb("qk", [P, 2, 512])
        q_parts, k_parts = sb("q_parts", [P, 3, 512], BF16), sb("k_parts", [P, 3, 512], BF16)
        q_stack, k_stack = sb("q_stack", [P, HEADS, 512], BF16), sb("k_stack", [P, PAIRS, 512], BF16)
        stacker = sb("stacker", [P, PAIRS, 6, P], BF16)
        pick = sb("pick", [P, GROUP * P], BF16)
        vals = sb("vals", [P, TILES * HEADS + 1, P])
        biggest, big_parts = sb("biggest", [P, TILES, HEADS]), sb("big_parts", [P, TILES, HEADS // GROUP, 2 * GROUP], BF16)
        turned_max = sb("turned_max", [P, 2, 512], BF16)
        weights = sb("weights", [P, 2, 1280])
        gate = weights[:, :, 0:512]
        acc = xin
        logits, top = sb("logits", [P, TILES, EXPERTS]), sb("top", [P, TILES, 8])
        index, index_f = sb("index", [P, TILES, 8], mybir.dt.uint32), sb("index_f", [P, TILES, 8])
        e_top, e_sum, combine, second_pick = sb("e_top", [P, TILES, 8]), sb("e_sum", [P, TILES]), sb("combine", [P, TILES, 8]), sb("second_pick", [P, TILES, 8])
        prod = sb("prod", [P, 2, HT, 512])
        inv_den, turned = prod[:, 0, 0:2, :], prod[:, 1, 0, :]
        dve_step, rotate_step, split_step, set_up, pool_set_up = (sem(n) for n in ("dve_step", "rotate_step", "split_step", "set_up", "pool_set_up"))
        xrT_done, xrT_ready, qk_done, rotated, part_ready, v_done, v_ready = (
            sem(n) for n in ("xrT_done", "xrT_ready", "qk_done", "rotated", "part_ready", "v_done", "v_ready"))
        high_ready, low_ready = sem("high_ready"), sem("low_ready")
        stack_done, q_stack_ready, k_stack_ready, split_ready = (sem(n) for n in ("stack_done", "q_stack_ready", "k_stack_ready", "split_ready"))
        row_done, row_read, max_done, max_ready, score_done, weight_ready, sum_done, sum_ready, den_done, attn_ready = (
            sem(n) for n in ("row_done", "row_read", "max_done", "max_ready", "score_done", "weight_ready", "sum_done", "sum_ready", "den_done", "attn_ready"))
        o_done, h_ready, hrT_done, hrT_ready, logits_done, top_ready, e_ready, combine_ready = (
            sem(n) for n in ("o_done", "h_ready", "hrT_done", "hrT_ready", "logits_done", "top_ready", "e_ready", "combine_ready"))
        gate_done, gate_ready, up_done, prod_ready, down_done, acc_ready = (
            sem(n) for n in ("gate_done", "gate_ready", "up_done", "prod_ready", "down_done", "acc_ready"))
        p_row, p_score, p_sum, p_t = k.banks[0:2], k.banks[2:5], k.banks[5:7], k.banks[7]
        p_den, p_logits = p_row, k.banks[6]
        p_q, p_q_rot, p_k, p_k_rot, p_v = k.banks[0], *k.banks[2:6]
        p_stack = k.banks[7], k.banks[6]
        p_gate, p_up, p_down = k.banks[0:2], k.banks[2:4], k.banks[4:6]

        with nc.Block() as block:
            @block.gpsimd
            def _(pool):
                nc.gpsimd.memset(vals[:, :, :], 0.0).then_inc(pool_set_up, 1)
                nc.gpsimd.memset(turned_max[:, :, :], 0.0).then_inc(set_up, 1)
                pool.wait_ge(pool_set_up, 1)
                nc.gpsimd.memset(vals[:, 0:TILES * HEADS, P - VW + D:P - VW + D + 1], 1.0).then_inc(set_up, 1)

            @block.vector
            def _(dve):
                k.await_parameters(dve, "moe")
                nc.vector.tensor_copy(pick[:, :].rearrange("p (r m) -> p r m", m=P), w("attn_pick").unsqueeze(2).broadcast_to([P, GROUP, P])).then_inc(set_up, 1)
                nc.vector.tensor_copy(future[:, :], w("future")).then_inc(set_up, 1)
                nc.vector.tensor_copy(ident[:, :], w("ident")).then_inc(set_up, 1)
                outer.statistics(dve, 0)

                def rotate(s, n):
                    step = Steps(dve, rotate_step, s * 2 + n, 2)
                    (plain, rot), out = ((p_q, p_q_rot), (p_k, p_k_rot))[n], qk[:, n, :]
                    dve.wait_ge(qk_done, s * 4 + 2 * n + 1)
                    step(nc.vector.tensor_tensor(out, plain[:, :], w("attn_cos"), ALU.mult))
                    dve.wait_ge(qk_done, s * 4 + 2 * n + 2)
                    step(nc.vector.tensor_tensor(turned, rot[:, :], w("attn_sin"), ALU.mult))
                    nc.vector.tensor_tensor(out, out, turned, ALU.add).then_inc(rotated, 1)
                    dve.wait_ge(rotated, s * 2 + n + 1)
                    step.end()

                def values(s):
                    dve.wait_ge(v_done, s + 1)
                    nc.vector.tensor_copy(vals[:, 0:TILES * HEADS, P - VW:P - VW + D],
                                          p_v[:, :].rearrange("p (n d) -> p n d", d=D)).then_inc(v_ready, 1)

                def split(s, n):
                    step = Steps(dve, split_step, s * 2 + n, 3)
                    rest, parts = qk[:, n, :], (q_parts, k_parts)[n]
                    step(nc.vector.tensor_copy(parts[:, 0, :], rest))
                    step(nc.vector.tensor_tensor(rest, rest, parts[:, 0, :], ALU.subtract))
                    step(nc.vector.tensor_copy(parts[:, 1, :], rest))
                    nc.vector.tensor_tensor(parts[:, 2, :], rest, parts[:, 1, :], ALU.subtract).then_inc(part_ready, 1)
                    step.end()

                def query_stacks(s, n):
                    dve.wait_ge(stack_done, (s * PAIRS + n) * 2 + 2)
                    for e in range(2):
                        nc.vector.tensor_scalar(q_stack[:, 2 * n + e, :], p_stack[1][:, :], w("attn_of_head")[:, e:e + 1],
                                                None, ALU.mult).then_inc(q_stack_ready, 1)

                def sequence(s, more):
                    step = Steps(dve, dve_step, s, HEADS // GROUP + 2 + 13)

                    def row_max(h):
                        for part in range(3):
                            n = h * 3 + part
                            dve.wait_ge(row_done, s * HEADS * 3 + n + 1)
                            for i in range(TILES):
                                if BY_QUERIES[i][0] == part:
                                    c = BY_QUERIES[i][1]
                                    last = nc.vector.reduce_max(biggest[:, i, h:h + 1], p_row[n % 2][:, c:c + (i + 1) * P], AX)
                            last.then_inc(row_read, 1)
                        if h % GROUP == GROUP - 1:
                            heads = slice(h - GROUP + 1, h + 1)
                            high, low = (big_parts[:, :, h // GROUP, n * GROUP:(n + 1) * GROUP] for n in range(2))
                            dve.wait_ge(row_read, (s * HEADS + h + 1) * 3)
                            step(nc.vector.tensor_copy(high, biggest[:, :, heads]))
                            nc.vector.tensor_tensor(low, biggest[:, :, heads], high, ALU.subtract).then_inc(split_ready, 1)

                    for h in range(HEADS):
                        row_max(h)
                    outer.scale(s, lambda t: xin[:, t, :])
                    if more:
                        outer.scale(s + 1, lambda t: xr[:, t, :], 1)
                    for n in range(2):
                        dve.wait_ge(den_done, s * 2 + n + 1)
                        step(nc.vector.reciprocal(inv_den[:, n, :], p_den[n][:, :]))
                        nc.vector.tensor_tensor(attn[:, n, :], attn[:, n, :], inv_den[:, n, :], ALU.mult).then_inc(attn_ready, 1)
                    if more:
                        rotate(s + 1, 0)
                    dve.wait_ge(o_done, s + 1)
                    dve.wait_ge(outer.rows_ready[0], s + 1)
                    nc.vector.tensor_tensor(acc[:, :, :], xin[:, :, :], p_t[:, :].rearrange("p (t d) -> p t d", d=P), ALU.add).then_inc(h_ready, 1)
                    dve.wait_ge(h_ready, s + 1)
                    second.stats(dve, s, lambda t: acc[:, t, :])
                    if more:
                        rotate(s + 1, 1)
                    second.scale(dve, s, lambda t: hr[:, t, :], lambda t: acc[:, t, :])
                    if more:
                        values(s + 1)
                    dve.wait_ge(hrT_ready, s + 1)
                    dve.wait_ge(high_ready, s + 1)
                    nc.vector.tensor_tensor(hrT_parts[:, 1, :], hrT[:, :], hrT_parts[:, 0, :], ALU.subtract).then_inc(low_ready, 1)
                    if more:
                        split(s + 1, 0)
                    dve.wait_ge(logits_done, s + 1)
                    step(nc.vector.tensor_copy(logits[:, :, :], p_logits[:, 0:TILES * EXPERTS].rearrange("p (t e) -> p t e", e=EXPERTS)))
                    carry_wait(nc, k.spare)
                    for t in range(TILES):
                        last = nc.vector.max(top[:, t, :], logits[:, t, :])
                    step(last)
                    carry_wait(nc, k.spare)
                    for t in range(TILES):
                        last = nc.vector.max_index(index[:, t, :], top[:, t, :], logits[:, t, :])
                    step(last)
                    step(nc.vector.tensor_copy(index_f[:, :, :], index[:, :, :]))
                    largest = top[:, :, 0:1].broadcast_to([P, TILES, 8])
                    nc.vector.tensor_tensor(e_top[:, :, :], top[:, :, :], largest, ALU.subtract).then_inc(top_ready, 1)
                    dve.wait_ge(e_ready, s + 1)
                    step(nc.vector.reduce_sum(e_sum[:, :], e_top[:, :, :], AX))
                    step(nc.vector.reciprocal(e_sum[:, :], e_sum[:, :]))
                    step(nc.vector.tensor_tensor(e_top[:, :, 0:2], e_top[:, :, 0:2], e_sum[:, :].unsqueeze(2).broadcast_to([P, TILES, 2]), ALU.mult))
                    step(nc.vector.tensor_tensor(e_sum[:, :], e_top[:, :, 0], e_top[:, :, 1], ALU.add))
                    step(nc.vector.reciprocal(e_sum[:, :], e_sum[:, :]))
                    step(nc.vector.tensor_tensor(e_top[:, :, 0:2], e_top[:, :, 0:2], e_sum[:, :].unsqueeze(2).broadcast_to([P, TILES, 2]), ALU.mult))
                    for n, out in enumerate((combine, second_pick)):
                        at = index_f[:, :, n:n + 1].broadcast_to([P, TILES, 8])
                        step(nc.vector.tensor_tensor(out[:, :, :], w("moe_index").unsqueeze(1).broadcast_to([P, TILES, 8]), at, ALU.is_equal))
                        last = nc.vector.tensor_tensor(out[:, :, :], out[:, :, :], e_top[:, :, n:n + 1].broadcast_to([P, TILES, 8]), ALU.mult)
                        last.then_inc(combine_ready, 1)
                    dve.wait_ge(combine_ready, s * 3 + 2)
                    nc.vector.tensor_tensor(combine[:, :, :], combine[:, :, :], second_pick[:, :, :], ALU.add).then_inc(combine_ready, 1)
                    dve.wait_ge(combine_ready, s * 3 + 3)

                    def product(e, m):
                        n = e * HT + m
                        if m == 0 and e >= 2:
                            dve.wait_ge(down_done, s * EXPERTS + e - 1)
                        dve.wait_ge(gate_ready, s * EXPERTS * HT + n + 1)
                        dve.wait_ge(up_done, s * EXPERTS * HT + n + 1)
                        nc.vector.tensor_tensor(prod[:, e % 2, m, :], p_up[n % 2][:, :], gate[:, n % 2, :], ALU.mult).then_inc(prod_ready, 1)

                    def add_expert(e):
                        dve.wait_ge(down_done, s * EXPERTS + e + 1)
                        if e > 0:
                            dve.wait_ge(acc_ready, s * EXPERTS + e)
                        for t in range(TILES):
                            last = nc.vector.scalar_tensor_tensor(acc[:, t, :], p_down[e % 2][:, t * P:(t + 1) * P], combine[:, t, e:e + 1],
                                                                  acc[:, t, :], ALU.mult, ALU.add)
                        last.then_inc(acc_ready, 1)

                    for e in range(EXPERTS):
                        for m in range(HT):
                            product(e, m)
                        if e == 0 and more:
                            split(s + 1, 1)
                        if e > 0:
                            add_expert(e - 1)
                            if more:
                                query_stacks(s + 1, e - 1)
                    add_expert(EXPERTS - 1)
                    if more:
                        query_stacks(s + 1, EXPERTS - 1)
                    dve.wait_ge(acc_ready, (s + 1) * EXPERTS)
                    xs = k.x[:, bass.ds(s * TILES, TILES), :]
                    step(nc.vector.tensor_tensor(xs, xs, acc[:, :, :], ALU.add))
                    step.end()

                outer.scale(0, lambda t: xr[:, t, :], 1)
                outer.statistics(dve, 1)
                rotate(0, 0)
                rotate(0, 1)
                values(0)
                split(0, 0)
                split(0, 1)
                for n in range(PAIRS):
                    query_stacks(0, n)
                with dve.Fori(0, SEQS - 1) as s:
                    sequence(s, True)
                sequence(SEQS - 1, False)

            @block.scalar
            def _(act):
                k.await_parameters(act, "moe")
                nc.scalar.preload_act_table_set("natural_log_exp_and_others")
                for n in range(PAIRS):
                    nc.scalar.activation(stacker[:, n, :, :], w("attn_stack").rearrange("p (j m) -> p j m", m=P), ACT.Identity,
                                         scale=w("attn_of_pair")[:, n:n + 1], bias=k.const(0.0)).then_inc(set_up, 1)
                outer.first_guesses(act, 0)

                def turn_rows(s):
                    act.wait_ge(xrT_done, s + 1)
                    nc.scalar.activation(xrT[:, :], p_t[:, :], ACT.Identity, scale=w("attn_g1"), bias=k.const(0.0)).then_inc(xrT_ready, 1)

                def key_stack(s, n):
                    act.wait_ge(stack_done, (s * PAIRS + n) * 2 + 1)
                    nc.scalar.copy(k_stack[:, n, :], p_stack[0][:, :]).then_inc(k_stack_ready, 1)

                def sequence(s, more):
                    nc.scalar.preload_act_table_set("natural_log_exp_and_others")

                    def turn(g):
                        act.wait_ge(max_done, s * GROUP + g + 1)
                        nc.scalar.copy(turned_max[0:2 * GROUP, g % 2, :], p_t[0:2 * GROUP, :]).then_inc(max_ready, 1)

                    def take_sums(n):
                        act.wait_ge(sum_done, s * HEADS + (n + 1) * PER)
                        nc.scalar.copy(attn[:, n, :], p_sum[n][:, :]).then_inc(sum_ready, 1)

                    turn(0)
                    for h in range(HEADS):
                        if h >= 2:
                            act.wait_ge(sum_done, s * HEADS + h - 1)
                        for bank in range(3):
                            act.wait_ge(score_done, (s * HEADS + h) * 3 + bank + 1)
                            nc.scalar.activation(weights[:, h % 2, FLAT[bank]:FLAT[bank] + USED[bank]], p_score[bank][:, 0:USED[bank]],
                                                 ACT.Exp, scale=SCALE).then_inc(weight_ready, 1)
                        if h % GROUP == GROUP - 1 and h + 1 < HEADS:
                            turn(h // GROUP + 1)
                        if h == PER + 1:
                            take_sums(0)
                    if more:
                        turn_rows(s + 1)
                    take_sums(1)
                    second.first_guess(act, s)
                    act.wait_ge(hrT_done, s + 1)
                    nc.scalar.activation(hrT[:, :], p_t[:, :], ACT.Identity, scale=w("attn_g2"), bias=k.const(0.0)).then_inc(hrT_ready, 1)
                    nc.scalar.activation(hrT_parts[:, 0, :], p_t[:, :], ACT.Identity, scale=w("attn_g2"), bias=k.const(0.0)).then_inc(high_ready, 1)
                    act.wait_ge(top_ready, s + 1)
                    nc.scalar.activation(e_top[:, :, :], e_top[:, :, :], ACT.Exp).then_inc(e_ready, 1)
                    for n in range(EXPERTS * HT):
                        act.wait_ge(gate_done, s * EXPERTS * HT + n + 1)
                        if n >= 2:
                            act.wait_ge(prod_ready, s * EXPERTS * HT + n - 1)
                        nc.scalar.activation(gate[:, n % 2, :], p_gate[n % 2][:, :], ACT.Silu).then_inc(gate_ready, 1)
                        if more and n % HT == HT - 1 and n >= HT:
                            key_stack(s + 1, n // HT - 1)
                    if more:
                        key_stack(s + 1, EXPERTS - 1)

                turn_rows(0)
                outer.first_guesses(act, 1)
                for n in range(PAIRS):
                    key_stack(0, n)
                with act.Fori(0, SEQS - 1) as s:
                    sequence(s, True)
                sequence(SEQS - 1, False)

            @block.tensor
            def _(pe):
                k.await_parameters(pe, "moe")
                mm = nc.tensor.matmul
                pe.wait_ge(set_up, 5 + PAIRS)

                def turn_rows(s):
                    pe.wait_ge(outer.rows_ready[1], s + 1)
                    transpose_tiles(nc, pe, p_t, lambda t: xr[:, t, :], w("ident")).then_inc(xrT_done, 1)

                def project(s):
                    pe.wait_ge(xrT_ready, s + 1)
                    for bank, name in ((p_q, "attn_wq"), (p_q_rot, "attn_wq_rot"), (p_k, "attn_wk"), (p_k_rot, "attn_wk_rot")):
                        mm(bank[:, :], w(name), xrT[:, :], start=True, stop=True).then_inc(qk_done, 1)
                    for t in range(TILES):
                        last = mm(p_v[:, t * P:(t + 1) * P], xrT[:, t * P:(t + 1) * P], w("attn_wv"), start=True, stop=True)
                    last.then_inc(v_done, 1)

                def stacks(s, n):
                    if n == 0:
                        pe.wait_ge(part_ready, s * 2 + 2)
                    else:
                        pe.wait_ge(k_stack_ready, s * PAIRS + n)
                        pe.wait_ge(q_stack_ready, s * HEADS + 2 * n)
                    for parts, bank, j0 in ((k_parts, p_stack[0], 0), (q_parts, p_stack[1], 3)):
                        for j in range(3):
                            last = mm(bank[:, :], stacker[:, n, j0 + j, :], parts[:, j, :], start=(j == 0), stop=(j == 2))
                        last.then_inc(stack_done, 1)

                def sequence(s, more):
                    def query_rows(h, parts=range(3)):
                        if h == 0:
                            pe.wait_ge(q_stack_ready, (s + 1) * HEADS)
                            pe.wait_ge(k_stack_ready, (s + 1) * PAIRS)
                        for part in parts:
                            n = h * 3 + part
                            if n >= 2:
                                pe.wait_ge(row_read, s * HEADS * 3 + n - 1)
                            for i in range(TILES):
                                if BY_QUERIES[i][0] == part:
                                    c = BY_QUERIES[i][1]
                                    mm(p_row[n % 2][:, c + i * P:c + (i + 1) * P], future[:, :], ident[:, :],
                                       start=True, stop=True)
                                    last = mm(p_row[n % 2][:, c:c + (i + 1) * P], q_stack[:, h, i * P:(i + 1) * P],
                                              k_stack[:, h // 2, 0:(i + 1) * P], start=False, stop=True, skip_group_check=True)
                            last.then_inc(row_done, 1)

                    def turn_max(g):
                        pe.wait_ge(split_ready, s * GROUP + g + 1)
                        if g > 0:
                            pe.wait_ge(max_ready, s * GROUP + g)
                        for t in range(TILES):
                            last = mm(p_t[0:2 * GROUP, t * P:(t + 1) * P], big_parts[:, t, g, :], ident[:, :],
                                      start=True, stop=True)
                        last.then_inc(max_done, 1)

                    def key_rows(h):
                        g, r = h // GROUP, h % GROUP
                        if r == 0:
                            pe.wait_ge(max_ready, s * GROUP + g + 1)
                        for bank in range(3):
                            if h > 0:
                                pe.wait_ge(weight_ready, (s * HEADS + h - 1) * 3 + bank + 1)
                            for i in range(TILES):
                                if BY_KEYS[i][0] == bank:
                                    c, n = BY_KEYS[i][1], 512 - i * P
                                    out = p_score[bank][:, c:c + n]
                                    mm(p_score[bank][:, c:c + P], ident[:, :], future[:, :], start=True, stop=True)
                                    mm(out, pick[:, r * P:(r + 1) * P], turned_max[:, g % 2, i * P:512], start=False, stop=False,
                                       skip_group_check=True)
                                    last = mm(out, k_stack[:, h // 2, i * P:(i + 1) * P], q_stack[:, h, i * P:512], start=False, stop=True,
                                              skip_group_check=True)
                            last.then_inc(score_done, 1)

                    def sums(h):
                        flat = vals[:, :, :].rearrange("p n v -> p (n v)")
                        for j in range(TILES):
                            bank, c = BY_KEYS[j]
                            pe.wait_ge(weight_ready, (s * HEADS + h) * 3 + (bank + 1 if j != 3 else 2))
                            at = (j * HEADS + h) * P + P - VW - h % PER * VW
                            last = mm(p_sum[h // PER][:, j * P:512], flat[:, at:at + P], weights[:, h % 2, FLAT[bank] + c:FLAT[bank] + c + 512 - j * P],
                                      start=(h % PER == 0 and j == 0), stop=(h % PER == 0 and j == 0),
                                      skip_group_check=not (h % PER == 0 and j == 0))
                        last.then_inc(sum_done, 1)

                    def denominators(n):
                        pe.wait_ge(sum_ready, s * 2 + n + 1)
                        mm(p_den[n][:, :], w("attn_den"), attn[:, n, :], start=True, stop=True).then_inc(den_done, 1)

                    for h in range(GROUP):
                        query_rows(h)
                    turn_max(0)
                    for h in range(HEADS):
                        if h + GROUP < HEADS:
                            query_rows(h + GROUP, (0, 1))
                        key_rows(h)
                        if h + GROUP < HEADS:
                            query_rows(h + GROUP, (2,))
                        if h > 0:
                            sums(h - 1)
                        if h % GROUP == GROUP - 1 and h + 1 < HEADS:
                            turn_max(h // GROUP + 1)
                        if h == HEADS - 2:
                            pe.wait_ge(row_read, (s + 1) * HEADS * 3)
                            denominators(0)
                            if more:
                                turn_rows(s + 1)
                    sums(HEADS - 1)
                    denominators(1)
                    if more:
                        pe.wait_ge(attn_ready, s * 2 + 1)
                        project(s + 1)
                    pe.wait_ge(attn_ready, (s + 1) * 2)
                    for t in range(TILES):
                        for n in range(2):
                            last = mm(p_t[:, t * P:(t + 1) * P], attn[:, n, t * P:(t + 1) * P], w("attn_wo_rows")[:, n * P:(n + 1) * P],
                                      start=(n == 0), stop=(n == 1))
                    last.then_inc(o_done, 1)
                    pe.wait_ge(second.rows_ready, s + 1)
                    transpose_tiles(nc, pe, p_t, lambda t: hr[:, t, :], w("ident")).then_inc(hrT_done, 1)
                    pe.wait_ge(hrT_ready, s + 1)
                    for t in range(TILES):
                        last = mm(p_logits[:, t * EXPERTS:(t + 1) * EXPERTS], hrT[:, t * P:(t + 1) * P], w("moe_router"), start=True, stop=True)
                    last.then_inc(logits_done, 1)

                    if more:
                        pe.wait_ge(rotated, (s + 2) * 2)

                    def up_product(bank, at):
                        weight = k.expert_parts[:, :, at:at + P]
                        mm(bank, weight[:, 0, :], hrT_parts[:, 0, :], start=True, stop=False)
                        mm(bank, weight[:, 1, :], hrT_parts[:, 0, :], start=False, stop=False)
                        return mm(bank, weight[:, 0, :], hrT_parts[:, 1, :], start=False, stop=True)

                    def up(e):
                        for m in range(HT):
                            n = e * HT + m
                            if n >= 2:
                                pe.wait_ge(gate_ready, s * EXPERTS * HT + n - 1)
                            up_product(p_gate[n % 2][:, :], n * P).then_inc(gate_done, 1)
                            if n >= 2:
                                pe.wait_ge(prod_ready, s * EXPERTS * HT + n - 1)
                            up_product(p_up[n % 2][:, :], (EXPERTS * HT + n) * P).then_inc(up_done, 1)

                    def down(e):
                        pe.wait_ge(prod_ready, s * EXPERTS * HT + (e + 1) * HT)
                        if e >= 2:
                            pe.wait_ge(acc_ready, s * EXPERTS + e - 1)
                        for t in range(TILES):
                            for m in range(HT):
                                n = e * HT + m
                                last = mm(p_down[e % 2][:, t * P:(t + 1) * P], prod[:, e % 2, m, t * P:(t + 1) * P],
                                          w("moe_wd")[:, n * P:(n + 1) * P], start=(m == 0), stop=(m == HT - 1))
                        last.then_inc(down_done, 1)

                    pe.wait_ge(low_ready, s + 1)
                    up(0)
                    for e in range(EXPERTS):
                        if e + 1 < EXPERTS:
                            up(e + 1)
                        if e == 1 and more:
                            pe.wait_ge(v_ready, s + 2)
                        down(e)
                        if more:
                            if e == 0:
                                pe.wait_ge(top_ready, s + 1)
                            stacks(s + 1, e)

                turn_rows(0)
                project(0)
                for n in range(PAIRS):
                    stacks(0, n)
                with pe.Fori(0, SEQS - 1) as s:
                    sequence(s, True)
                sequence(SEQS - 1, False)


def ssd_stage(nc, k, n_stage):
    H, HD, INNER = 4, 64, 256
    LOG1P = log1p_series()
    with ExitStack() as ctx:
        sb = lambda name, shape: ctx.enter_context(nc.sbuf_tensor("ssd_" + name, shape, F32))
        sem = lambda name: k.semaphore(ctx, "ssd_" + name)
        w = k.w
        outer = InputNorm(nc, ctx, k, "ssd_outer", 1e-5, 1e-5)
        gnorm = Norm(nc, ctx, k, "ssd_gnorm", 1e-5, rms=True)
        xin, xn, xnT = sb("xin", [P, TILES, P]), sb("xn", [P, TILES, P]), sb("xnT", [P, 512])
        padded, conv, chan = sb("padded", [P, 4, 515]), sb("conv", [P, 4, 512]), sb("chan", [P, 4, 512])
        zs = sb("zs", [P, TILES, INNER])
        a_rate = sb("a_rate", [P, H])
        raw, u, dt, da = (sb(n, [P, TILES, H]) for n in ("raw", "u", "dt", "da"))
        tok = sb("tok", [P, 2, 384])
        decays = sb("decays", [P, 2, 3 * H])
        after_da, seg = sb("after_da", [P, 2, H, P]), sb("seg", [P, 2, H, P])
        cb, mix = sb("cb", [P, 2, P]), sb("mix", [P, 2, H, P])
        xdt, xdecay = sb("xdt", [P, 2, H, HD]), sb("xdecay", [P, 2, H, HD])
        state, faded = sb("state", [P, 2, H, HD]), sb("faded", [P, H, HD])
        y, skip, yn, ynT = sb("y", [P, TILES, INNER]), sb("skip", [P, 2, INNER]), sb("yn", [P, TILES, INNER]), sb("ynT", [P, 2, 512])
        dve_step, conv_step, dt_step, act_step, set_up = (sem(n) for n in ("dve_step", "conv_step", "dt_step", "act_step", "set_up"))
        xnT_done, xnT_ready, chan_done, padded_ready, conv_ready, chan_ready, z_done, zs_ready, dt_done, raw_ready, u_ready, da_ready = (
            sem(n) for n in ("xnT_done", "xnT_ready", "chan_done", "padded_ready", "conv_ready", "chan_ready", "z_done", "zs_ready",
                             "dt_done", "raw_ready", "u_ready", "da_ready"))
        tok_done, tok_ready, sums_done, decays_ready, after_ready, seg_done, seg_ready, cb_done, mix_ready, xdt_ready, xdecay_ready = (
            sem(n) for n in ("tok_done", "tok_ready", "sums_done", "decays_ready", "after_ready", "seg_done", "seg_ready", "cb_done",
                             "mix_ready", "xdt_ready", "xdecay_ready"))
        off_done, add_done, diag_done, state_ready, y_ready, ynT_done, ynT_ready, out_done, out_taken, xin_ready = (
            sem(n) for n in ("off_done", "add_done", "diag_done", "state_ready", "y_ready", "ynT_done", "ynT_ready", "out_done", "out_taken", "xin_ready"))
        p_t, p_seg, p_cb, p_diag, p_off, p_add, p_z, p_small = k.banks
        p_xn, p_chan, p_dt, p_zs = p_z, p_z, p_cb, (p_add, p_z)
        p_yn, p_out = (p_t, p_seg), p_diag

        with nc.Block() as block:
            @block.vector
            def _(dve):
                k.await_parameters(dve, "ssd")
                nc.vector.memset(padded[:, :, 0:3], 0.0).then_inc(set_up, 1)
                outer.statistics(dve, 0)

                def steps_of_time(s):
                    step = Steps(dve, dt_step, s, 11)
                    dve.wait_ge(dt_done, s + 1)
                    nc.vector.tensor_tensor(raw[:, :, :], p_dt[:, 0:TILES * H].rearrange("p (t h) -> p t h", h=H),
                                            w("ssd_dt_bias").unsqueeze(1).broadcast_to([P, TILES, H]), ALU.add).then_inc(raw_ready, 1)
                    dve.wait_ge(u_ready, s + 1)
                    step(nc.vector.tensor_scalar(dt[:, :, :], u[:, :, :], LOG1P[9], None, ALU.mult))
                    for n in range(8, -1, -1):
                        step(nc.vector.scalar_tensor_tensor(dt[:, :, :], dt[:, :, :], LOG1P[n], u[:, :, :], ALU.add, ALU.mult))
                    step(nc.vector.scalar_tensor_tensor(dt[:, :, :], raw[:, :, :], 0.0, dt[:, :, :], ALU.max, ALU.add))
                    nc.vector.scalar_tensor_tensor(da[:, :, :], dt[:, :, :], -1.0, a_rate[:, :].unsqueeze(1).broadcast_to([P, TILES, H]),
                                                   ALU.mult, ALU.mult).then_inc(da_ready, 1)
                    step.end()

                def convolve(s, m):
                    step = Steps(dve, conv_step, s * 4 + m, 2)
                    dve.wait_ge(padded_ready, s * 4 + m + 1)
                    cw = w("ssd_conv_w")
                    for tap in range(3):
                        last = nc.vector.scalar_tensor_tensor(conv[:, m, :], padded[:, m, tap:tap + 512], cw[:, 4 * m + tap:4 * m + tap + 1],
                                                              conv[:, m, :], ALU.mult, ALU.add)
                        if tap < 2:
                            step(last)
                    last.then_inc(conv_ready, 1)
                    step.end()

                def sequence(s, more):
                    step = Steps(dve, dve_step, s, 22)
                    outer.scale(s, lambda t: xin[:, t, :], signal=xin_ready)
                    if more:
                        outer.scale(s + 1, lambda t: xn[:, t, :], 1)
                    per_head = lambda ap, n: ap.unsqueeze(2).broadcast_to([P, H, n])

                    def front(c):
                        b = c % 2
                        if c == 0:
                            dve.wait_ge(da_ready, s + 1)
                        for h in range(H):
                            last = nc.vector.tensor_scalar(after_da[:, b, h, :], w("after"), da[:, c, h:h + 1], None, ALU.mult)
                        last.then_inc(after_ready, 1)
                        dve.wait_ge(tok_ready, s * TILES + c + 1)
                        inputs = tok[:, b, 0:INNER].rearrange("p (h d) -> p h d", d=HD)
                        nc.vector.tensor_tensor(xdt[:, b, :, :], inputs, per_head(dt[:, c, :], HD), ALU.mult).then_inc(xdt_ready, 1)
                        step(nc.vector.tensor_tensor(skip[:, b, :], tok[:, b, 0:INNER], w("ssd_d"), ALU.mult))
                        dve.wait_ge(decays_ready, s * TILES + c + 1)
                        dve.wait_ge(xdt_ready, s * TILES + c + 1)
                        nc.vector.tensor_tensor(xdecay[:, b, :, :], xdt[:, b, :, :], per_head(decays[:, b, H:2 * H], HD), ALU.mult).then_inc(xdecay_ready, 1)
                        dve.wait_ge(cb_done, s * TILES + c + 1)
                        step(nc.vector.tensor_tensor(cb[:, b, :], p_cb[:, 0:P], w("causal"), ALU.mult))
                        dve.wait_ge(seg_ready, s * TILES + c + 1)
                        nc.vector.tensor_tensor(mix[:, b, :, :], seg[:, b, :, :], cb[:, b, :].unsqueeze(1).broadcast_to([P, H, P]), ALU.mult).then_inc(mix_ready, 1)

                    def back(c):
                        b = c % 2
                        add = p_add[:, 0:INNER].rearrange("p (h d) -> p h d", d=HD)
                        if c < TILES - 1:
                            dve.wait_ge(add_done, s * (TILES - 1) + c + 1)
                            if c == 0:
                                nc.vector.tensor_copy(state[:, 1, :, :], add).then_inc(state_ready, 1)
                            else:
                                step(nc.vector.tensor_tensor(faded[:, :, :], state[:, b, :, :], per_head(decays[:, b, 2 * H:3 * H], HD), ALU.mult))
                                nc.vector.tensor_tensor(state[:, 1 - b, :, :], faded[:, :, :], add, ALU.add).then_inc(state_ready, 1)
                        yc = y[:, c, :]
                        yh = yc.rearrange("p (h d) -> p h d", d=HD)
                        if c > 0:
                            dve.wait_ge(off_done, s * (TILES - 1) + c)
                            off = p_off[:, 0:INNER].rearrange("p (h d) -> p h d", d=HD)
                            step(nc.vector.tensor_tensor(yh, off, per_head(decays[:, b, 0:H], HD), ALU.mult))
                            step(nc.vector.tensor_tensor(skip[:, b, :], skip[:, b, :], yc, ALU.add))
                        dve.wait_ge(diag_done, s * TILES + c + 1)
                        step(nc.vector.tensor_tensor(skip[:, b, :], p_diag[:, 0:INNER], skip[:, b, :], ALU.add))
                        dve.wait_ge(zs_ready, (s + 1) * 2)
                        nc.vector.tensor_tensor(yc, skip[:, b, :], zs[:, c, :], ALU.mult).then_inc(y_ready, 1)
                        if c < TILES - 1:
                            dve.wait_ge(state_ready, s * (TILES - 1) + c + 1)
                        dve.wait_ge(y_ready, s * TILES + c + 1)

                    front(0)
                    for c in range(TILES):
                        if c + 1 < TILES:
                            front(c + 1)
                        back(c)
                        if more:
                            convolve(s + 1, c)
                    gnorm.stats(dve, s, lambda t: y[:, t, :])
                    gnorm.scale(dve, s, lambda t: yn[:, t, :], lambda t: y[:, t, :])
                    if more:
                        steps_of_time(s + 1)
                    xs = k.x[:, bass.ds(s * TILES, TILES), :]
                    dve.wait_ge(xin_ready, s + 1)
                    step(nc.vector.tensor_tensor(xs, xs, xin[:, :, :], ALU.add))
                    dve.wait_ge(out_done, s + 1)
                    step(nc.vector.tensor_tensor(xs, xs, p_out[:, :].rearrange("p (t d) -> p t d", d=P), ALU.add))
                    carry_wait(nc, k.spare).then_inc(out_taken, 1)
                    step.end()

                outer.scale(0, lambda t: xn[:, t, :], 1)
                outer.statistics(dve, 1)
                for m in range(4):
                    convolve(0, m)
                steps_of_time(0)
                carry_wait(nc, k.spare).then_inc(out_taken, 1)
                with dve.Fori(0, SEQS - 1) as s:
                    sequence(s, True)
                sequence(SEQS - 1, False)

            @block.scalar
            def _(act):
                k.await_parameters(act, "ssd")
                nc.scalar.preload_act_table_set("natural_log_exp_and_others")
                act.wait_ge(set_up, 1)
                nc.scalar.activation(a_rate[:, :], w("ssd_a_log"), ACT.Exp).then_inc(set_up, 1)
                act.wait_ge(set_up, 2)
                outer.first_guesses(act, 0)

                def turn_rows(s):
                    act.wait_ge(xnT_done, s + 1)
                    nc.scalar.activation(xnT[:, :], p_xn[:, :], ACT.Identity, scale=w("ssd_norm_w"), bias=k.const(0.0)).then_inc(xnT_ready, 1)

                def channels(s, m):
                    act.wait_ge(chan_done, s * 4 + m + 1)
                    nc.scalar.copy(padded[:, m, 3:515], p_chan[:, :])
                    nc.scalar.activation(conv[:, m, :], p_chan[:, :], ACT.Identity, scale=w("ssd_conv_w")[:, 4 * m + 3:4 * m + 4],
                                         bias=w("ssd_conv_b")[:, m:m + 1]).then_inc(padded_ready, 1)

                def exp_of_time(s):
                    step = Steps(act, act_step, s, 1)
                    act.wait_ge(raw_ready, s + 1)
                    step(nc.scalar.activation(u[:, :, :], raw[:, :, :], ACT.Abs))
                    nc.scalar.activation(u[:, :, :], u[:, :, :], ACT.Exp, scale=-1.0).then_inc(u_ready, 1)
                    step.end()

                def silu_channels(s):
                    for m in range(4):
                        act.wait_ge(conv_ready, s * 4 + m + 1)
                        nc.scalar.activation(chan[:, m, :], conv[:, m, :], ACT.Silu).then_inc(chan_ready, 1)

                def silu_gates(s):
                    for n in range(2):
                        act.wait_ge(z_done, s * 2 + n + 1)
                        nc.scalar.activation(zs[:, 2 * n:2 * n + 2, :], p_zs[n][:, :].rearrange("p (t d) -> p t d", d=INNER), ACT.Silu).then_inc(zs_ready, 1)

                def sequence(s, more):
                    nc.scalar.preload_act_table_set("natural_log_exp_and_others")
                    if more:
                        turn_rows(s + 1)
                    for c in range(TILES):
                        b = c % 2
                        if c >= 2:
                            act.wait_ge(y_ready, s * TILES + c - 1)
                        act.wait_ge(tok_done, s * TILES + c + 1)
                        nc.scalar.copy(tok[:, b, :], p_t[:, 0:384]).then_inc(tok_ready, 1)
                        act.wait_ge(sums_done, s * TILES + c + 1)
                        nc.scalar.activation(decays[:, b, :], p_small[:, 0:3 * H], ACT.Exp).then_inc(decays_ready, 1)
                        act.wait_ge(seg_done, s * TILES + c + 1)
                        nc.scalar.activation(seg[:, b, :, :], p_seg[:, :].rearrange("p (h i) -> p h i", i=P), ACT.Exp).then_inc(seg_ready, 1)
                        if more and c > 0:
                            channels(s + 1, c - 1)
                    if more:
                        channels(s + 1, TILES - 1)
                    gnorm.first_guess(act, s)
                    if more:
                        exp_of_time(s + 1)
                    for n in range(2):
                        act.wait_ge(ynT_done, s * 2 + n + 1)
                        nc.scalar.activation(ynT[:, n, :], p_yn[n][:, :], ACT.Identity, scale=w("ssd_gnorm_w")[:, n:n + 1],
                                             bias=k.const(0.0)).then_inc(ynT_ready, 1)
                    if more:
                        act.wait_ge(y_ready, (s + 1) * TILES)
                        silu_channels(s + 1)
                        silu_gates(s + 1)

                turn_rows(0)
                outer.first_guesses(act, 1)
                for m in range(4):
                    channels(0, m)
                exp_of_time(0)
                silu_channels(0)
                silu_gates(0)
                with act.Fori(0, SEQS - 1) as s:
                    sequence(s, True)
                sequence(SEQS - 1, False)

            @block.tensor
            def _(pe):
                k.await_parameters(pe, "ssd")
                mm = nc.tensor.matmul

                def turn_rows(s):
                    pe.wait_ge(outer.rows_ready[1], s + 1)
                    transpose_tiles(nc, pe, p_xn, lambda t: xn[:, t, :], w("ident")).then_inc(xnT_done, 1)

                def channels(s, m):
                    if m == 0:
                        pe.wait_ge(xnT_ready, s + 1)
                    else:
                        pe.wait_ge(padded_ready, s * 4 + m)
                    mm(p_chan[:, :], w("ssd_wx")[:, m * P:(m + 1) * P], xnT[:, :], start=True, stop=True).then_inc(chan_done, 1)

                def times_and_gates(s):
                    for t in range(TILES):
                        last = mm(p_dt[:, t * H:(t + 1) * H], xnT[:, t * P:(t + 1) * P], w("ssd_wdt"), start=True, stop=True)
                    last.then_inc(dt_done, 1)
                    pe.wait_ge(padded_ready, (s + 1) * 4)
                    for n in range(2):
                        for t in (2 * n, 2 * n + 1):
                            last = mm(p_zs[n][:, t % 2 * INNER:(t % 2 + 1) * INNER], xnT[:, t * P:(t + 1) * P], w("ssd_wz"), start=True, stop=True)
                        last.then_inc(z_done, 1)

                def sequence(s, more):
                    if more:
                        pe.wait_ge(zs_ready, (s + 1) * 2)
                        turn_rows(s + 1)
                    def front(c):
                        tokens = slice(c * P, (c + 1) * P)
                        if c == 0:
                            pe.wait_ge(da_ready, s + 1)
                        else:
                            pe.wait_ge(decays_ready, s * TILES + c)
                        for n, name in enumerate(("causal", "after", "ones")):
                            last = mm(p_small[:, n * H:(n + 1) * H], w(name), da[:, c, :], start=True, stop=True)
                        last.then_inc(sums_done, 1)
                        if c == 0:
                            pe.wait_ge(chan_ready, (s + 1) * 4)
                        else:
                            pe.wait_ge(tok_ready, s * TILES + c)
                        for m in range(3):
                            last = nc.tensor.transpose(p_t[:, m * P:(m + 1) * P], chan[:, m, tokens], w("ident"))
                        last.then_inc(tok_done, 1)
                        if c > 0:
                            pe.wait_ge(mix_ready, s * TILES + c)
                        mm(p_cb[:, 0:P], chan[:, 2, tokens], chan[:, 3, tokens], start=True, stop=True).then_inc(cb_done, 1)
                        pe.wait_ge(after_ready, s * TILES + c + 1)
                        if c > 0:
                            pe.wait_ge(seg_ready, s * TILES + c)
                        for h in range(H):
                            last = mm(p_seg[:, h * P:(h + 1) * P], after_da[:, c % 2, h, :], w("causal"), start=True, stop=True)
                        last.then_inc(seg_done, 1)

                    def back(c):
                        tokens = slice(c * P, (c + 1) * P)
                        if c > 0:
                            pe.wait_ge(state_ready, s * (TILES - 1) + c)
                            pe.wait_ge(y_ready, s * TILES + c)
                            mm(p_off[:, 0:INNER], chan[:, 3, tokens], state[:, c % 2, :, :], start=True, stop=True).then_inc(off_done, 1)
                        if c < TILES - 1:
                            pe.wait_ge(xdecay_ready, s * TILES + c + 1)
                            mm(p_add[:, 0:INNER], tok[:, c % 2, INNER:384], xdecay[:, c % 2, :, :], start=True, stop=True).then_inc(add_done, 1)
                        if c == 0:
                            pe.wait_ge(out_taken, s + 1)
                        pe.wait_ge(mix_ready, s * TILES + c + 1)
                        for h in range(H):
                            last = mm(p_diag[:, h * HD:(h + 1) * HD], mix[:, c % 2, h, :], xdt[:, c % 2, h, :], start=True, stop=True)
                        last.then_inc(diag_done, 1)

                    front(0)
                    for c in range(TILES):
                        if c + 1 < TILES:
                            front(c + 1)
                        back(c)
                        if more:
                            channels(s + 1, c)
                    if more:
                        times_and_gates(s + 1)
                    pe.wait_ge(gnorm.rows_ready, s + 1)
                    for n in range(2):
                        transpose_tiles(nc, pe, p_yn[n], lambda t: yn[:, t, n * P:(n + 1) * P], w("ident")).then_inc(ynT_done, 1)
                    pe.wait_ge(ynT_ready, (s + 1) * 2)
                    for t in range(TILES):
                        for n in range(2):
                            last = mm(p_out[:, t * P:(t + 1) * P], ynT[:, n, t * P:(t + 1) * P], w("ssd_wo")[:, n * P:(n + 1) * P],
                                      start=(n == 0), stop=(n == 1))
                    last.then_inc(out_done, 1)

                turn_rows(0)
                for m in range(4):
                    channels(0, m)
                times_and_gates(0)
                with pe.Fori(0, SEQS - 1) as s:
                    sequence(s, True)
                sequence(SEQS - 1, False)


class Kit:

    FIRST = 128

    def __init__(self, nc):
        self.nc, self.semaphores = nc, []

    def semaphore(self, ctx, name):
        self.semaphores.append(ctx.enter_context(self.nc.semaphore(name, num=self.FIRST + len(self.semaphores))))
        return self.semaphores[-1]

    def end_stage(self):
        self.nc.gpsimd.sem_clear(range(self.FIRST, self.FIRST + len(self.semaphores)))
        self.nc.all_engine_barrier()
        self.semaphores = []


STAGE = {"gla": gla_stage, "ffn": ffn_stage, "favor": favor_stage, "taylor": taylor_stage, "moe": moe_stage, "ssd": ssd_stage}
CONSTS = (0.0, 1e-12, 1e-5, 1e-6, 1.0, -0.5 * float(np.log(32.0)), 4.0 / 32.0 ** 0.5)


def program(nc, x_dram, w_dram, out_dram, places, groups, width):
    k = Kit(nc)
    with ExitStack() as ctx:
        k.x = ctx.enter_context(nc.sbuf_tensor("x", [P, SEQS * TILES, DIM], F32))
        resident = ctx.enter_context(nc.sbuf_tensor("resident", [P, sum(z - a for g, (a, z) in groups.items() if g not in EARLY + LATE + (SPLIT,))], F32))
        consts = ctx.enter_context(nc.sbuf_tensor("consts", [P, len(CONSTS)], F32))
        k.spare = ctx.enter_context(nc.sbuf_tensor("spare", [P, 2], F32))
        k.banks = [ctx.enter_context(nc.psum_tensor(f"bank{n}", [P, 512], F32)) for n in range(8)]
        x_loaded = ctx.enter_context(nc.semaphore("x_loaded"))
        loaded = {g: ctx.enter_context(nc.semaphore(g + "_loaded")) for g in groups}
        consts_set = ctx.enter_context(nc.semaphore("consts_set"))
        stored = ctx.enter_context(nc.semaphore("stored"))

        held = {}

        def hold(tensor, names):
            at = 0
            for g in names:
                size = groups[g][1] - groups[g][0]
                held[g] = tensor[:, at:at + size]
                at += size

        def w(name):
            at, rows, cols = places[name]
            group = next(g for g, (a, z) in groups.items() if a <= at < z)
            at -= groups[group][0]
            return held[group][0:rows, at:at + cols]

        def load(sp, group):
            a, z = groups[group]
            sp.dma_start(held[group].rearrange("p (r c) -> p r c", c=RUN),
                         w_dram[:, a:z].rearrange("p (r c) -> p r c", c=RUN)).then_inc(loaded[group], 16)

        def await_parameters(eng, group):
            eng.wait_ge(loaded["common"], 16)
            eng.wait_ge(loaded[group], 16)

        k.w = w
        k.await_parameters = await_parameters
        k.const = lambda v: consts[:, CONSTS.index(v):CONSTS.index(v) + 1]
        x_tiles = x_dram.rearrange("b (t p) d -> p (b t) d", p=P)
        out_tiles = out_dram.rearrange("b (t p) d -> p (b t) d", p=P)

        stages = STAGES.split()
        turn = next((n for n, name in enumerate(stages) if name not in EARLY), len(stages))
        width_of = lambda names: sum(groups[g][1] - groups[g][0] for g in names)
        hold(resident, [g for g in groups if g not in EARLY + LATE + (SPLIT,)])

        early = ExitStack()
        hold(early.enter_context(nc.sbuf_tensor("early", [P, width_of(EARLY)], F32)), EARLY)
        with nc.Block() as block:
            @block.sync
            def _(sp):
                sp.dma_start(k.x[:, :, :], x_tiles).then_inc(x_loaded, 16)
                for g in groups:
                    if g not in LATE + (SPLIT,):
                        load(sp, g)
                sp.wait_ge(x_loaded, 16)

            @block.vector
            def _(dve):
                for n, v in enumerate(CONSTS):
                    nc.vector.memset(consts[:, n:n + 1], v).then_inc(consts_set, 1)
                nc.vector.memset(k.spare[:, :], 0.0).then_inc(consts_set, 1)
                dve.wait_ge(consts_set, len(CONSTS) + 1)

        for n, name in enumerate(stages[:turn]):
            STAGE[name](nc, k, n)
            k.end_stage()

        with nc.Block() as block:
            @block.sync
            def _(sp):
                for g in EARLY:
                    sp.wait_ge(loaded[g], 16)
        early.close()
        hold(ctx.enter_context(nc.sbuf_tensor("late", [P, width_of(LATE)], F32)), LATE)
        wide = width_of([SPLIT])
        k.expert_parts = ctx.enter_context(nc.sbuf_tensor("expert_parts", [P, 2, wide], BF16))
        with ExitStack() as once:
            whole = once.enter_context(nc.sbuf_tensor("expert_whole", [P, wide], F32))
            chunk_loaded = [once.enter_context(nc.semaphore(f"chunk_loaded{n}")) for n in range(4)]
            high_ready, low_ready = once.enter_context(nc.semaphore("high_ready")), once.enter_context(nc.semaphore("low_ready"))
            chunks = [slice(n * wide // 4, (n + 1) * wide // 4) for n in range(4)]
            with nc.Block() as block:
                @block.sync
                def _(sp):
                    a, z = groups[SPLIT]
                    for n, c in enumerate(chunks):
                        sp.dma_start(whole[:, c].rearrange("p (r c) -> p r c", c=RUN),
                                     w_dram[:, a:z][:, c].rearrange("p (r c) -> p r c", c=RUN)).then_inc(chunk_loaded[n], 16)
                    for g in LATE:
                        load(sp, g)

                @block.scalar
                def _(act):
                    for n, c in enumerate(chunks):
                        act.wait_ge(chunk_loaded[n], 16)
                        nc.scalar.copy(k.expert_parts[:, 0, c], whole[:, c]).then_inc(high_ready, 1)

                @block.vector
                def _(dve):
                    for n, c in enumerate(chunks):
                        dve.wait_ge(chunk_loaded[n], 16)
                        dve.wait_ge(high_ready, n + 1)
                        nc.vector.tensor_tensor(k.expert_parts[:, 1, c], whole[:, c], k.expert_parts[:, 0, c], ALU.subtract).then_inc(low_ready, 1)
                    dve.wait_ge(low_ready, 4)
        for n, name in enumerate(stages[turn:]):
            STAGE[name](nc, k, turn + n)
            k.end_stage()

        with nc.Block() as block:
            @block.sync
            def _(sp):
                for g in groups:
                    if g != SPLIT:
                        sp.wait_ge(loaded[g], 16)
                sp.dma_start(out_tiles, k.x[:, :, :]).then_inc(stored, 16)
                sp.wait_ge(stored, 16)


def kernel(**inputs):
    import concourse.bacc as _bacc
    from concourse.bass_utils import run_bass_kernel_spmd as _run

    nc = _bacc.Bacc("TRN2", target_bir_lowering=False, num_devices=1)
    blocks = parameter_blocks(inputs)
    places, groups, width = placed(blocks)
    packed = np.zeros((P, width), np.float32)
    for name, (at, rows, cols) in places.items():
        packed[:rows, at:at + cols] = blocks[name]
    x = np.ascontiguousarray(inputs["L0_attn_a_x"])
    x_dram = nc.dram_tensor("x_dram", x.shape, F32, kind="ExternalInput").ap()
    w_dram = nc.dram_tensor("w_dram", packed.shape, F32, kind="ExternalInput").ap()
    out_dram = nc.dram_tensor("out_dram", x.shape, F32, kind="ExternalOutput").ap()
    program(nc, x_dram, w_dram, out_dram, places, groups, width)
    r = _run(nc, [{"x_dram": x, "w_dram": packed}], core_ids=[0])
    return r.results[0]["out_dram"]
```
